# Optimizing a Trainium2 kernel written in Bass

```python
import numpy as np
import jax
import jax.numpy as jnp

def _softmax(x, axis=-1):
    return jax.nn.softmax(x, axis=axis)

def _gelu(x):
    return jax.nn.gelu(x, approximate=True)

def _silu(x):
    return jax.nn.silu(x)

def _sigmoid(x):
    return jax.nn.sigmoid(x)

def _layernorm(x, axis=-1, eps=1e-05):
    m = jnp.mean(x, axis=axis, keepdims=True)
    v = jnp.var(x, axis=axis, keepdims=True)
    return (x - m) / jnp.sqrt(v + eps)

def _scatter_add(tgt, idx, src, axis=0):
    return tgt.at[idx].add(src)

def _segment_sum(src, seg, n):
    return jax.ops.segment_sum(src, seg, n)
kernel_name = 'mk_flamingo_gated_d1_seqx_r8_0cec83'

def setup_inputs(seed: int=0):
    np.random.seed(seed)
    _w = jnp.asarray

    def _rec_inputs():
        import jax
        import jax.numpy as jnp
        _rk = jax.random.key(seed)
        x = -0.0002928 + 1 * jax.random.normal(jax.random.fold_in(_rk, 1), (16, 128, 128), jnp.float32)
        _lenS = 128 - jax.random.randint(jax.random.fold_in(_rk, 7), (16,), 0, max(1, 128 // 4) + 1, jnp.int32)
        _lenS2 = 128 - jax.random.randint(jax.random.fold_in(_rk, 8), (16,), 0, max(1, 128 // 4) + 1, jnp.int32)
        _ctx_1024P = jax.random.normal(jax.random.fold_in(_rk, 11), (16, 16, 128), jnp.float32)
        _ctx_1024c = jax.random.dirichlet(jax.random.fold_in(_rk, 511), 0.3 * jnp.ones((16,), jnp.float32), (16, 128))
        _ctx_1024t = jnp.einsum('bsk,bkd->bsd', _ctx_1024c, _ctx_1024P)
        _ctx_1024t = _ctx_1024t * jax.lax.rsqrt(jnp.mean(jnp.square(_ctx_1024t)) + 1e-12) * 0.953939
        ctx_1024 = -1.39393e-06 + 0.999914 * (_ctx_1024t + 0.3 * jax.random.normal(jax.random.fold_in(_rk, 611), (16, 128, 128), jnp.float32))
        fside_BxS2_0 = jax.random.uniform(jax.random.fold_in(_rk, 12), (16, 128), jnp.float32, 0.0, 0.999833)
        _g = jax.random.normal(jax.random.fold_in(_rk, 9001), (2, 1), jnp.float32)
        _g = jnp.sign(_g) * jnp.maximum(jnp.abs(_g), 1.0) + (_g == 0) * 1.0
        g_xattn = _g[0]
        g_ffn = _g[1]
        return (x, ctx_1024, fside_BxS2_0, g_xattn, g_ffn)
    x, ctx_1024, fside_BxS2_0, g_xattn, g_ffn = _rec_inputs()

    def _L0_xattn_setup():
        import jax, jax.numpy as jnp
        import numpy as np
        D_MODEL = 128
        NHEAD = 16
        HEAD_DIM = D_MODEL // NHEAD
        CLAMP_MIN = -0.2
        CLAMP_MAX = 0.2
        key = jax.random.key(seed)
        ks = jax.random.split(key, 16)
        B, T = (2, 256)
        s = 1.0 / np.sqrt(D_MODEL)
        inp = {'query': jax.random.normal(ks[0], (B, T, D_MODEL), jnp.float32), 'key': jax.random.normal(ks[1], (B, T, D_MODEL), jnp.float32), 'value': jax.random.normal(ks[2], (B, T, D_MODEL), jnp.float32), 'frac': jax.random.uniform(ks[3], (B, T), jnp.float32), 'Wq': jax.random.normal(ks[4], (D_MODEL, D_MODEL), jnp.float32) * s, 'bq': jnp.zeros((D_MODEL,), jnp.float32), 'Wk': jax.random.normal(ks[5], (D_MODEL, D_MODEL), jnp.float32) * s, 'bk': jnp.zeros((D_MODEL,), jnp.float32), 'Wv': jax.random.normal(ks[6], (D_MODEL, D_MODEL), jnp.float32) * s, 'bv': jnp.zeros((D_MODEL,), jnp.float32), 'Wo': jax.random.normal(ks[7], (D_MODEL, D_MODEL), jnp.float32) * s, 'bo': jnp.zeros((D_MODEL,), jnp.float32), 'alpha_pos': jax.random.normal(ks[8], (NHEAD,), jnp.float32) * 0.1, 'alpha_neg': jax.random.normal(ks[9], (NHEAD,), jnp.float32) * 0.1, 'gamma': jnp.float32(1.0), 'delta': jnp.float32(1.0)}
        return inp
    _L0_xattn_all = _L0_xattn_setup()
    _L0_xattn_in = {k: v for k, v in _L0_xattn_all.items() if k in ('Wq', 'bq', 'Wk', 'bk', 'Wv', 'bv', 'Wo', 'bo', 'alpha_pos', 'alpha_neg', 'gamma', 'delta')}
    del _L0_xattn_all

    def _L0_ffn_setup():
        import jax, jax.numpy as jnp
        import numpy as np
        DIM = 128
        DEPTH = 6
        HEADS = 16
        DIM_HEAD = 64
        WINDOW = 32
        INNER = HEADS * DIM_HEAD
        DIM_INNER = int(DIM * 4 * 2 / 3)
        QK_SCALE = 8.0

        def shift_tokens(t):
            a, s = jnp.split(t, 2, -1)
            s = jnp.pad(s, ((0, 0), (1, 0), (0, 0)))[:, :-1]
            return jnp.concatenate([a, s], -1)

        def l2norm(t):
            return t / jnp.maximum(jnp.linalg.norm(t, axis=-1, keepdims=True), 1e-12)

        def rotate_half(x):
            x1, x2 = jnp.split(x, 2, -1)
            return jnp.concatenate([-x2, x1], -1)

        def rotary_tables(n):
            half = jnp.arange(0, DIM_HEAD, 2, dtype=jnp.float32)
            inv_freq = 1.0 / 10000.0 ** (half / DIM_HEAD)
            t = jnp.arange(n, dtype=jnp.float32)
            freqs = t[:, None] * inv_freq[None, :]
            freqs = jnp.concatenate([freqs, freqs], -1)
            base_scale = (half + 0.4 * DIM_HEAD) / (1.4 * DIM_HEAD)
            power = (t - n // 2) / (WINDOW // 2)
            scale = base_scale[None, :] ** power[:, None]
            scale = jnp.concatenate([scale, scale], -1)
            return (freqs, scale)

        def local_attention(q, k, v):
            b, h, n, d = q.shape
            w = WINDOW
            nw = n // w
            bq = q.reshape(b, h, nw, w, d)
            bk = k.reshape(b, h, nw, w, d)
            bv = v.reshape(b, h, nw, w, d)

            def look(t):
                p = jnp.pad(t, ((0, 0), (0, 0), (1, 0), (0, 0), (0, 0)))
                return jnp.concatenate([p[:, :, :nw], p[:, :, 1:]], axis=3)
            bk2, bv2 = (look(bk), look(bv))
            seq = jnp.arange(n).reshape(nw, w)
            seq_p = jnp.pad(seq, ((1, 0), (0, 0)), constant_values=-1)
            jt = jnp.concatenate([seq_p[:nw], seq_p[1:]], axis=1)
            it = seq[:, :, None]
            jb = jt[:, None, :]
            mask = (it < jb) | (it > jb + w) | (jb == -1)
            sim = jnp.einsum('bhwie,bhwje->bhwij', bq, bk2) * QK_SCALE
            sim = jnp.where(mask, -jnp.finfo(sim.dtype).max, sim)
            attn = jax.nn.softmax(sim, -1)
            out = jnp.einsum('bhwij,bhwje->bhwie', attn, bv2)
            return out.reshape(b, h, n, d)

        def attn_layer(x, Wqkv, qs, ksc, Wo):
            b, n, _ = x.shape
            qkv = x @ Wqkv
            q, k, v = jnp.split(qkv, 3, -1)
            sh = lambda t: t.reshape(b, n, HEADS, DIM_HEAD).transpose(0, 2, 1, 3)
            q, k, v = (sh(q), sh(k), sh(v))
            q = l2norm(q) * qs
            k = l2norm(k) * ksc
            freqs, scale = rotary_tables(n)
            cos, sin = (jnp.cos(freqs), jnp.sin(freqs))
            q = q * cos * scale + rotate_half(q) * sin * scale
            inv = 1.0 / scale
            k = k * cos * inv + rotate_half(k) * sin * inv
            out = local_attention(q, k, v)
            out = out.transpose(0, 2, 1, 3).reshape(b, n, INNER)
            return out @ Wo

        def ffn_layer(x, g, bln, W1, b1, W2, b2):
            mu = x.mean(-1, keepdims=True)
            var = ((x - mu) ** 2).mean(-1, keepdims=True)
            xn = (x - mu) / jnp.sqrt(var + 1e-05) * g + bln
            hg = xn @ W1 + b1
            a, gate = jnp.split(hg, 2, -1)
            return a * jax.nn.gelu(gate, approximate=False) @ W2 + b2
        key = jax.random.key(seed)
        ks = jax.random.split(key, 8)
        B, N = (2, 256)
        init = lambda k, shape: jax.random.normal(k, shape, jnp.float32) * 0.02
        return {'x': jax.random.normal(ks[0], (B, N, DIM), jnp.float32), 'Wqkv': init(ks[1], (DEPTH, DIM, 3 * INNER)), 'q_scale': jnp.ones((DEPTH, DIM_HEAD), jnp.float32), 'k_scale': jnp.ones((DEPTH, DIM_HEAD), jnp.float32), 'Wo': init(ks[2], (DEPTH, INNER, DIM)), 'ln_g': jnp.ones((DEPTH, DIM), jnp.float32), 'ln_b': jnp.zeros((DEPTH, DIM), jnp.float32), 'W1': init(ks[3], (DEPTH, DIM, 2 * DIM_INNER)), 'b1': jnp.zeros((DEPTH, 2 * DIM_INNER), jnp.float32), 'W2': init(ks[4], (DEPTH, DIM_INNER, DIM)), 'b2': jnp.zeros((DEPTH, DIM), jnp.float32)}
    _L0_ffn_all = _L0_ffn_setup()
    _L0_ffn_in = {k: v for k, v in _L0_ffn_all.items() if k in ('Wqkv', 'q_scale', 'k_scale', 'Wo', 'ln_g', 'ln_b', 'W1', 'b1', 'W2', 'b2')}
    del _L0_ffn_all
    return {'x': x, 'ctx_1024': ctx_1024, 'fside_BxS2_0': fside_BxS2_0, 'g_xattn': g_xattn, 'g_ffn': g_ffn, 'L0_xattn_Wq': _L0_xattn_in['Wq'], 'L0_xattn_bq': _L0_xattn_in['bq'], 'L0_xattn_Wk': _L0_xattn_in['Wk'], 'L0_xattn_bk': _L0_xattn_in['bk'], 'L0_xattn_Wv': _L0_xattn_in['Wv'], 'L0_xattn_bv': _L0_xattn_in['bv'], 'L0_xattn_Wo': _L0_xattn_in['Wo'], 'L0_xattn_bo': _L0_xattn_in['bo'], 'L0_xattn_alpha_pos': _L0_xattn_in['alpha_pos'], 'L0_xattn_alpha_neg': _L0_xattn_in['alpha_neg'], 'L0_xattn_gamma': _L0_xattn_in['gamma'], 'L0_xattn_delta': _L0_xattn_in['delta'], 'L0_ffn_Wqkv': _L0_ffn_in['Wqkv'], 'L0_ffn_q_scale': _L0_ffn_in['q_scale'], 'L0_ffn_k_scale': _L0_ffn_in['k_scale'], 'L0_ffn_Wo': _L0_ffn_in['Wo'], 'L0_ffn_ln_g': _L0_ffn_in['ln_g'], 'L0_ffn_ln_b': _L0_ffn_in['ln_b'], 'L0_ffn_W1': _L0_ffn_in['W1'], 'L0_ffn_b1': _L0_ffn_in['b1'], 'L0_ffn_W2': _L0_ffn_in['W2'], 'L0_ffn_b2': _L0_ffn_in['b2']}

def reference(x, ctx_1024, fside_BxS2_0, g_xattn, g_ffn, L0_xattn_Wq, L0_xattn_bq, L0_xattn_Wk, L0_xattn_bk, L0_xattn_Wv, L0_xattn_bv, L0_xattn_Wo, L0_xattn_bo, L0_xattn_alpha_pos, L0_xattn_alpha_neg, L0_xattn_gamma, L0_xattn_delta, L0_ffn_Wqkv, L0_ffn_q_scale, L0_ffn_k_scale, L0_ffn_Wo, L0_ffn_ln_g, L0_ffn_ln_b, L0_ffn_W1, L0_ffn_b1, L0_ffn_W2, L0_ffn_b2):
    import jax
    import jax.numpy as jnp

    def _L0_xattn_ref(query, key, value, frac, Wq, bq, Wk, bk, Wv, bv, Wo, bo, alpha_pos, alpha_neg, gamma, delta):
        import jax, jax.numpy as jnp
        import numpy as np
        D_MODEL = 128
        NHEAD = 16
        HEAD_DIM = D_MODEL // NHEAD
        CLAMP_MIN = -0.2
        CLAMP_MAX = 0.2
        B, T, _ = query.shape
        scale = HEAD_DIM ** (-0.5)

        def proj(x, W, b):
            y = x @ W.T + b
            return y.reshape(B, T, NHEAD, HEAD_DIM).transpose(0, 2, 1, 3)
        Q = proj(query, Wq, bq)
        K = proj(key, Wk, bk)
        V = proj(value, Wv, bv)
        logits = jnp.einsum('bhqd,bhkd->bhqk', Q, K) * scale
        D = jnp.clip(frac[:, None, :] - frac[:, :, None], CLAMP_MIN, CLAMP_MAX)
        D_pos = jnp.maximum(D, 0.0)
        D_neg = jnp.minimum(D, 0.0)
        ap = alpha_pos[None, :, None, None]
        an = alpha_neg[None, :, None, None]
        stoich_bias = ap * D_pos[:, None] + an * D_neg[:, None]
        attn = gamma * logits + delta * stoich_bias
        probs = jax.nn.softmax(attn, axis=-1)
        out = jnp.einsum('bhqk,bhkd->bhqd', probs, V)
        out = out.transpose(0, 2, 1, 3).reshape(B, T, D_MODEL)
        return out @ Wo.T + bo

    def _L0_ffn_ref(x, Wqkv, q_scale, k_scale, Wo, ln_g, ln_b, W1, b1, W2, b2):
        import jax, jax.numpy as jnp
        import numpy as np
        DIM = 128
        DEPTH = 6
        HEADS = 16
        DIM_HEAD = 64
        WINDOW = 32
        INNER = HEADS * DIM_HEAD
        DIM_INNER = int(DIM * 4 * 2 / 3)
        QK_SCALE = 8.0

        def shift_tokens(t):
            a, s = jnp.split(t, 2, -1)
            s = jnp.pad(s, ((0, 0), (1, 0), (0, 0)))[:, :-1]
            return jnp.concatenate([a, s], -1)

        def l2norm(t):
            return t / jnp.maximum(jnp.linalg.norm(t, axis=-1, keepdims=True), 1e-12)

        def rotate_half(x):
            x1, x2 = jnp.split(x, 2, -1)
            return jnp.concatenate([-x2, x1], -1)

        def rotary_tables(n):
            half = jnp.arange(0, DIM_HEAD, 2, dtype=jnp.float32)
            inv_freq = 1.0 / 10000.0 ** (half / DIM_HEAD)
            t = jnp.arange(n, dtype=jnp.float32)
            freqs = t[:, None] * inv_freq[None, :]
            freqs = jnp.concatenate([freqs, freqs], -1)
            base_scale = (half + 0.4 * DIM_HEAD) / (1.4 * DIM_HEAD)
            power = (t - n // 2) / (WINDOW // 2)
            scale = base_scale[None, :] ** power[:, None]
            scale = jnp.concatenate([scale, scale], -1)
            return (freqs, scale)

        def local_attention(q, k, v):
            b, h, n, d = q.shape
            w = WINDOW
            nw = n // w
            bq = q.reshape(b, h, nw, w, d)
            bk = k.reshape(b, h, nw, w, d)
            bv = v.reshape(b, h, nw, w, d)

            def look(t):
                p = jnp.pad(t, ((0, 0), (0, 0), (1, 0), (0, 0), (0, 0)))
                return jnp.concatenate([p[:, :, :nw], p[:, :, 1:]], axis=3)
            bk2, bv2 = (look(bk), look(bv))
            seq = jnp.arange(n).reshape(nw, w)
            seq_p = jnp.pad(seq, ((1, 0), (0, 0)), constant_values=-1)
            jt = jnp.concatenate([seq_p[:nw], seq_p[1:]], axis=1)
            it = seq[:, :, None]
            jb = jt[:, None, :]
            mask = (it < jb) | (it > jb + w) | (jb == -1)
            sim = jnp.einsum('bhwie,bhwje->bhwij', bq, bk2) * QK_SCALE
            sim = jnp.where(mask, -jnp.finfo(sim.dtype).max, sim)
            attn = jax.nn.softmax(sim, -1)
            out = jnp.einsum('bhwij,bhwje->bhwie', attn, bv2)
            return out.reshape(b, h, n, d)

        def attn_layer(x, Wqkv, qs, ksc, Wo):
            b, n, _ = x.shape
            qkv = x @ Wqkv
            q, k, v = jnp.split(qkv, 3, -1)
            sh = lambda t: t.reshape(b, n, HEADS, DIM_HEAD).transpose(0, 2, 1, 3)
            q, k, v = (sh(q), sh(k), sh(v))
            q = l2norm(q) * qs
            k = l2norm(k) * ksc
            freqs, scale = rotary_tables(n)
            cos, sin = (jnp.cos(freqs), jnp.sin(freqs))
            q = q * cos * scale + rotate_half(q) * sin * scale
            inv = 1.0 / scale
            k = k * cos * inv + rotate_half(k) * sin * inv
            out = local_attention(q, k, v)
            out = out.transpose(0, 2, 1, 3).reshape(b, n, INNER)
            return out @ Wo

        def ffn_layer(x, g, bln, W1, b1, W2, b2):
            mu = x.mean(-1, keepdims=True)
            var = ((x - mu) ** 2).mean(-1, keepdims=True)
            xn = (x - mu) / jnp.sqrt(var + 1e-05) * g + bln
            hg = xn @ W1 + b1
            a, gate = jnp.split(hg, 2, -1)
            return a * jax.nn.gelu(gate, approximate=False) @ W2 + b2
        for i in range(DEPTH):
            x = attn_layer(shift_tokens(x), Wqkv[i], q_scale[i], k_scale[i], Wo[i]) + x
            x = ffn_layer(shift_tokens(x), ln_g[i], ln_b[i], W1[i], b1[i], W2[i], b2[i]) + x
        return x
    x = x + jnp.tanh(g_xattn[0]) * _L0_xattn_ref(_layernorm(x, axis=-1), ctx_1024, ctx_1024, fside_BxS2_0, L0_xattn_Wq, L0_xattn_bq, L0_xattn_Wk, L0_xattn_bk, L0_xattn_Wv, L0_xattn_bv, L0_xattn_Wo, L0_xattn_bo, L0_xattn_alpha_pos, L0_xattn_alpha_neg, L0_xattn_gamma, L0_xattn_delta)
    x = x + jnp.tanh(g_ffn[0]) * _L0_ffn_ref(_layernorm(x, axis=-1), L0_ffn_Wqkv, L0_ffn_q_scale, L0_ffn_k_scale, L0_ffn_Wo, L0_ffn_ln_g, L0_ffn_ln_b, L0_ffn_W1, L0_ffn_b1, L0_ffn_W2, L0_ffn_b2)
    return x

_drawn_inputs = setup_inputs


def setup_inputs(seed=0):
    import zlib

    import numpy as np

    out = dict(_drawn_inputs(seed))
    spreads = {'L0_xattn_bq': (0.0, 0.388),
     'L0_xattn_bk': (0.0, 2.0),
     'L0_xattn_bv': (0.0, 0.1),
     'L0_xattn_bo': (0.0, 0.1),
     'L0_ffn_q_scale': (1.0, 0.2),
     'L0_ffn_k_scale': (1.0, 0.2),
     'L0_ffn_ln_g': (1.0, 0.6),
     'L0_ffn_ln_b': (0.0, 0.732),
     'L0_ffn_b1': (0.0, 0.1),
     'L0_ffn_b2': (0.0, 0.1)}
    factors = {'fside_BxS2_0': 64.0, 'L0_xattn_alpha_pos': 64.0, 'L0_xattn_alpha_neg': 64.0}
    for name, (base, spread) in spreads.items():
        noise = np.random.default_rng([zlib.crc32(name.encode()), seed]).standard_normal(out[name].shape)
        drawn = base * np.exp(spread * noise) if base else spread * noise
        out[name] = jnp.asarray(drawn.astype(out[name].dtype))
    for name, factor in factors.items():
        out[name] = (out[name] * factor).astype(out[name].dtype)
    return out
```

```python
from contextlib import ExitStack

import concourse.bass as bass
import numpy as np
from concourse import mybir

f32 = mybir.dt.float32
f32r = mybir.dt.float32r
ALU = mybir.AluOpType
ACT = mybir.ActivationFunctionType
AX = mybir.AxisListType.X

NB, NT, D = 16, 128, 128
H, DH = 16, 64
HALF = DH // 2
LAYERS = 6
INNER = H * DH
WINDOW = 32
QK_SCALE = 8.0
FI = D * 4 * 2 // 3
FC = [128, 128, FI - 256]
XH, XD = 16, 8
GH = 4
NG = H // GH
FG = 4
NF = NB // FG
CLAMP = 0.2
NEG = -1.0e30
LN_EPS = 1e-5
CHUNK_COL = [0, INNER, 512, INNER + 512, 2 * INNER, 2 * INNER + 512]


def build(nc, t):
    ctx = ExitStack()
    with ctx:
        ctx.enter_context(nc.allow_non_contiguous_dma(reason="small vectors laid along the partitions"))

        def sb(name, shape, dt=f32):
            return ctx.enter_context(nc.sbuf_tensor(name, shape, dt))

        def bank(name):
            return ctx.enter_context(nc.psum_tensor(name, [128, 512], f32))

        def sem(name):
            return ctx.enter_context(nc.semaphore(name))

        z = sb("z", [128, NB, D])
        ident = sb("ident", [128, 128])
        shift = sb("shift", [128, 128])
        band = sb("band", [128, 128])
        rot = sb("rot", [128, 4, DH])
        qk_scale = sb("qk_scale", [128, 2, LAYERS, DH])
        tab = sb("tab", [128, 4, LAYERS, DH])
        eps = sb("eps", [128, 1])
        params = sb("params", [128, LAYERS, 8])
        param = sb("param", [128, 8])
        w_raw = sb("w_raw", [128, 3 * INNER])
        w_hi = sb("w_hi", [128, 3 * INNER], f32r)
        w_lo = sb("w_lo", [128, 3 * INNER], f32r)
        w1_raw = sb("w1_raw", [128, 2 * FI])
        w1_hi = sb("w1_hi", [128, 2 * FI], f32r)
        w1_lo = sb("w1_lo", [128, 2 * FI], f32r)
        wo = sb("wo", [128, INNER // 128, D])
        w2 = sb("w2", [128, 3, D])
        z_stage = sb("z_stage", [128, D])
        x_all = sb("x_all", [128, NT])
        x_hi = sb("x_hi", [128, NT], f32r)
        x_lo = sb("x_lo", [128, NT], f32r)
        square = sb("square", [128, 2, 512])
        by_cos = sb("by_cos", [128, 2, 512])
        by_sin = sb("by_sin", [128, 2, 512])
        sumsq = sb("sumsq", [128, 2, 2 * 8])
        log_sq = sb("log_sq", [128, 2, 2 * 8])
        inv_norm = sb("inv_norm", [128, 2, 2 * 8])
        qk = sb("qk", [128, 4, 512])
        q_T = [sb(f"q_T{i}", [128, 8, NT]) for i in range(2)]
        k_T = [sb(f"k_T{i}", [128, 8, NT]) for i in range(2)]
        v = [sb(f"v{i}", [128, H, DH + 1]) for i in range(2)]
        s_sb = sb("s_sb", [128, 2, GH, NT])
        row_max = sb("row_max", [128, 2, GH])
        p_sb = sb("p_sb", [128, 2, GH, NT])
        p_T = sb("p_T", [128, 2, GH, NT])
        inv_sum = sb("inv_sum", [128, GH])
        att = sb("att", [128, H, DH])
        att_T = sb("att_T", [128, INNER // 128, NT])
        xs = sb("xs", [128, D])
        x_res = sb("x_res", [128, NB, D])
        xw_raw = sb("xw_raw", [128, 4, D])
        xw_T = sb("xw_T", [128, 4, D])
        xb_col = sb("xb_col", [128, 2])
        xb_row = sb("xb_row", [128, 2, D])
        alpha = sb("alpha", [128, 2, XH])
        gates = sb("gates", [128, 4])
        tanh_g = sb("tanh_g", [128, 2])
        q_scale = sb("q_scale", [128, 2])
        frac_q = sb("frac_q", [128, NB])
        head_of = sb("head_of", [128, GH])
        x_mv = sb("x_mv", [128, NB, 2])
        x_st = sb("x_st", [128, NB, 6])
        x_log = sb("x_log", [128, NB])
        x_rstd = sb("x_rstd", [128, NB])
        x_in = sb("x_in", [128, 2, D])
        c_in = sb("c_in", [128, 2, D])
        xc_T = sb("xc_T", [128, 2, NT])
        xq = sb("xq", [128, 2, NT])
        xk = sb("xk", [128, NT])
        xv = sb("xv", [128, 2, XH, XD + 1])
        d_clip = sb("d_clip", [128, 2, NT])
        d_pos = sb("d_pos", [128, 2, NT])
        d_neg = sb("d_neg", [128, 2, NT])
        bias_neg = sb("bias_neg", [128, GH, NT])
        x_att = sb("x_att", [128, XH, XD])
        x_att_T = sb("x_att_T", [128, NT])
        stats = sb("stats", [128, 6])
        mean_var = sb("mean_var", [128, 2])
        log_var = sb("log_var", [128, 1])
        rstd = sb("rstd", [128, 1])
        xn = sb("xn", [128, NB, D])
        f_all = sb("f_all", [128, 2, 512])
        f_hi = sb("f_hi", [128, 2, 512], f32r)
        f_lo = sb("f_lo", [128, 2, 512], f32r)
        gelu = sb("gelu", [128, 2, 512])
        frac_k = xn
        bias_pos = f_all[:].rearrange("p i (h k) -> p i h k", k=NT)
        xk_bd = gelu[:].rearrange("p i (h k) -> p i h k", k=NT)
        h_T = [[sb(f"h_T{i}{c}", [128, 512]) for c in range(3)] for i in range(2)]

        proj_ps = [bank("proj_ps0"), bank("proj_ps1")]
        tr_ps = bank("tr_ps")
        pt_ps = bank("pt_ps")
        s_ps = ctx.enter_context(nc.psum_tensor("s_ps", [128, 2, 512], f32))
        pv_ps = bank("pv_ps")
        y_ps = bank("y_ps")

        const_ld = sem("const_ld")
        ld_w = sem("ld_w")
        ld_w1 = sem("ld_w1")
        ld_wo = sem("ld_wo")
        ld_w2 = sem("ld_w2")
        setup_done = sem("setup_done")
        tab_done = sem("tab_done")
        w_hi_done = sem("w_hi_done")
        w_split = sem("w_split")
        w1_hi_done = sem("w1_hi_done")
        w1_split = sem("w1_split")
        params_clear = sem("params_clear")
        param_ready = sem("param_ready")
        z_staged = sem("z_staged")
        x_split = sem("x_split")
        tr_full = sem("tr_full")
        tr_evac = sem("tr_evac")
        proj_full = sem("proj_full")
        squared = sem("squared")
        rotated = sem("rotated")
        summed = sem("summed")
        norm_ready = sem("norm_ready")
        inv_log = sem("inv_log")
        inv_ready = sem("inv_ready")
        qk_added = sem("qk_added")
        qk_ready = sem("qk_ready")
        v_ready = sem("v_ready")
        s_full = sem("s_full")
        masked = sem("masked")
        max_ready = sem("max_ready")
        centered = sem("centered")
        p_ready = sem("p_ready")
        pt_full = sem("pt_full")
        pt_evac = sem("pt_evac")
        pv_full = sem("pv_full")
        recip_done = sem("recip_done")
        att_ready = sem("att_ready")
        ot_full = sem("ot_full")
        ot_evac = sem("ot_evac")
        y_full = sem("y_full")
        z_attn = sem("z_attn")
        sh_full = sem("sh_full")
        xs_ready = sem("xs_ready")
        stat_done = sem("stat_done")
        var_ready = sem("var_ready")
        log_done = sem("log_done")
        rstd_ready = sem("rstd_ready")
        xn_ready = sem("xn_ready")
        ft_full = sem("ft_full")
        ft_evac = sem("ft_evac")
        f_split = sem("f_split")
        gate_full = sem("gate_full")
        a_full = sem("a_full")
        gelu_done = sem("gelu_done")
        h_ready = sem("h_ready")
        fy_full = sem("fy_full")
        z_ready = sem("z_ready")
        out_done = sem("out_done")
        result_ready = sem("result_ready")
        xw_ld = sem("xw_ld")
        bc_ld = sem("bc_ld")
        frac_ready = sem("frac_ready")
        x_ld = sem("x_ld")
        ctx_ld = [sem("ctx_ld_even"), sem("ctx_ld_odd")]
        xw_full = sem("xw_full")
        xw_evac = sem("xw_evac")
        xstat_done = sem("xstat_done")
        xvar_ready = sem("xvar_ready")
        xlog_done = sem("xlog_done")
        xrstd_ready = sem("xrstd_ready")
        xin_ready = sem("xin_ready")
        xt_full = sem("xt_full")
        xt_evac = sem("xt_evac")
        xproj_full = sem("xproj_full")
        xqk_out = sem("xqk_out")
        xk_ready = sem("xk_ready")
        xv_ready = sem("xv_ready")
        scalar_ready = sem("scalar_ready")
        tanh_done = sem("tanh_done")
        xscaled = sem("xscaled")
        xclip = sem("xclip")
        clip_ready = sem("clip_ready")
        bias_ready = sem("bias_ready")
        added_pos = sem("added_pos")
        neg_ready = sem("neg_ready")
        xo_full = sem("xo_full")
        xo_evac = sem("xo_evac")
        xy_full = sem("xy_full")
        xy_ready = sem("xy_ready")
        xg_ready = sem("xg_ready")
        block = ctx.enter_context(nc.Block())

        def heads(ap):
            return ap.rearrange("p (h x d) -> p h x d", x=2, d=HALF)

        def tile_of(ap, n, lo=0, hi=D):
            return ap[:, bass.ds(n, 1), lo:hi].rearrange("p a b -> p (a b)")

        def flat(ap):
            return ap.rearrange("p a b -> p (a b)")

        def layer_slots(eng_fori, L, front, slot, drain):
            T0 = L * NB
            front(T0)
            slot(T0, 0, 0, first=True, behind=0)
            slot(T0 + 1, 1, 1, behind=1)
            with eng_fori(0, (NB - 4) // 2) as pair:
                n = pair * 2 + 2
                slot(T0 + n, n, 0)
                slot(T0 + n + 1, n + 1, 1)
            slot(T0 + NB - 2, NB - 2, 0, last_front=True)
            slot(T0 + NB - 1, NB - 1, 1, front_on=False)
            drain(T0 + NB, NB, 0)

        @block.sync
        def _(sp):
            consts = [(ident[:], t["ident"]), (shift[:], t["shift"]), (band[:], t["band"]),
                      (flat(rot[:]), t["rot"])]
            for dst, src in consts:
                sp.dma_start(dst, src).then_inc(const_ld, 16)
            for i, name in enumerate(("L0_ffn_q_scale", "L0_ffn_k_scale")):
                src = t[name].rearrange("l d -> (l d)").unsqueeze(0).to_broadcast([128, LAYERS * DH])
                sp.dma_start(flat(qk_scale[:, i]), src).then_inc(const_ld, 16)

            def load_w(layer):
                sp.dma_start(w_raw[:], t["L0_ffn_Wqkv"][layer]).then_inc(ld_w, 16)

            def load_w1(layer):
                sp.dma_start(w1_raw[:], t["L0_ffn_W1"][layer]).then_inc(ld_w1, 16)

            def load_wo(layer):
                sp.dma_start(wo[:], t["L0_ffn_Wo"][layer].rearrange("(c p) d -> p c d", p=128)).then_inc(ld_wo, 16)

            def load_w2(layer):
                w2_d = t["L0_ffn_W2"][layer]
                sp.dma_start(w2[:, 0:2, :], w2_d[0:256, :].rearrange("(c p) d -> p c d", p=128)).then_inc(ld_w2, 16)
                sp.dma_start(w2[0:FC[2], 2, :], w2_d[256:FI, :]).then_inc(ld_w2, 16)
                sp.dma_start(w2[FC[2]:FC[2] + 1, 2, :], t["L0_ffn_b2"][layer].unsqueeze(0)).then_inc(ld_w2, 16)

            for i, n in enumerate(("Wq", "Wk", "Wv", "Wo")):
                sp.dma_start(xw_raw[:, i], t["L0_xattn_" + n]).then_inc(xw_ld, 16)
            sp.dma_start(x_res[:], t["x"].rearrange("b t d -> t b d")).then_inc(x_ld, 16)
            for i, n in enumerate(("bq", "bk")):
                sp.dma_start(xb_col[:, i:i + 1], t["L0_xattn_" + n].unsqueeze(1)).then_inc(bc_ld, 16)
            for i, n in enumerate(("bv", "bo")):
                sp.dma_start(xb_row[:, i], t["L0_xattn_" + n].unsqueeze(0).to_broadcast([128, D])).then_inc(bc_ld, 16)
            for i, n in enumerate(("alpha_pos", "alpha_neg")):
                sp.dma_start(alpha[:, i], t["L0_xattn_" + n].unsqueeze(0).to_broadcast([128, XH])).then_inc(bc_ld, 16)
            for i, n in enumerate(("L0_xattn_gamma", "L0_xattn_delta", "g_xattn", "g_ffn")):
                sp.dma_start(gates[:, i:i + 1], t[n].unsqueeze(0).to_broadcast([128, 1])).then_inc(bc_ld, 16)
            sp.dma_start(head_of[:], t["head_of"]).then_inc(bc_ld, 16)
            sp.dma_start(frac_q[:], t["fside_BxS2_0"].rearrange("b t -> t b")).then_inc(bc_ld, 16)
            sp.dma_start(flat(frac_k[:]), t["fside_BxS2_0"].rearrange("b t -> (b t)").unsqueeze(0).to_broadcast([128, NB * NT])).then_inc(bc_ld, 16)
            for T in range(2):
                sp.dma_start(c_in[:, T], t["ctx_1024"][T]).then_inc(ctx_ld[T], 16)

            load_w(0)
            load_w1(0)
            load_wo(0)
            load_w2(0)
            sp.wait_ge(params_clear, 1)
            sp.dma_start(params[:, :, 0], t["L0_ffn_ln_g"].rearrange("l d -> d l")).then_inc(const_ld, 16)
            sp.dma_start(params[:, :, 1], t["L0_ffn_ln_b"].rearrange("l d -> d l")).then_inc(const_ld, 16)
            for half in range(2):
                for c in range(3):
                    col = half * FI + 128 * c
                    sp.dma_start(params[0:FC[c], :, 2 + 3 * half + c],
                                 t["L0_ffn_b1"][:, col:col + FC[c]].rearrange("l d -> d l")).then_inc(const_ld, 16)
            ctx_d = t["ctx_1024"].rearrange("b t d -> t b d")
            with sp.Fori(1, NB // 2) as pair:
                for par in range(2):
                    sp.wait_ge(xt_full, pair * 2 + (par - 1))
                    sp.dma_start(c_in[:, par:par + 1, :], ctx_d[:, bass.ds(pair * 2 + par, 1), :]).then_inc(ctx_ld[par], 16)
            with sp.Fori(1, LAYERS + 1) as L:
                nxt = L % LAYERS
                sp.wait_ge(w_split, L * 3)
                sp.dma_start(w_raw[:].unsqueeze(1), t["L0_ffn_Wqkv"].rearrange("l p n -> p l n")[:, bass.ds(nxt, 1), :]).then_inc(ld_w, 16)
                sp.wait_ge(w1_split, L)
                sp.dma_start(w1_raw[:].unsqueeze(1), t["L0_ffn_W1"].rearrange("l p n -> p l n")[:, bass.ds(nxt, 1), :]).then_inc(ld_w1, 16)
                sp.wait_ge(y_full, L * NB + NB)
                sp.dma_start(wo[:], t["L0_ffn_Wo"].rearrange("l (c p) d -> p (l c) d", p=128)[:, bass.ds(nxt * 8, 8), :]).then_inc(ld_wo, 16)
                sp.wait_ge(fy_full, L * NF + NF)
                w2_d = t["L0_ffn_W2"]
                for c in range(3):
                    sp.dma_start(w2[0:FC[c], c:c + 1, :], w2_d[:, 128 * c:128 * c + FC[c], :].rearrange("l p d -> p l d")[:, bass.ds(nxt, 1), :]).then_inc(ld_w2, 16)
                sp.dma_start(w2[FC[2]:FC[2] + 1, 2:3, :], t["L0_ffn_b2"].unsqueeze(0)[:, bass.ds(nxt, 1), :]).then_inc(ld_w2, 16)
            sp.wait_ge(result_ready, 1)
            sp.dma_start(t["out"].rearrange("b t d -> t b d"), z[:]).then_inc(out_done, 16)
            sp.wait_ge(out_done, 16)
            sp.wait_ge(ld_w, 16 * (LAYERS + 1))
            sp.wait_ge(ld_w1, 16 * (LAYERS + 1))
            sp.wait_ge(ld_wo, 16 * (LAYERS + 1))
            sp.wait_ge(ld_w2, 48 + 64 * LAYERS)

        N_CONST = 16 * (6 + 2 + 6)
        N_BC = 16 * 13

        @block.tensor
        def _(pe):
            pe.sem_inc(tr_full, 5 * NB)
            pe.sem_inc(proj_full, 6 * NB)
            pe.sem_inc(ot_full, 2 * NB)
            pe.sem_inc(y_full, NB)
            pe.sem_inc(sh_full, NB)
            pe.sem_inc(ft_full, NF)
            pe.sem_inc(gate_full, 3 * NF)
            pe.sem_inc(a_full, 3 * NF)
            pe.sem_inc(fy_full, NF)
            pe.wait_ge(const_ld, N_CONST)
            pe.wait_ge(setup_done, 2)

            def x_transpose(T):
                pe.wait_ge(z_staged, T + 1)
                pe.wait_ge(tr_evac, T * 5)
                pe.transpose(tr_ps[:, 0:128], z_stage[:], ident[:]).then_inc(tr_full, 1)

            def project(T, c, boundary=None):
                if c == 0:
                    pe.wait_ge(x_split, T + 1)
                if boundary is not None:
                    if c == 0:
                        pe.wait_ge(gelu_done, boundary * 12)
                        pe.wait_ge(h_ready, boundary * 12)
                        pe.wait_ge(w_split, boundary * 3)
                elif c < 2:
                    pe.wait_ge(v_ready, T * 2 + (c - 1))
                if 2 <= c:
                    pe.wait_ge(rotated, T * 4 + (c - 1))
                col = slice(CHUNK_COL[c], CHUNK_COL[c] + 512)
                ps = proj_ps[c % 2]
                pe.matmul(ps[:], x_hi[:], w_hi[:, col], start=True, stop=False)
                pe.matmul(ps[:], x_hi[:], w_lo[:, col], start=False, stop=False)
                pe.matmul(ps[:], x_lo[:], w_hi[:, col], start=False, stop=True).then_inc(proj_full, 1)

            def qk_transpose(T, c):
                pe.wait_ge(qk_ready, T * 4 + (c + 1))
                pe.wait_ge(tr_evac, T * 5 + (c + 1))
                for j in range(4):
                    mm = pe.transpose(tr_ps[:, 128 * j:128 * j + 128], qk[:, c, 128 * j:128 * j + 128], ident[:])
                mm.then_inc(tr_full, 1)

            def scores(T, par, g):
                pe.wait_ge(tr_evac, T * 5 + (2 * (g // 2) + 3))
                pe.wait_ge(masked, T * 4 + g)
                for j in range(GH):
                    pair, row = 2 * g + j // 2, 64 * (j % 2)
                    mm = pe.matmul(s_ps[:, j % 2, NT * (j // 2):NT * (j // 2 + 1)], q_T[par][row:row + 64, pair, :],
                                   k_T[par][row:row + 64, pair, :], start=True, stop=True)
                mm.then_inc(s_full, 1)

            def p_transpose(T, g, first=False):
                pe.wait_ge(p_ready, T * 4 + (g + 1))
                if not first:
                    pe.wait_ge(pt_evac, T * 4 + g)
                for j in range(GH):
                    mm = pe.transpose(pt_ps[:, 128 * j:128 * j + 128], p_sb[:, g % 2, j, :], ident[:])
                mm.then_inc(pt_full, 1)

            def values(T, par, g):
                pe.wait_ge(pt_evac, T * 4 + (g + 1))
                pe.wait_ge(v_ready, T * 2 + 2)
                pe.wait_ge(att_ready, T * 4 + g)
                for j in range(GH):
                    mm = pe.matmul(pv_ps[:, (DH + 1) * j:(DH + 1) * (j + 1)], p_T[:, g % 2, j, :],
                                   v[par][:, GH * g + j, :], start=True, stop=True)
                mm.then_inc(pv_full, 1)

            def att_transpose(T, i):
                pe.wait_ge(att_ready, T * 4 + (2 * i + 2))
                pe.wait_ge(ot_evac, T * 2 + i)
                if i == 0:
                    pe.wait_ge(xs_ready, T * 2)
                for j in range(4):
                    mm = pe.transpose(y_ps[:, 128 * j:128 * j + 128],
                                      att[:, 8 * i + 2 * j:8 * i + 2 * j + 2, :].rearrange("p a b -> p (a b)"), ident[:])
                mm.then_inc(ot_full, 1)

            def out_project(T, L):
                pe.wait_ge(ld_wo, L * 16)
                pe.wait_ge(ot_evac, T * 2 + 2)
                for c in range(8):
                    mm = pe.matmul(y_ps[:, 0:D], att_T[:, c, :], wo[:, c, :], start=(c == 0), stop=(c == 7))
                mm.then_inc(y_full, 1)

            def shift_state(T, src):
                pe.wait_ge(z_attn, T + 1)
                pe.matmul(y_ps[:, 0:D // 2], shift[:], src, start=True, stop=True).then_inc(sh_full, 1)

            def x_setup():
                pe.wait_ge(xw_ld, 64)
                for i in range(4):
                    mm = pe.transpose(pt_ps[:, 128 * i:128 * i + 128], xw_raw[:, i], ident[:])
                mm.then_inc(xw_full, 1)

            def x_inputs(T, par):
                pe.wait_ge(ctx_ld[par], (T - par) * 8 + 16)
                pe.wait_ge(xin_ready, T + 1)
                pe.transpose(tr_ps[:, 0:128], x_in[:, par], ident[:])
                pe.transpose(tr_ps[:, 128:256], c_in[:, par], ident[:]).then_inc(xt_full, 1)

            def x_project(T):
                pe.wait_ge(xt_evac, T + 1)
                if not isinstance(T, int) or T > 0:
                    pe.wait_ge(xv_ready, T)
                else:
                    pe.wait_ge(xw_evac, 1)
                pe.matmul(proj_ps[0][:, 0:128], xw_T[:, 0], xc_T[:, 0], start=True, stop=True)
                pe.matmul(proj_ps[0][:, 128:256], xw_T[:, 1], xc_T[:, 1], start=True, stop=True)
                pe.matmul(proj_ps[0][:, 256:384], xc_T[:, 1], xw_T[:, 2], start=True, stop=True).then_inc(xproj_full, 1)

            def x_scores(T, par, g, first=False):
                if g == 0:
                    pe.wait_ge(xk_ready, T + 1)
                if not (first and g == 0):
                    pe.wait_ge(masked, T * 4 + g)
                rows = slice(32 * g, 32 * g + 32)
                pe.matmul(s_ps[:, 0, :], xq[rows, par, :], flat(xk_bd[rows, par]), start=True, stop=True).then_inc(s_full, 1)

            def x_values(T, par, g, first=False):
                pe.wait_ge(pt_evac, T * 4 + (g + 1))
                pe.wait_ge(xv_ready, T + 1)
                if not (first and g == 0):
                    pe.wait_ge(att_ready, T * 4 + g)
                for j in range(GH):
                    mm = pe.matmul(pv_ps[:, (XD + 1) * j:(XD + 1) * (j + 1)], p_T[:, g % 2, j, :],
                                   xv[:, par, GH * g + j, :], start=True, stop=True)
                mm.then_inc(pv_full, 1)

            def x_out(T):
                pe.wait_ge(att_ready, T * 4 + 4)
                pe.transpose(y_ps[:, 0:128], x_att[:].rearrange("p h d -> p (h d)"), ident[:]).then_inc(xo_full, 1)

            def x_out_project(T):
                pe.wait_ge(xo_evac, T + 1)
                pe.matmul(y_ps[:, 0:128], x_att_T[:], xw_T[:, 3], start=True, stop=True).then_inc(xy_full, 1)

            def x_slot(T, par, first=False, front_on=True):
                x_scores(T, par, 0, first)
                if not first:
                    p_transpose(T - 1, 3)
                    x_values(T - 1, 1 - par, 2)
                x_scores(T, par, 1)
                p_transpose(T, 0, first)
                if not first:
                    x_values(T - 1, 1 - par, 3)
                x_scores(T, par, 2)
                p_transpose(T, 1)
                if front_on:
                    x_inputs(T + 1, 1 - par)
                if not first:
                    x_out(T - 1)
                x_values(T, par, 0, first)
                x_scores(T, par, 3)
                p_transpose(T, 2)
                if front_on:
                    x_project(T + 1)
                if not first:
                    x_out_project(T - 1)
                x_values(T, par, 1)

            x_setup()
            x_inputs(0, 0)
            x_project(0)
            x_slot(0, 0, first=True)
            with pe.Fori(0, NB // 2 - 1) as pair:
                x_slot(pair * 2 + 1, 1)
                x_slot(pair * 2 + 2, 0)
            x_slot(NB - 1, 1, front_on=False)
            p_transpose(NB - 1, 3)
            x_values(NB - 1, 1, 2)
            x_values(NB - 1, 1, 3)
            x_out(NB - 1)
            x_out_project(NB - 1)

            with pe.Fori(1, LAYERS + 1) as L:
                def front(T):
                    x_transpose(T)
                    for c in range(6):
                        project(T, c, boundary=L)
                    for c in range(4):
                        qk_transpose(T, c)
                    x_transpose(T + 1)

                def slot(T, n, par, first=False, behind=2, front_on=True, last_front=False):
                    scores(T, par, 0)
                    if behind >= 1:
                        p_transpose(T - 1, 3)
                    if front_on:
                        project(T + 1, 0)
                        project(T + 1, 1)
                    if behind >= 1:
                        values(T - 1, 1 - par, 2)
                    scores(T, par, 1)
                    p_transpose(T, 0)
                    if front_on:
                        project(T + 1, 2)
                        project(T + 1, 3)
                    if behind >= 2:
                        shift_state(T - 2, tile_of(z, n - 2, D // 2))
                    if behind >= 1:
                        values(T - 1, 1 - par, 3)
                    scores(T, par, 2)
                    p_transpose(T, 1)
                    if front_on:
                        project(T + 1, 4)
                        project(T + 1, 5)
                    if behind >= 1:
                        att_transpose(T - 1, 0)
                    values(T, par, 0)
                    if front_on:
                        qk_transpose(T + 1, 0)
                        qk_transpose(T + 1, 1)
                    scores(T, par, 3)
                    p_transpose(T, 2)
                    if behind >= 1:
                        att_transpose(T - 1, 1)
                    values(T, par, 1)
                    if front_on:
                        qk_transpose(T + 1, 2)
                        qk_transpose(T + 1, 3)
                        if not last_front:
                            x_transpose(T + 2)
                    if behind >= 1:
                        out_project(T - 1, L)

                def drain(T, n, par):
                    p_transpose(T - 1, 3)
                    values(T - 1, 1 - par, 2)
                    shift_state(T - 2, tile_of(z, n - 2, D // 2))
                    values(T - 1, 1 - par, 3)
                    att_transpose(T - 1, 0)
                    att_transpose(T - 1, 1)
                    out_project(T - 1, L)
                    shift_state(T - 1, tile_of(z, n - 1, D // 2))

                layer_slots(pe.Fori, L, front, slot, drain)

                def f_transpose(j):
                    F = L * NF + j
                    pe.wait_ge(xn_ready, L * NB + (FG * j + FG))
                    pe.wait_ge(ft_evac, F)
                    for i in range(FG):
                        mm = pe.transpose(pt_ps[:, 128 * i:128 * i + 128], xn[:, FG * j + i, :], ident[:])
                    mm.then_inc(ft_full, 1)

                def f_up(j, c):
                    F = L * NF + j
                    if c == 0:
                        pe.wait_ge(f_split, F + 1)
                    pe.wait_ge(w1_split, L)
                    for half, ps, full, free in ((1, proj_ps[0], gate_full, gelu_done), (0, proj_ps[1], a_full, h_ready)):
                        col = slice(half * FI + 128 * c, half * FI + 128 * c + FC[c])
                        pe.wait_ge(free, F * 3 + c)
                        o = ps[0:FC[c], :]
                        pe.matmul(o, w1_hi[:, col], f_hi[:, j % 2, :], start=True, stop=False)
                        pe.matmul(o, w1_hi[:, col], f_lo[:, j % 2, :], start=False, stop=False)
                        pe.matmul(o, w1_lo[:, col], f_hi[:, j % 2, :], start=False, stop=True).then_inc(full, 1)

                def f_down(j):
                    F = L * NF + j
                    pe.wait_ge(ld_w2, L * 64 - 16)
                    pe.wait_ge(h_ready, F * 3 + 3)
                    pe.wait_ge(z_ready, F + 12)
                    for i in range(FG):
                        for c in range(3):
                            k = FC[c] + (c == 2)
                            mm = pe.matmul(s_ps[:, 0, 128 * i:128 * i + 128], h_T[j % 2][c][0:k, 128 * i:128 * i + 128],
                                           w2[0:k, c, :], start=(c == 0), stop=(c == 2))
                    mm.then_inc(fy_full, 1)

                f_transpose(0)
                for j in range(NF):
                    if j + 1 < NF:
                        f_transpose(j + 1)
                    f_up(j, 0)
                    if j >= 1:
                        f_down(j - 1)
                    f_up(j, 1)
                    f_up(j, 2)
                f_down(NF - 1)

        @block.scalar
        def _(act):
            act.sem_inc(tr_evac, 5 * NB)
            act.sem_inc(squared, 4 * NB)
            act.sem_inc(inv_log, 2 * NB)
            act.sem_inc(inv_ready, 2 * NB)
            act.sem_inc(v_ready, 2 * NB)
            act.sem_inc(ot_evac, 2 * NB)
            act.sem_inc(log_done, NB)
            act.sem_inc(rstd_ready, NB)
            act.sem_inc(ft_evac, NF)
            act.sem_inc(gelu_done, 3 * NF)
            act.preload_act_table_set("natural_log_exp_and_others")
            act.wait_ge(setup_done, 2)
            act.wait_ge(const_ld, N_CONST)

            def x_out(T):
                act.wait_ge(tr_full, T * 5 + 1)
                half = D // 2
                for dst in (x_all, x_hi):
                    act.activation(dst[0:half, :], tr_ps[0:half, 0:NT], ACT.Copy)
                    last = act.activation(dst[half:D, 1:NT], tr_ps[half:D, 0:NT - 1], ACT.Copy)
                last.then_inc(tr_evac, 1)

            def square_chunk(T, c):
                act.wait_ge(proj_full, T * 6 + (c + 1))
                act.wait_ge(summed, T * 4 + (c - 1))
                act.activation(square[:, c % 2, :], proj_ps[c % 2][:], ACT.Square).then_inc(squared, 1)

            def norms(T, i):
                act.wait_ge(norm_ready, T * 2 + (i + 1))
                act.activation(log_sq[:, i, :], sumsq[:, i, :], ACT.Ln).then_inc(inv_log, 1)
                act.wait_ge(inv_log, T * 2 + (i + 1))
                act.activation(inv_norm[:, i, :], log_sq[:, i, :], ACT.Exp, scale=-0.5).then_inc(inv_ready, 1)

            def qk_out(T, par, c):
                act.wait_ge(tr_full, T * 5 + (c + 2))
                dst = (q_T, k_T)[c % 2][par]
                i = c // 2
                act.activation(flat(dst[:, 4 * i:4 * i + 4, :]), tr_ps[:], ACT.Copy).then_inc(tr_evac, 1)

            def v_out(T, par, i):
                act.wait_ge(proj_full, T * 6 + (5 + i))
                act.activation(v[par][:, 8 * i:8 * i + 8, 0:DH], proj_ps[i][:].rearrange("p (h d) -> p h d", d=DH),
                               ACT.Copy).then_inc(v_ready, 1)

            def exps(T, g, first=False):
                act.wait_ge(centered, T * 4 + (g + 1))
                if not first:
                    act.wait_ge(pt_full, T * 4 + (g - 1))
                act.activation(flat(p_sb[:, g % 2]), flat(s_sb[:, g % 2]), ACT.Exp).then_inc(p_ready, 1)

            def p_out(T, g):
                act.wait_ge(pt_full, T * 4 + (g + 1))
                act.activation(flat(p_T[:, g % 2]), pt_ps[:], ACT.Copy).then_inc(pt_evac, 1)

            def att_out(T, i):
                act.wait_ge(ot_full, T * 2 + (i + 1))
                act.activation(flat(att_T[:, 4 * i:4 * i + 4, :]), y_ps[:], ACT.Copy).then_inc(ot_evac, 1)

            def ln_std(T):
                act.wait_ge(var_ready, T + 1)
                act.activation(log_var[:], mean_var[:, 1:2], ACT.Ln, bias=eps[:]).then_inc(log_done, 1)
                act.wait_ge(log_done, T + 1)
                act.activation(rstd[:], log_var[:], ACT.Exp, scale=-0.5).then_inc(rstd_ready, 1)

            act.wait_ge(bc_ld, N_BC)
            act.activation(tanh_g[:], gates[:, 2:4], ACT.Tanh).then_inc(tanh_done, 1)
            act.preload_act_table_set("natural_log_exp_and_others")
            act.wait_ge(xw_full, 1)
            act.activation(flat(xw_T[:]), pt_ps[:], ACT.Copy).then_inc(xw_evac, 1)
            act.wait_ge(xvar_ready, 1)
            act.activation(x_log[:], x_mv[:, :, 1], ACT.Ln, bias=eps[:]).then_inc(xlog_done, 1)
            act.wait_ge(xlog_done, 1)
            act.activation(x_rstd[:], x_log[:], ACT.Exp, scale=-0.5).then_inc(xrstd_ready, 1)
            act.wait_ge(scalar_ready, 1)

            def x_inputs_out(T):
                act.wait_ge(xt_full, T + 1)
                act.activation(flat(xc_T[:]), tr_ps[:, 0:256], ACT.Copy).then_inc(xt_evac, 1)

            def x_qk_out(T, par):
                act.wait_ge(xproj_full, T + 1)
                if not isinstance(T, int):
                    act.wait_ge(xk_ready, T)
                act.activation(xq[:, par], proj_ps[0][:, 0:128], ACT.Identity, bias=q_scale[:, 1:2], scale=q_scale[:, 0:1])
                act.activation(xk[:], proj_ps[0][:, 128:256], ACT.Identity, bias=xb_col[:, 1:2]).then_inc(xqk_out, 1)

            def x_att_out(T):
                act.wait_ge(xo_full, T + 1)
                act.activation(x_att_T[:], y_ps[:, 0:128], ACT.Copy).then_inc(xo_evac, 1)

            def x_slot(T, par, first=False, front_on=True):
                if not first:
                    p_out(T - 1, 3)
                exps(T, 0, first)
                p_out(T, 0)
                exps(T, 1, first)
                p_out(T, 1)
                if front_on:
                    x_inputs_out(T + 1)
                if not first:
                    x_att_out(T - 1)
                exps(T, 2)
                p_out(T, 2)
                if front_on:
                    x_qk_out(T + 1, 1 - par)
                exps(T, 3)

            x_inputs_out(0)
            x_qk_out(0, 0)
            x_slot(0, 0, first=True)
            with act.Fori(0, NB // 2 - 1) as pair:
                x_slot(pair * 2 + 1, 1)
                x_slot(pair * 2 + 2, 0)
            x_slot(NB - 1, 1, front_on=False)
            p_out(NB - 1, 3)
            x_att_out(NB - 1)
            act.wait_ge(xvar_ready, 2)
            act.activation(x_log[:], x_mv[:, :, 1], ACT.Ln, bias=eps[:]).then_inc(xlog_done, 1)
            act.wait_ge(xlog_done, 2)
            act.activation(x_rstd[:], x_log[:], ACT.Exp, scale=-0.5).then_inc(xrstd_ready, 1)

            with act.Fori(1, LAYERS + 1) as L:
                act.preload_act_table_set("natural_log_exp_and_others")

                def front(T):
                    x_out(T)
                    for i in range(2):
                        square_chunk(T, 2 * i)
                        square_chunk(T, 2 * i + 1)
                        norms(T, i)
                    v_out(T, 0, 0)
                    v_out(T, 0, 1)
                    for c in range(4):
                        qk_out(T, 0, c)
                    x_out(T + 1)

                def slot(T, n, par, first=False, behind=2, front_on=True, last_front=False):
                    if behind >= 1:
                        p_out(T - 1, 3)
                    if front_on:
                        square_chunk(T + 1, 0)
                        square_chunk(T + 1, 1)
                    exps(T, 0)
                    if front_on:
                        norms(T + 1, 0)
                    p_out(T, 0)
                    if front_on:
                        square_chunk(T + 1, 2)
                        square_chunk(T + 1, 3)
                    exps(T, 1)
                    if front_on:
                        norms(T + 1, 1)
                    if behind >= 2:
                        ln_std(T - 2)
                    p_out(T, 1)
                    if front_on:
                        v_out(T + 1, 1 - par, 0)
                        v_out(T + 1, 1 - par, 1)
                    exps(T, 2)
                    if behind >= 1:
                        att_out(T - 1, 0)
                    if front_on:
                        qk_out(T + 1, 1 - par, 0)
                        qk_out(T + 1, 1 - par, 1)
                    p_out(T, 2)
                    exps(T, 3)
                    if behind >= 1:
                        att_out(T - 1, 1)
                    if front_on:
                        qk_out(T + 1, 1 - par, 2)
                        qk_out(T + 1, 1 - par, 3)
                        if not last_front:
                            x_out(T + 2)

                def drain(T, n, par):
                    p_out(T - 1, 3)
                    ln_std(T - 2)
                    att_out(T - 1, 0)
                    att_out(T - 1, 1)
                    ln_std(T - 1)

                layer_slots(act.Fori, L, front, slot, drain)

                act.preload_act_table_set("gelu_and_others")

                def f_out(j):
                    F = L * NF + j
                    act.wait_ge(ft_full, F + 1)
                    for dst in (f_all, f_hi):
                        last = act.activation(dst[:, j % 2, :], pt_ps[:], ACT.Identity,
                                              bias=param[:, 1:2], scale=param[:, 0:1])
                    last.then_inc(ft_evac, 1)

                def f_gelu(j, c):
                    F = L * NF + j
                    act.wait_ge(gate_full, F * 3 + (c + 1))
                    if j or c == 2:
                        act.wait_ge(h_ready, F * 3 + (c - 1))
                    m = FC[c]
                    act.activation(gelu[0:m, (3 * j + c) % 2, :], proj_ps[0][0:m, :], ACT.Gelu,
                                   bias=param[0:m, 5 + c:6 + c]).then_inc(gelu_done, 1)

                act.wait_ge(param_ready, L)
                f_out(0)
                for j in range(NF):
                    if j + 1 < NF:
                        f_out(j + 1)
                    for c in range(3):
                        f_gelu(j, c)

        @block.vector
        def _(dve):
            dve.sem_inc(rotated, 4 * NB)
            dve.sem_inc(summed, 4 * NB)
            dve.sem_inc(norm_ready, 2 * NB)
            dve.sem_inc(z_attn, NB)
            dve.sem_inc(xs_ready, 2 * NB)
            dve.sem_inc(stat_done, NB)
            dve.sem_inc(var_ready, NB)
            dve.sem_inc(xn_ready, NB)
            dve.sem_inc(h_ready, 3 * NF)
            dve.sem_inc(z_staged, NB)
            dve.memset(eps[:], LN_EPS)
            for i in range(2):
                dve.memset(v[i][:, :, DH], 1.0)
                dve.memset(h_T[i][2][:], 1.0)
            dve.memset(x_all[:], 0.0)
            dve.memset(x_hi[:].bitcast(f32), 0.0).then_inc(setup_done, 1)
            dve.wait_ge(const_ld, N_CONST)
            for i in range(4):
                last = dve.tensor_tensor(tab[:, i], qk_scale[:, i // 2],
                                         rot[:, i, :].unsqueeze(1).to_broadcast([128, LAYERS, DH]), ALU.mult)
            last.then_inc(setup_done, 1)
            dve.wait_ge(setup_done, 2)

            def w_round(k, L1):
                col = slice(INNER * k, INNER * (k + 1))
                dve.tensor_copy(w_hi[:, col], w_raw[:, col]).then_inc(w_hi_done, 1)

            dve.wait_ge(ld_w, 16)
            for k in range(3):
                w_round(k, 0)

            def rotate(T, c, L):
                dve.wait_ge(squared, T * 4 + (c + 1))
                dve.wait_ge(qk_added, T * 4 + (c - 1))
                ps = proj_ps[c % 2][:].rearrange("p (h d) -> p h d", d=DH)
                for dst, i in ((by_cos, 0), (by_sin, 1)):
                    tb = tab[:, 2 * (c % 2) + i, bass.ds(L - 1, 1), :].to_broadcast([128, 8, DH])
                    last = dve.tensor_tensor(dst[:, c % 2, :].rearrange("p (h d) -> p h d", d=DH), ps, tb, ALU.mult)
                last.then_inc(rotated, 1)
                i = c // 2
                dve.tensor_reduce(sumsq[:, i, 8 * (c % 2):8 * (c % 2) + 8],
                                  square[:, c % 2, :].rearrange("p (h d) -> p h d", d=DH), AX, ALU.add).then_inc(summed, 1)

            def clamp_norm(T, i):
                dve.wait_ge(summed, T * 4 + (2 * i + 2))
                dve.tensor_scalar(sumsq[:, i, :], sumsq[:, i, :], 1e-24, None, ALU.max).then_inc(norm_ready, 1)

            def mask(T, g):
                dve.wait_ge(s_full, T * 4 + (g + 1))
                dve.wait_ge(p_ready, T * 4 + (g - 1))
                dve.tensor_tensor(s_sb[:, g % 2].rearrange("p (a b) k -> p b a k", b=2),
                                  s_ps[:, :, 0:GH // 2 * NT].rearrange("p b (a k) -> p b a k", k=NT),
                                  band[:].unsqueeze(1).unsqueeze(1).to_broadcast([128, 2, GH // 2, NT]),
                                  ALU.add).then_inc(masked, 1)
                dve.wait_ge(masked, T * 4 + (g + 1))
                dve.tensor_reduce(row_max[:, g % 2, :], s_sb[:, g % 2], AX, ALU.max).then_inc(max_ready, 1)

            def normalise(T, g):
                dve.wait_ge(pv_full, T * 4 + (g + 1))
                o = pv_ps[:, 0:GH * (DH + 1)].rearrange("p (h d) -> p h d", d=DH + 1)
                dve.reciprocal(inv_sum[:], o[:, :, DH]).then_inc(recip_done, 1)
                dve.wait_ge(recip_done, T * 4 + (g + 1))
                dve.tensor_tensor(att[:, GH * g:GH * g + GH, :], o[:, :, 0:DH],
                                  inv_sum[:].unsqueeze(2).to_broadcast([128, GH, DH]), ALU.mult).then_inc(att_ready, 1)

            dve.wait_ge(x_ld, 16)

            def x_moments(src, time):
                for b in range(NB):
                    last = dve.bn_stats(x_st[:, b], src[:, b])
                last.then_inc(xstat_done, 1)
                dve.wait_ge(xstat_done, time)
                for b in range(NB):
                    last = dve.bn_aggr(x_mv[:, b], x_st[:, b])
                last.then_inc(xvar_ready, 1)

            x_moments(x_res, 1)
            dve.memset(xv[:, :, :, XD], 1.0).then_inc(xscaled, 1)
            dve.wait_ge(bc_ld, N_BC)
            dve.tensor_scalar(q_scale[:, 0:1], gates[:, 0:1], float(XD) ** -0.5, None, ALU.mult).then_inc(xscaled, 1)
            dve.tensor_scalar(alpha[:, :, :], alpha[:, :, :], gates[:, 1:2], None, ALU.mult).then_inc(xscaled, 1)
            dve.wait_ge(xscaled, 3)
            dve.tensor_tensor(q_scale[:, 1:2], xb_col[:, 0:1], q_scale[:, 0:1], ALU.mult).then_inc(scalar_ready, 1)
            dve.wait_ge(tanh_done, 1)
            dve.tensor_scalar(xb_row[:, 1], xb_row[:, 1], tanh_g[:, 0:1], None, ALU.mult).then_inc(xscaled, 1)
            dve.wait_ge(xrstd_ready, 1)

            def x_normalise(T, par):
                if not isinstance(T, int):
                    dve.wait_ge(xt_full, T - 1)
                b = T if isinstance(T, int) else None
                src = x_res[:, T] if isinstance(T, int) else tile_of(x_res, T)
                mu = x_mv[:, T, 0:1] if b is not None else x_mv[:, bass.ds(T, 1), 0]
                rs = x_rstd[:, T:T + 1] if b is not None else x_rstd[:, bass.ds(T, 1)]
                dve.tensor_scalar(x_in[:, par], src, mu, rs, ALU.subtract, ALU.mult).then_inc(xin_ready, 1)

            def x_value_out(T, par):
                dve.wait_ge(xqk_out, T + 1)
                dve.tensor_tensor(xv[:, par, :, 0:XD], proj_ps[0][:, 256:384].rearrange("p (h d) -> p h d", d=XD),
                                  xb_row[:, 0].rearrange("p (h d) -> p h d", d=XD), ALU.add).then_inc(xv_ready, 1)

            def x_clip(T, par, n3):
                if not isinstance(T, int):
                    dve.wait_ge(bias_ready, T * 4 - 4)
                src = frac_k[:, T] if isinstance(T, int) else tile_of(frac_k, T)
                fq = frac_q[:, T:T + 1] if isinstance(T, int) else frac_q[:, bass.ds(T, 1)]
                dve.tensor_scalar(d_clip[:, par], src, fq, -CLAMP, ALU.subtract, ALU.max).then_inc(xclip, 1)
                dve.wait_ge(xclip, T + 1)
                dve.tensor_scalar(d_neg[:, par], d_clip[:, par], 0.0, None, ALU.min)
                dve.tensor_scalar(d_pos[:, par], d_clip[:, par], CLAMP, 0.0, ALU.min, ALU.max).then_inc(clip_ready, 1)

            def x_bias(T, par, g, first=False):
                G = T * 4 + g
                if not (first and g == 0):
                    dve.wait_ge(added_pos, G)
                dve.wait_ge(clip_ready, T + 1)
                dve.tensor_tensor(bias_neg[:], d_neg[:, par].unsqueeze(1).to_broadcast([128, GH, NT]),
                                  alpha[:, 1, GH * g:GH * g + GH].unsqueeze(2).to_broadcast([128, GH, NT]),
                                  ALU.mult).then_inc(neg_ready, 1)
                dve.wait_ge(s_full, G + 1)
                dve.wait_ge(bias_ready, G + 1)
                if not first:
                    dve.wait_ge(p_ready, G - 1)
                dve.tensor_tensor(s_sb[:, g % 2], s_ps[:, 0, :].rearrange("p (h k) -> p h k", k=NT),
                                  bias_pos[:, g % 2], ALU.add).then_inc(masked, 1)
                dve.wait_ge(masked, G + 1)
                dve.wait_ge(neg_ready, G + 1)
                dve.tensor_tensor(s_sb[:, g % 2], s_sb[:, g % 2], bias_neg[:], ALU.add).then_inc(added_pos, 1)
                dve.wait_ge(added_pos, G + 1)
                dve.tensor_reduce(row_max[:, g % 2, :], s_sb[:, g % 2], AX, ALU.max).then_inc(max_ready, 1)

            def x_attention(T, g):
                dve.wait_ge(pv_full, T * 4 + (g + 1))
                o = pv_ps[:, 0:GH * (XD + 1)].rearrange("p (h d) -> p h d", d=XD + 1)
                dve.reciprocal(inv_sum[:], o[:, :, XD]).then_inc(recip_done, 1)
                dve.wait_ge(recip_done, T * 4 + (g + 1))
                dve.tensor_tensor(x_att[:, GH * g:GH * g + GH, :], o[:, :, 0:XD],
                                  inv_sum[:].unsqueeze(2).to_broadcast([128, GH, XD]), ALU.mult).then_inc(att_ready, 1)

            def x_add(T):
                dve.wait_ge(xy_full, T + 1)
                xt = x_res[:, T] if isinstance(T, int) else tile_of(x_res, T)
                dve.scalar_tensor_tensor(xt, y_ps[:, 0:D], tanh_g[:, 0:1], xt, ALU.mult, ALU.add).then_inc(xy_ready, 1)

            def x_gate_bias(T):
                xt = x_res[:, T] if isinstance(T, int) else tile_of(x_res, T)
                dve.tensor_tensor(xt, xt, xb_row[:, 1], ALU.add).then_inc(xg_ready, 1)

            def x_slot(T, par, first=False, front_on=True):
                x_bias(T, par, 0, first)
                if not first:
                    x_attention(T - 1, 2)
                x_bias(T, par, 1, first)
                if front_on:
                    x_normalise(T + 1, 1 - par)
                if not first:
                    x_attention(T - 1, 3)
                x_bias(T, par, 2)
                if front_on:
                    x_gate_bias(T)
                    x_clip(T + 1, 1 - par, None)
                x_attention(T, 0)
                x_bias(T, par, 3)
                if front_on:
                    x_value_out(T + 1, 1 - par)
                if not first:
                    dve.wait_ge(xg_ready, T)
                    x_add(T - 1)
                x_attention(T, 1)

            dve.wait_ge(xscaled, 4)
            x_normalise(0, 0)
            x_clip(0, 0, None)
            x_value_out(0, 0)
            x_slot(0, 0, first=True)
            with dve.Fori(0, NB // 2 - 1) as pair:
                x_slot(pair * 2 + 1, 1)
                x_slot(pair * 2 + 2, 0)
            x_slot(NB - 1, 1, front_on=False)
            x_attention(NB - 1, 2)
            x_attention(NB - 1, 3)
            x_gate_bias(NB - 1)
            dve.wait_ge(xg_ready, NB)
            x_add(NB - 1)
            dve.wait_ge(xy_ready, NB)
            x_moments(x_res, 2)
            dve.wait_ge(xrstd_ready, 2)
            for b in range(NB):
                dve.tensor_scalar(z[:, b], x_res[:, b], x_mv[:, b, 0:1], x_rstd[:, b:b + 1],
                                  ALU.subtract, ALU.mult).then_inc(z_ready, 1)

            with dve.Fori(1, LAYERS + 1) as L:
                def add_out(T, n):
                    dve.wait_ge(y_full, T + 1)
                    zt = tile_of(z, n)
                    dve.tensor_tensor(zt, zt, y_ps[:, 0:D], ALU.add).then_inc(z_attn, 1)

                def ln_stats(T, n):
                    zt = tile_of(z, n, 0, D // 2)
                    dve.wait_ge(sh_full, T + 1)
                    dve.tensor_scalar(xs[:, 0:D // 2], zt, 1.0, None, ALU.mult).then_inc(xs_ready, 1)
                    dve.tensor_copy(xs[:, D // 2:D], y_ps[:, 0:D // 2]).then_inc(xs_ready, 1)
                    dve.wait_ge(xs_ready, T * 2 + 2)
                    dve.bn_stats(stats[:], xs[:]).then_inc(stat_done, 1)

                def ln_variance(T):
                    dve.bn_aggr(mean_var[:], stats[:]).then_inc(var_ready, 1)

                def ln_apply(T, n):
                    dve.wait_ge(rstd_ready, T + 1)
                    dve.tensor_scalar(tile_of(xn, n), xs[:],
                                      mean_var[:, 0:1], rstd[:], ALU.subtract, ALU.mult).then_inc(xn_ready, 1)

                def stage(T, n, groups_done):
                    dve.wait_ge(z_ready, groups_done)
                    dve.wait_ge(tr_full, T * 5 - 4)
                    dve.tensor_scalar(z_stage[:], tile_of(z, n), 1.0, None, ALU.mult).then_inc(z_staged, 1)

                def front(T):
                    stage(T, 0, L * 4 + 12)
                    for i in range(2):
                        rotate(T, 2 * i, L)
                        rotate(T, 2 * i + 1, L)
                        clamp_norm(T, i)
                    stage(T + 1, 1, L * 4 + 12)

                def slot(T, n, par, first=False, behind=2, front_on=True, last_front=False):
                    mask(T, 0)
                    if front_on:
                        rotate(T + 1, 0, L)
                        rotate(T + 1, 1, L)
                        clamp_norm(T + 1, 0)
                    if behind >= 1:
                        normalise(T - 1, 2)
                    mask(T, 1)
                    if front_on:
                        rotate(T + 1, 2, L)
                        rotate(T + 1, 3, L)
                        clamp_norm(T + 1, 1)
                    if behind >= 2:
                        ln_stats(T - 2, n - 2)
                        dve.wait_ge(stat_done, T - 1)
                    if behind >= 1:
                        normalise(T - 1, 3)
                    if behind >= 2:
                        ln_variance(T - 2)
                    mask(T, 2)
                    if behind >= 2:
                        ln_apply(T - 2, n - 2)
                    normalise(T, 0)
                    if front_on and not last_front:
                        stage(T + 2, n + 2, L * 4 + 12)
                    mask(T, 3)
                    normalise(T, 1)
                    if behind >= 1:
                        add_out(T - 1, n - 1)
                    if first:
                        dve.wait_ge(ld_w1, L * 16)
                        dve.tensor_copy(w1_hi[:], w1_raw[:]).then_inc(w1_hi_done, 1)
                        dve.tensor_scalar(param[:], params[:, bass.ds(L - 1, 1), :].rearrange("p a b -> p (a b)"), 1.0, None,
                                          ALU.mult).then_inc(param_ready, 1)

                def drain(T, n, par):
                    normalise(T - 1, 2)
                    ln_stats(T - 2, n - 2)
                    dve.wait_ge(stat_done, T - 1)
                    normalise(T - 1, 3)
                    ln_variance(T - 2)
                    ln_apply(T - 2, n - 2)
                    add_out(T - 1, n - 1)
                    ln_stats(T - 1, n - 1)
                    dve.wait_ge(ld_w, L * 16 + 16)
                    dve.wait_ge(stat_done, T)
                    w_round(0, L + 1)
                    ln_variance(T - 1)
                    ln_apply(T - 1, n - 1)

                layer_slots(dve.Fori, L, front, slot, drain)

                def f_gate(j, c):
                    F = L * NF + j
                    dve.wait_ge(gelu_done, F * 3 + (c + 1))
                    dve.wait_ge(a_full, F * 3 + (c + 1))
                    m = FC[c]
                    dve.scalar_tensor_tensor(h_T[j % 2][c][0:m, :], proj_ps[1][0:m, :], param[0:m, 2 + c:3 + c],
                                             gelu[0:m, (3 * j + c) % 2, :], ALU.add, ALU.mult).then_inc(h_ready, 1)

                def f_add(j):
                    F = L * NF + j
                    dve.wait_ge(fy_full, F + 1)
                    zg = flat(z[:, FG * j:FG * j + FG, :])
                    dve.tensor_tensor(zg, zg, s_ps[:, 0], ALU.add).then_inc(z_ready, 1)

                for j in range(NF):
                    f_gate(j, 0)
                    if j < 2:
                        w_round(j + 1, L + 1)
                    if j >= 1:
                        f_add(j - 1)
                    f_gate(j, 1)
                    f_gate(j, 2)
                f_add(NF - 1)

            dve.wait_ge(z_ready, NB + NF * LAYERS)
            dve.scalar_tensor_tensor(flat(z[:]), flat(z[:]), tanh_g[:, 1:2], flat(x_res[:]), ALU.mult, ALU.add).then_inc(result_ready, 1)

        @block.gpsimd
        def _(pool):
            pool.sem_inc(qk_added, 4 * NB)
            pool.sem_inc(qk_ready, 4 * NB)
            pool.sem_inc(x_split, NB)
            pool.sem_inc(f_split, NF)
            pool.memset(params[:], 0.0).then_inc(params_clear, 1)

            def w_rest(k, done):
                pool.wait_ge(w_hi_done, done)
                col = slice(INNER * k, INNER * (k + 1))
                pool.tensor_tensor(w_lo[:, col], w_raw[:, col], w_hi[:, col].bitcast(f32), ALU.subtract).then_inc(w_split, 1)

            for k in range(3):
                w_rest(k, k + 1)

            def split_x(T):
                pool.wait_ge(tr_evac, T * 5 + 1)
                pool.tensor_tensor(x_lo[:], x_all[:], x_hi[:].bitcast(f32), ALU.subtract).then_inc(x_split, 1)

            def add_rotated(T, c):
                pool.wait_ge(rotated, T * 4 + (c + 1))
                pool.wait_ge(tr_full, T * 5 + (c - 3))
                pool.tensor_tensor(heads(qk[:, c, :]), heads(by_cos[:, c % 2, :]),
                                   heads(by_sin[:, c % 2, :])[:, :, ::-1, :], ALU.add).then_inc(qk_added, 1)

            def scale_rotated(T, c):
                i = c // 2
                pool.wait_ge(qk_added, T * 4 + (c + 1))
                pool.wait_ge(inv_ready, T * 2 + (i + 1))
                ap = qk[:, c, :].rearrange("p (h d) -> p h d", d=DH)
                pool.tensor_tensor(ap, ap, inv_norm[:, i, 8 * (c % 2):8 * (c % 2) + 8].unsqueeze(2).to_broadcast([128, 8, DH]),
                                   ALU.mult).then_inc(qk_ready, 1)

            def center(T, g):
                pool.wait_ge(max_ready, T * 4 + (g + 1))
                pool.tensor_tensor(s_sb[:, g % 2], s_sb[:, g % 2],
                                   row_max[:, g % 2, :].unsqueeze(2).to_broadcast([128, GH, NT]), ALU.subtract).then_inc(centered, 1)

            def x_keys(T, par):
                pool.wait_ge(xqk_out, T + 1)
                pool.tensor_tensor(xk_bd[:, par], xk[:].unsqueeze(1).to_broadcast([128, GH, NT]),
                                   head_of[:].unsqueeze(2).to_broadcast([128, GH, NT]), ALU.mult).then_inc(xk_ready, 1)

            def x_bias_pos(T, par, g, first=False):
                if not (first and g < 2):
                    pool.wait_ge(masked, T * 4 + (g - 1))
                pool.wait_ge(clip_ready, T + 1)
                pool.tensor_tensor(bias_pos[:, g % 2], d_pos[:, par].unsqueeze(1).to_broadcast([128, GH, NT]),
                                   alpha[:, 0, GH * g:GH * g + GH].unsqueeze(2).to_broadcast([128, GH, NT]),
                                   ALU.mult).then_inc(bias_ready, 1)

            def x_slot(T, par, first=False, front_on=True):
                x_bias_pos(T, par, 1, first)
                center(T, 0)
                x_bias_pos(T, par, 2)
                center(T, 1)
                x_bias_pos(T, par, 3)
                center(T, 2)
                if front_on:
                    x_bias_pos(T + 1, 1 - par, 0)
                    x_keys(T + 1, 1 - par)
                center(T, 3)

            pool.wait_ge(bc_ld, N_BC)
            pool.wait_ge(scalar_ready, 1)
            x_bias_pos(0, 0, 0, first=True)
            x_keys(0, 0)
            x_slot(0, 0, first=True)
            with pool.Fori(0, NB // 2 - 1) as pair:
                x_slot(pair * 2 + 1, 1)
                x_slot(pair * 2 + 2, 0)
            x_slot(NB - 1, 1, front_on=False)

            with pool.Fori(1, LAYERS + 1) as L:
                def pair(T, i):
                    add_rotated(T, 2 * i)
                    add_rotated(T, 2 * i + 1)
                    scale_rotated(T, 2 * i)
                    scale_rotated(T, 2 * i + 1)

                def front(T):
                    split_x(T)
                    pair(T, 0)
                    pair(T, 1)
                    split_x(T + 1)

                def slot(T, n, par, first=False, behind=2, front_on=True, last_front=False):
                    center(T, 0)
                    if front_on:
                        pair(T + 1, 0)
                    center(T, 1)
                    if front_on:
                        pair(T + 1, 1)
                    center(T, 2)
                    center(T, 3)
                    if front_on and not last_front:
                        split_x(T + 2)
                    if first:
                        pool.wait_ge(w1_hi_done, L)
                        pool.tensor_tensor(w1_lo[:], w1_raw[:], w1_hi[:].bitcast(f32), ALU.subtract).then_inc(w1_split, 1)

                def drain(T, n, par):
                    pass

                layer_slots(pool.Fori, L, front, slot, drain)

                for j in range(NF):
                    F = L * NF + j
                    pool.wait_ge(ft_evac, F + 1)
                    pool.tensor_tensor(f_lo[:, j % 2, :], f_all[:, j % 2, :], f_hi[:, j % 2, :].bitcast(f32),
                                       ALU.subtract).then_inc(f_split, 1)
                    if j < 3:
                        w_rest(j, L * 3 + (j + 1))


def constants():
    one = np.float32
    half = np.arange(0, DH, 2, dtype=np.float32)
    inv_freq = (one(1.0) / one(10000.0) ** (half / one(DH))).astype(np.float32)
    pos = np.arange(NT, dtype=np.float32)
    freqs = pos[:, None] * inv_freq[None, :]
    base = (half + one(0.4 * DH)) / one(1.4 * DH)
    power = (pos - NT // 2) / one(WINDOW // 2)
    scale = base[None, :] ** power[:, None]
    cos, sin = np.cos(freqs), np.sin(freqs)
    rot = np.zeros((NT, 4, DH), np.float32)
    for i, s in ((0, QK_SCALE * scale), (2, 1.0 / scale)):
        rot[:, i] = np.concatenate([cos * s, cos * s], 1)
        rot[:, i + 1] = np.concatenate([sin * s, -sin * s], 1)
    p = np.arange(128)
    d = p[:, None] - p[None, :]
    band = np.where((d >= 0) & (d <= WINDOW), 0.0, NEG).astype(np.float32)
    head_of = (np.arange(128)[:, None] // XD % GH == np.arange(GH)[None, :]).astype(np.float32)
    return {"head_of": head_of, "ident": np.eye(128, dtype=np.float32), "shift": np.eye(128, k=1, dtype=np.float32),
            "band": band, "rot": rot.reshape(NT, 4 * DH)}


NAMES = ['x', 'ctx_1024', 'fside_BxS2_0', 'g_xattn', 'g_ffn', 'L0_xattn_Wq', 'L0_xattn_bq', 'L0_xattn_Wk', 'L0_xattn_bk',
         'L0_xattn_Wv', 'L0_xattn_bv', 'L0_xattn_Wo', 'L0_xattn_bo', 'L0_xattn_alpha_pos', 'L0_xattn_alpha_neg',
         'L0_xattn_gamma', 'L0_xattn_delta', 'L0_ffn_Wqkv', 'L0_ffn_q_scale', 'L0_ffn_k_scale', 'L0_ffn_Wo',
         'L0_ffn_ln_g', 'L0_ffn_ln_b', 'L0_ffn_W1', 'L0_ffn_b1', 'L0_ffn_W2', 'L0_ffn_b2']


def kernel(**inputs):
    import numpy as _np
    import concourse.bacc as _bacc
    from concourse import mybir as _mybir
    from concourse.bass_utils import run_bass_kernel_spmd as _run

    nc = _bacc.Bacc("TRN2", target_bir_lowering=False, num_devices=1)
    arrays, args = {}, {}
    given = {n: inputs[n] for n in NAMES} | constants()
    for name, a in given.items():
        a = _np.ascontiguousarray(a)
        arrays[f"in_{name}"] = a
        args[name] = nc.dram_tensor(f"in_{name}", a.shape, _mybir.dt.from_np(a.dtype), kind="ExternalInput").ap()
    args["out"] = nc.dram_tensor("out_0", (NB, NT, D), _mybir.dt.float32, kind="ExternalOutput").ap()
    build(nc, args)
    r = _run(nc, [arrays], core_ids=[0])
    return r.results[0]["out_0"]
```

```python
from contextlib import ExitStack

import concourse.bass as bass
import numpy as np
from concourse import mybir

f32 = mybir.dt.float32
f32r = mybir.dt.float32r
ALU = mybir.AluOpType
ACT = mybir.ActivationFunctionType
AX = mybir.AxisListType.X

NB, NT, D = 16, 128, 128
H, DH = 16, 64
HALF = DH // 2
LAYERS = 6
INNER = H * DH
WINDOW = 32
QK_SCALE = 8.0
FI = D * 4 * 2 // 3
FC = [128, 128, FI - 256]
XH, XD = 16, 8
GH = 4
NG = H // GH
FG = 4
NF = NB // FG
CLAMP = 0.2
NEG = -1.0e30
LN_EPS = 1e-5
CHUNK_COL = [0, INNER, 2 * INNER, 512, 2 * INNER + 512, INNER + 512]
QK_AT = [0, 1, 3, 5]
V_AT = [2, 4]


def build(nc, t):
    ctx = ExitStack()
    with ctx:
        ctx.enter_context(nc.allow_non_contiguous_dma(reason="small vectors laid along the partitions"))

        def sb(name, shape, dt=f32):
            return ctx.enter_context(nc.sbuf_tensor(name, shape, dt))

        def bank(name):
            return ctx.enter_context(nc.psum_tensor(name, [128, 512], f32))

        def sem(name):
            return ctx.enter_context(nc.semaphore(name))

        z = sb("z", [128, NB, D])
        ident = sb("ident", [128, 128])
        shift = sb("shift", [128, 128])
        band = sb("band", [128, 128])
        rot = sb("rot", [128, 4, DH])
        qk_scale = sb("qk_scale", [128, 2, LAYERS, DH])
        tab = sb("tab", [128, 4, LAYERS, DH])
        eps = sb("eps", [128, 1])
        params = sb("params", [128, LAYERS, 8])
        param = sb("param", [128, 8])
        w_raw = sb("w_raw", [128, 3 * INNER])
        w_hi = sb("w_hi", [128, 3 * INNER], f32r)
        w_lo = sb("w_lo", [128, 3 * INNER], f32r)
        w1_raw = sb("w1_raw", [128, 2 * FI])
        w1_hi = sb("w1_hi", [128, 2 * FI], f32r)
        w1_lo = sb("w1_lo", [128, 2 * FI], f32r)
        wo = sb("wo", [128, INNER // 128, D])
        w2 = sb("w2", [128, 3, D])
        z_stage = sb("z_stage", [128, D])
        x_all = sb("x_all", [128, NT])
        x_hi = sb("x_hi", [128, NT], f32r)
        x_lo = sb("x_lo", [128, NT], f32r)
        square = sb("square", [128, 2, 512])
        by_cos = sb("by_cos", [128, 2, 512])
        by_sin = sb("by_sin", [128, 2, 512])
        sumsq = sb("sumsq", [128, 4, 8])
        log_sq = sb("log_sq", [128, 4, 8])
        inv_norm = sb("inv_norm", [128, 4, 8])
        qk = sb("qk", [128, 4, 512])
        q_T = [sb(f"q_T{i}", [128, 8, NT]) for i in range(2)]
        k_T = [sb(f"k_T{i}", [128, 8, NT]) for i in range(2)]
        v = [sb(f"v{i}", [128, H, DH + 1]) for i in range(2)]
        s_sb = sb("s_sb", [128, 2, GH, NT])
        row_max = sb("row_max", [128, 2, GH])
        p_sb = sb("p_sb", [128, 2, GH, NT])
        p_T = sb("p_T", [128, 2, GH, NT])
        inv_sum = sb("inv_sum", [128, GH])
        att = sb("att", [128, H, DH])
        att_T = sb("att_T", [128, INNER // 128, NT])
        xs = sb("xs", [128, D])
        x_res = sb("x_res", [128, NB, D])
        xw_raw = sb("xw_raw", [128, 4, D])
        xw_T = sb("xw_T", [128, 4, D])
        xb_col = sb("xb_col", [128, 2])
        xb_row = sb("xb_row", [128, 2, D])
        alpha = sb("alpha", [128, 2, XH])
        gates = sb("gates", [128, 4])
        tanh_g = sb("tanh_g", [128, 2])
        q_scale = sb("q_scale", [128, 2])
        frac_q = sb("frac_q", [128, NB])
        head_of = sb("head_of", [128, GH])
        x_mv = sb("x_mv", [128, NB, 2])
        x_st = sb("x_st", [128, NB, 6])
        x_log = sb("x_log", [128, NB])
        x_rstd = sb("x_rstd", [128, NB])
        x_in = sb("x_in", [128, 2, D])
        c_in = sb("c_in", [128, 2, D])
        xc_T = sb("xc_T", [128, 2, NT])
        xq = sb("xq", [128, 2, NT])
        xk = sb("xk", [128, NT])
        xv = sb("xv", [128, 2, XH, XD + 1])
        d_clip = sb("d_clip", [128, 2, NT])
        d_pos = sb("d_pos", [128, 2, NT])
        d_neg = sb("d_neg", [128, 2, NT])
        bias_neg = sb("bias_neg", [128, GH, NT])
        x_att = sb("x_att", [128, XH, XD])
        x_att_T = sb("x_att_T", [128, NT])
        stats = sb("stats", [128, 6])
        mean_var = sb("mean_var", [128, 2])
        log_var = sb("log_var", [128, 1])
        rstd = sb("rstd", [128, 1])
        xn = sb("xn", [128, NB, D])
        f_all = sb("f_all", [128, 2, 512])
        f_hi = sb("f_hi", [128, 2, 512], f32r)
        f_lo = sb("f_lo", [128, 2, 512], f32r)
        gelu = sb("gelu", [128, 2, 512])
        frac_k = xn
        bias_pos = f_all[:].rearrange("p i (h k) -> p i h k", k=NT)
        xk_bd = gelu[:].rearrange("p i (h k) -> p i h k", k=NT)
        h_T = [[sb(f"h_T{i}{c}", [128, 512]) for c in range(3)] for i in range(2)]

        proj_ps = [bank("proj_ps0"), bank("proj_ps1")]
        tr_ps = bank("tr_ps")
        pt_ps = bank("pt_ps")
        s_ps = ctx.enter_context(nc.psum_tensor("s_ps", [128, 2, 512], f32))
        pv_ps = bank("pv_ps")
        y_ps = bank("y_ps")

        const_ld = sem("const_ld")
        ld_w = sem("ld_w")
        ld_w1 = sem("ld_w1")
        ld_wo = sem("ld_wo")
        ld_w2 = sem("ld_w2")
        setup_done = sem("setup_done")
        tab_done = sem("tab_done")
        w_hi_done = sem("w_hi_done")
        w_split = sem("w_split")
        w1_hi_done = sem("w1_hi_done")
        w1_split = sem("w1_split")
        params_clear = sem("params_clear")
        param_ready = sem("param_ready")
        z_staged = sem("z_staged")
        x_split = sem("x_split")
        tr_full = sem("tr_full")
        tr_evac = sem("tr_evac")
        zt_full = sem("zt_full")
        zt_evac = sem("zt_evac")
        proj_full = sem("proj_full")
        squared = sem("squared")
        rotated = sem("rotated")
        summed = sem("summed")
        norm_ready = sem("norm_ready")
        inv_log = sem("inv_log")
        inv_ready = sem("inv_ready")
        qk_added = sem("qk_added")
        qk_ready = sem("qk_ready")
        v_ready = sem("v_ready")
        s_full = sem("s_full")
        masked = sem("masked")
        max_ready = sem("max_ready")
        centered = sem("centered")
        p_ready = sem("p_ready")
        pt_full = sem("pt_full")
        pt_evac = sem("pt_evac")
        pv_full = sem("pv_full")
        recip_done = sem("recip_done")
        att_ready = sem("att_ready")
        ot_full = sem("ot_full")
        ot_evac = sem("ot_evac")
        y_full = sem("y_full")
        z_attn = sem("z_attn")
        sh_full = sem("sh_full")
        xs_ready = sem("xs_ready")
        stat_done = sem("stat_done")
        var_ready = sem("var_ready")
        log_done = sem("log_done")
        rstd_ready = sem("rstd_ready")
        xn_ready = sem("xn_ready")
        ft_full = sem("ft_full")
        ft_evac = sem("ft_evac")
        f_split = sem("f_split")
        gate_full = sem("gate_full")
        a_full = sem("a_full")
        gelu_done = sem("gelu_done")
        h_ready = sem("h_ready")
        fy_full = sem("fy_full")
        z_ready = sem("z_ready")
        out_done = sem("out_done")
        result_ready = sem("result_ready")
        xw_ld = sem("xw_ld")
        bc_ld = sem("bc_ld")
        frac_ready = sem("frac_ready")
        x_ld = sem("x_ld")
        ctx_ld = [sem("ctx_ld_even"), sem("ctx_ld_odd")]
        xw_full = sem("xw_full")
        xw_evac = sem("xw_evac")
        xstat_done = sem("xstat_done")
        xvar_ready = sem("xvar_ready")
        xlog_done = sem("xlog_done")
        xrstd_ready = sem("xrstd_ready")
        xin_ready = sem("xin_ready")
        xt_full = sem("xt_full")
        xt_evac = sem("xt_evac")
        xproj_full = sem("xproj_full")
        xqk_out = sem("xqk_out")
        xk_ready = sem("xk_ready")
        xv_ready = sem("xv_ready")
        scalar_ready = sem("scalar_ready")
        tanh_done = sem("tanh_done")
        xscaled = sem("xscaled")
        xclip = sem("xclip")
        clip_ready = sem("clip_ready")
        bias_ready = sem("bias_ready")
        added_pos = sem("added_pos")
        neg_ready = sem("neg_ready")
        xo_full = sem("xo_full")
        xo_evac = sem("xo_evac")
        xy_full = sem("xy_full")
        xy_ready = sem("xy_ready")
        xg_ready = sem("xg_ready")
        block = ctx.enter_context(nc.Block())

        def heads(ap):
            return ap.rearrange("p (h x d) -> p h x d", x=2, d=HALF)

        def tile_of(ap, n, lo=0, hi=D):
            return ap[:, bass.ds(n, 1), lo:hi].rearrange("p a b -> p (a b)")

        def flat(ap):
            return ap.rearrange("p a b -> p (a b)")

        def layer_slots(eng_fori, L, front, slot, drain):
            T0 = L * NB
            front(T0)
            slot(T0, 0, 0, first=True, behind=0)
            slot(T0 + 1, 1, 1, behind=1)
            with eng_fori(0, (NB - 4) // 2) as pair:
                n = pair * 2 + 2
                slot(T0 + n, n, 0)
                slot(T0 + n + 1, n + 1, 1)
            slot(T0 + NB - 2, NB - 2, 0, last_front=True)
            slot(T0 + NB - 1, NB - 1, 1, front_on=False)
            drain(T0 + NB, NB, 0)

        @block.sync
        def _(sp):
            consts = [(ident[:], t["ident"]), (shift[:], t["shift"]), (band[:], t["band"]),
                      (flat(rot[:]), t["rot"])]
            for dst, src in consts:
                sp.dma_start(dst, src).then_inc(const_ld, 16)
            for i, name in enumerate(("L0_ffn_q_scale", "L0_ffn_k_scale")):
                src = t[name].rearrange("l d -> (l d)").unsqueeze(0).to_broadcast([128, LAYERS * DH])
                sp.dma_start(flat(qk_scale[:, i]), src).then_inc(const_ld, 16)

            def load_w(layer):
                sp.dma_start(w_raw[:], t["L0_ffn_Wqkv"][layer]).then_inc(ld_w, 16)

            def load_w1(layer):
                sp.dma_start(w1_raw[:], t["L0_ffn_W1"][layer]).then_inc(ld_w1, 16)

            def load_wo(layer):
                sp.dma_start(wo[:], t["L0_ffn_Wo"][layer].rearrange("(c p) d -> p c d", p=128)).then_inc(ld_wo, 16)

            def load_w2(layer):
                w2_d = t["L0_ffn_W2"][layer]
                sp.dma_start(w2[:, 0:2, :], w2_d[0:256, :].rearrange("(c p) d -> p c d", p=128)).then_inc(ld_w2, 16)
                sp.dma_start(w2[0:FC[2], 2, :], w2_d[256:FI, :]).then_inc(ld_w2, 16)
                sp.dma_start(w2[FC[2]:FC[2] + 1, 2, :], t["L0_ffn_b2"][layer].unsqueeze(0)).then_inc(ld_w2, 16)

            for i, n in enumerate(("Wq", "Wk", "Wv", "Wo")):
                sp.dma_start(xw_raw[:, i], t["L0_xattn_" + n]).then_inc(xw_ld, 16)
            sp.dma_start(x_res[:], t["x"].rearrange("b t d -> t b d")).then_inc(x_ld, 16)
            for i, n in enumerate(("bq", "bk")):
                sp.dma_start(xb_col[:, i:i + 1], t["L0_xattn_" + n].unsqueeze(1)).then_inc(bc_ld, 16)
            for i, n in enumerate(("bv", "bo")):
                sp.dma_start(xb_row[:, i], t["L0_xattn_" + n].unsqueeze(0).to_broadcast([128, D])).then_inc(bc_ld, 16)
            for i, n in enumerate(("alpha_pos", "alpha_neg")):
                sp.dma_start(alpha[:, i], t["L0_xattn_" + n].unsqueeze(0).to_broadcast([128, XH])).then_inc(bc_ld, 16)
            for i, n in enumerate(("L0_xattn_gamma", "L0_xattn_delta", "g_xattn", "g_ffn")):
                sp.dma_start(gates[:, i:i + 1], t[n].unsqueeze(0).to_broadcast([128, 1])).then_inc(bc_ld, 16)
            sp.dma_start(head_of[:], t["head_of"]).then_inc(bc_ld, 16)
            sp.dma_start(frac_q[:], t["fside_BxS2_0"].rearrange("b t -> t b")).then_inc(bc_ld, 16)
            sp.dma_start(flat(frac_k[:]), t["fside_BxS2_0"].rearrange("b t -> (b t)").unsqueeze(0).to_broadcast([128, NB * NT])).then_inc(bc_ld, 16)
            for T in range(2):
                sp.dma_start(c_in[:, T], t["ctx_1024"][T]).then_inc(ctx_ld[T], 16)

            load_w(0)
            load_w1(0)
            load_wo(0)
            load_w2(0)
            sp.wait_ge(params_clear, 1)
            sp.dma_start(params[:, :, 0], t["L0_ffn_ln_g"].rearrange("l d -> d l")).then_inc(const_ld, 16)
            sp.dma_start(params[:, :, 1], t["L0_ffn_ln_b"].rearrange("l d -> d l")).then_inc(const_ld, 16)
            for half in range(2):
                for c in range(3):
                    col = half * FI + 128 * c
                    sp.dma_start(params[0:FC[c], :, 2 + 3 * half + c],
                                 t["L0_ffn_b1"][:, col:col + FC[c]].rearrange("l d -> d l")).then_inc(const_ld, 16)
            ctx_d = t["ctx_1024"].rearrange("b t d -> t b d")
            with sp.Fori(1, NB // 2) as pair:
                for par in range(2):
                    sp.wait_ge(xt_full, pair * 2 + (par - 1))
                    sp.dma_start(c_in[:, par:par + 1, :], ctx_d[:, bass.ds(pair * 2 + par, 1), :]).then_inc(ctx_ld[par], 16)
            with sp.Fori(1, LAYERS + 1) as L:
                nxt = L % LAYERS
                sp.wait_ge(w_split, L * 3)
                sp.dma_start(w_raw[:].unsqueeze(1), t["L0_ffn_Wqkv"].rearrange("l p n -> p l n")[:, bass.ds(nxt, 1), :]).then_inc(ld_w, 16)
                sp.wait_ge(w1_split, L)
                sp.dma_start(w1_raw[:].unsqueeze(1), t["L0_ffn_W1"].rearrange("l p n -> p l n")[:, bass.ds(nxt, 1), :]).then_inc(ld_w1, 16)
                sp.wait_ge(y_full, L * NB + NB)
                sp.dma_start(wo[:], t["L0_ffn_Wo"].rearrange("l (c p) d -> p (l c) d", p=128)[:, bass.ds(nxt * 8, 8), :]).then_inc(ld_wo, 16)
                sp.wait_ge(fy_full, L * NF + NF)
                w2_d = t["L0_ffn_W2"]
                for c in range(3):
                    sp.dma_start(w2[0:FC[c], c:c + 1, :], w2_d[:, 128 * c:128 * c + FC[c], :].rearrange("l p d -> p l d")[:, bass.ds(nxt, 1), :]).then_inc(ld_w2, 16)
                sp.dma_start(w2[FC[2]:FC[2] + 1, 2:3, :], t["L0_ffn_b2"].unsqueeze(0)[:, bass.ds(nxt, 1), :]).then_inc(ld_w2, 16)
            sp.wait_ge(result_ready, 1)
            sp.dma_start(t["out"].rearrange("b t d -> t b d"), z[:]).then_inc(out_done, 16)
            sp.wait_ge(out_done, 16)
            sp.wait_ge(ld_w, 16 * (LAYERS + 1))
            sp.wait_ge(ld_w1, 16 * (LAYERS + 1))
            sp.wait_ge(ld_wo, 16 * (LAYERS + 1))
            sp.wait_ge(ld_w2, 48 + 64 * LAYERS)

        N_CONST = 16 * (6 + 2 + 6)
        N_BC = 16 * 13

        @block.tensor
        def _(pe):
            pe.sem_inc(tr_full, 4 * NB)
            pe.sem_inc(zt_full, NB)
            pe.sem_inc(proj_full, 6 * NB)
            pe.sem_inc(ot_full, 2 * NB)
            pe.sem_inc(y_full, NB)
            pe.sem_inc(sh_full, NB)
            pe.sem_inc(ft_full, NF)
            pe.sem_inc(gate_full, 3 * NF)
            pe.sem_inc(a_full, 3 * NF)
            pe.sem_inc(fy_full, NF)
            pe.wait_ge(const_ld, N_CONST)
            pe.wait_ge(setup_done, 2)

            def x_transpose(T, behind=2):
                pe.wait_ge(z_staged, T + 1)
                pe.wait_ge(tr_evac, T * 4 - behind)
                pe.transpose(tr_ps[:, 0:128], z_stage[:], ident[:]).then_inc(zt_full, 1)

            def project(T, m, boundary=None):
                if m == 0:
                    pe.wait_ge(x_split, T + 1)
                    if boundary is None:
                        pe.wait_ge(v_ready, T * 2)
                    else:
                        pe.wait_ge(gelu_done, boundary * 12)
                        pe.wait_ge(h_ready, boundary * 12)
                        pe.wait_ge(w_split, boundary * 3)
                elif m == 1:
                    pe.wait_ge(rotated, T * 4)
                elif m == 4:
                    pe.wait_ge(v_ready, T * 2 + 1)
                else:
                    pe.wait_ge(rotated, T * 4 + (1, 2, None, 3)[m - 2])
                col = slice(CHUNK_COL[m], CHUNK_COL[m] + 512)
                ps = proj_ps[m % 2]
                pe.matmul(ps[:], x_hi[:], w_hi[:, col], start=True, stop=False)
                pe.matmul(ps[:], x_hi[:], w_lo[:, col], start=False, stop=False)
                pe.matmul(ps[:], x_lo[:], w_hi[:, col], start=False, stop=True).then_inc(proj_full, 1)

            def qk_transpose(T, c, after_x=False):
                pe.wait_ge(qk_ready, T * 4 + (c + 1))
                pe.wait_ge(tr_evac, T * 4 + c)
                if after_x:
                    pe.wait_ge(zt_evac, T + 2)
                for j in range(4):
                    mm = pe.transpose(tr_ps[:, 128 * j:128 * j + 128], qk[:, c, 128 * j:128 * j + 128], ident[:])
                mm.then_inc(tr_full, 1)

            def scores(T, par, g):
                pe.wait_ge(tr_evac, T * 4 + (2 * (g // 2) + 2))
                pe.wait_ge(masked, T * 4 + g)
                for j in range(GH):
                    pair, row = 2 * g + j // 2, 64 * (j % 2)
                    mm = pe.matmul(s_ps[:, j % 2, NT * (j // 2):NT * (j // 2 + 1)], q_T[par][row:row + 64, pair, :],
                                   k_T[par][row:row + 64, pair, :], start=True, stop=True)
                mm.then_inc(s_full, 1)

            def p_transpose(T, g, first=False):
                pe.wait_ge(p_ready, T * 4 + (g + 1))
                if not first:
                    pe.wait_ge(pt_evac, T * 4 + g)
                for j in range(GH):
                    mm = pe.transpose(pt_ps[:, 128 * j:128 * j + 128], p_sb[:, g % 2, j, :], ident[:])
                mm.then_inc(pt_full, 1)

            def values(T, par, g):
                pe.wait_ge(pt_evac, T * 4 + (g + 1))
                pe.wait_ge(v_ready, T * 2 + 2)
                pe.wait_ge(att_ready, T * 4 + g)
                for j in range(GH):
                    mm = pe.matmul(pv_ps[:, (DH + 1) * j:(DH + 1) * (j + 1)], p_T[:, g % 2, j, :],
                                   v[par][:, GH * g + j, :], start=True, stop=True)
                mm.then_inc(pv_full, 1)

            def att_transpose(T, i):
                pe.wait_ge(att_ready, T * 4 + (2 * i + 2))
                pe.wait_ge(ot_evac, T * 2 + i)
                if i == 0:
                    pe.wait_ge(xs_ready, T * 2)
                for j in range(4):
                    mm = pe.transpose(y_ps[:, 128 * j:128 * j + 128],
                                      att[:, 8 * i + 2 * j:8 * i + 2 * j + 2, :].rearrange("p a b -> p (a b)"), ident[:])
                mm.then_inc(ot_full, 1)

            def out_project(T, L):
                pe.wait_ge(ld_wo, L * 16)
                pe.wait_ge(ot_evac, T * 2 + 2)
                for c in range(8):
                    mm = pe.matmul(y_ps[:, 0:D], att_T[:, c, :], wo[:, c, :], start=(c == 0), stop=(c == 7))
                mm.then_inc(y_full, 1)

            def shift_state(T, src):
                pe.wait_ge(z_attn, T + 1)
                pe.matmul(y_ps[:, 0:D // 2], shift[:], src, start=True, stop=True).then_inc(sh_full, 1)

            def x_setup():
                pe.wait_ge(xw_ld, 64)
                for i in range(4):
                    mm = pe.transpose(pt_ps[:, 128 * i:128 * i + 128], xw_raw[:, i], ident[:])
                mm.then_inc(xw_full, 1)

            def x_inputs(T, par):
                pe.wait_ge(ctx_ld[par], (T - par) * 8 + 16)
                pe.wait_ge(xin_ready, T + 1)
                pe.transpose(tr_ps[:, 0:128], x_in[:, par], ident[:])
                pe.transpose(tr_ps[:, 128:256], c_in[:, par], ident[:]).then_inc(xt_full, 1)

            def x_project(T):
                pe.wait_ge(xt_evac, T + 1)
                if not isinstance(T, int) or T > 0:
                    pe.wait_ge(xv_ready, T)
                else:
                    pe.wait_ge(xw_evac, 1)
                pe.matmul(proj_ps[0][:, 0:128], xw_T[:, 0], xc_T[:, 0], start=True, stop=True)
                pe.matmul(proj_ps[0][:, 128:256], xw_T[:, 1], xc_T[:, 1], start=True, stop=True)
                pe.matmul(proj_ps[0][:, 256:384], xc_T[:, 1], xw_T[:, 2], start=True, stop=True).then_inc(xproj_full, 1)

            def x_scores(T, par, g, first=False):
                if g == 0:
                    pe.wait_ge(xk_ready, T + 1)
                if not (first and g == 0):
                    pe.wait_ge(masked, T * 4 + g)
                rows = slice(32 * g, 32 * g + 32)
                pe.matmul(s_ps[:, 0, :], xq[rows, par, :], flat(xk_bd[rows, par]), start=True, stop=True).then_inc(s_full, 1)

            def x_values(T, par, g, first=False):
                pe.wait_ge(pt_evac, T * 4 + (g + 1))
                pe.wait_ge(xv_ready, T + 1)
                if not (first and g == 0):
                    pe.wait_ge(att_ready, T * 4 + g)
                for j in range(GH):
                    mm = pe.matmul(pv_ps[:, (XD + 1) * j:(XD + 1) * (j + 1)], p_T[:, g % 2, j, :],
                                   xv[:, par, GH * g + j, :], start=True, stop=True)
                mm.then_inc(pv_full, 1)

            def x_out(T):
                pe.wait_ge(att_ready, T * 4 + 4)
                pe.transpose(y_ps[:, 0:128], x_att[:].rearrange("p h d -> p (h d)"), ident[:]).then_inc(xo_full, 1)

            def x_out_project(T):
                pe.wait_ge(xo_evac, T + 1)
                pe.matmul(y_ps[:, 0:128], x_att_T[:], xw_T[:, 3], start=True, stop=True).then_inc(xy_full, 1)

            def x_slot(T, par, first=False, front_on=True):
                x_scores(T, par, 0, first)
                if not first:
                    p_transpose(T - 1, 3)
                    x_values(T - 1, 1 - par, 2)
                x_scores(T, par, 1)
                p_transpose(T, 0, first)
                if not first:
                    x_values(T - 1, 1 - par, 3)
                x_scores(T, par, 2)
                p_transpose(T, 1)
                if front_on:
                    x_inputs(T + 1, 1 - par)
                if not first:
                    x_out(T - 1)
                x_values(T, par, 0, first)
                x_scores(T, par, 3)
                p_transpose(T, 2)
                if front_on:
                    x_project(T + 1)
                if not first:
                    x_out_project(T - 1)
                x_values(T, par, 1)

            x_setup()
            x_inputs(0, 0)
            x_project(0)
            x_slot(0, 0, first=True)
            with pe.Fori(0, NB // 2 - 1) as pair:
                x_slot(pair * 2 + 1, 1)
                x_slot(pair * 2 + 2, 0)
            x_slot(NB - 1, 1, front_on=False)
            p_transpose(NB - 1, 3)
            x_values(NB - 1, 1, 2)
            x_values(NB - 1, 1, 3)
            x_out(NB - 1)
            x_out_project(NB - 1)

            with pe.Fori(1, LAYERS + 1) as L:
                def front(T):
                    x_transpose(T, behind=0)
                    for m in range(5):
                        project(T, m, boundary=L)
                    qk_transpose(T, 0)
                    project(T, 5)
                    qk_transpose(T, 1)
                    x_transpose(T + 1)
                    qk_transpose(T, 2, after_x=True)

                def slot(T, n, par, first=False, behind=2, front_on=True, last_front=False):
                    scores(T, par, 0)
                    if front_on:
                        project(T + 1, 0)
                    if behind >= 1:
                        p_transpose(T - 1, 3)
                        values(T - 1, 1 - par, 2)
                    if behind >= 2:
                        shift_state(T - 2, tile_of(z, n - 2, D // 2))
                    qk_transpose(T, 3)
                    scores(T, par, 1)
                    if front_on:
                        project(T + 1, 1)
                    p_transpose(T, 0)
                    if behind >= 1:
                        values(T - 1, 1 - par, 3)
                        att_transpose(T - 1, 0)
                    if front_on:
                        project(T + 1, 2)
                        qk_transpose(T + 1, 0)
                    scores(T, par, 2)
                    if front_on:
                        project(T + 1, 3)
                    p_transpose(T, 1)
                    values(T, par, 0)
                    if behind >= 1:
                        att_transpose(T - 1, 1)
                    if front_on:
                        project(T + 1, 4)
                        qk_transpose(T + 1, 1)
                    scores(T, par, 3)
                    if front_on:
                        project(T + 1, 5)
                        if not last_front:
                            x_transpose(T + 2)
                    p_transpose(T, 2)
                    values(T, par, 1)
                    if behind >= 1:
                        out_project(T - 1, L)
                    if front_on:
                        qk_transpose(T + 1, 2, after_x=not last_front)

                def drain(T, n, par):
                    p_transpose(T - 1, 3)
                    values(T - 1, 1 - par, 2)
                    shift_state(T - 2, tile_of(z, n - 2, D // 2))
                    values(T - 1, 1 - par, 3)
                    att_transpose(T - 1, 0)
                    att_transpose(T - 1, 1)
                    out_project(T - 1, L)
                    shift_state(T - 1, tile_of(z, n - 1, D // 2))

                layer_slots(pe.Fori, L, front, slot, drain)

                def f_transpose(j):
                    F = L * NF + j
                    pe.wait_ge(xn_ready, L * NB + (FG * j + FG))
                    pe.wait_ge(ft_evac, F)
                    for i in range(FG):
                        mm = pe.transpose(pt_ps[:, 128 * i:128 * i + 128], xn[:, FG * j + i, :], ident[:])
                    mm.then_inc(ft_full, 1)

                def f_up(j, c):
                    F = L * NF + j
                    if c == 0:
                        pe.wait_ge(f_split, F + 1)
                    pe.wait_ge(w1_split, L)
                    for half, ps, full, free in ((1, proj_ps[0], gate_full, gelu_done), (0, proj_ps[1], a_full, h_ready)):
                        col = slice(half * FI + 128 * c, half * FI + 128 * c + FC[c])
                        pe.wait_ge(free, F * 3 + c)
                        o = ps[0:FC[c], :]
                        pe.matmul(o, w1_hi[:, col], f_hi[:, j % 2, :], start=True, stop=False)
                        pe.matmul(o, w1_hi[:, col], f_lo[:, j % 2, :], start=False, stop=False)
                        pe.matmul(o, w1_lo[:, col], f_hi[:, j % 2, :], start=False, stop=True).then_inc(full, 1)

                def f_down(j):
                    F = L * NF + j
                    pe.wait_ge(ld_w2, L * 64 - 16)
                    pe.wait_ge(h_ready, F * 3 + 3)
                    pe.wait_ge(z_ready, F + 12)
                    for i in range(FG):
                        for c in range(3):
                            k = FC[c] + (c == 2)
                            mm = pe.matmul(s_ps[:, 0, 128 * i:128 * i + 128], h_T[j % 2][c][0:k, 128 * i:128 * i + 128],
                                           w2[0:k, c, :], start=(c == 0), stop=(c == 2))
                    mm.then_inc(fy_full, 1)

                f_transpose(0)
                for j in range(NF):
                    if j + 1 < NF:
                        f_transpose(j + 1)
                    f_up(j, 0)
                    if j >= 1:
                        f_down(j - 1)
                    f_up(j, 1)
                    f_up(j, 2)
                f_down(NF - 1)

        @block.scalar
        def _(act):
            act.sem_inc(tr_evac, 4 * NB)
            act.sem_inc(zt_evac, NB)
            act.sem_inc(squared, 4 * NB)
            act.sem_inc(inv_log, 4 * NB)
            act.sem_inc(inv_ready, 4 * NB)
            act.sem_inc(v_ready, 2 * NB)
            act.sem_inc(ot_evac, 2 * NB)
            act.sem_inc(log_done, NB)
            act.sem_inc(rstd_ready, NB)
            act.sem_inc(ft_evac, NF)
            act.sem_inc(gelu_done, 3 * NF)
            act.preload_act_table_set("natural_log_exp_and_others")
            act.wait_ge(setup_done, 2)
            act.wait_ge(const_ld, N_CONST)

            def x_out(T):
                act.wait_ge(zt_full, T + 1)
                half = D // 2
                for dst in (x_all, x_hi):
                    act.activation(dst[0:half, :], tr_ps[0:half, 0:NT], ACT.Copy)
                    last = act.activation(dst[half:D, 1:NT], tr_ps[half:D, 0:NT - 1], ACT.Copy)
                last.then_inc(zt_evac, 1)

            def square_chunk(T, c):
                act.wait_ge(proj_full, T * 6 + (QK_AT[c] + 1))
                act.wait_ge(summed, T * 4 + (c - 1))
                act.activation(square[:, c % 2, :], proj_ps[QK_AT[c] % 2][:], ACT.Square).then_inc(squared, 1)

            def norms(T, c):
                act.wait_ge(norm_ready, T * 4 + (c + 1))
                act.activation(log_sq[:, c, :], sumsq[:, c, :], ACT.Ln).then_inc(inv_log, 1)
                act.wait_ge(inv_log, T * 4 + (c + 1))
                act.activation(inv_norm[:, c, :], log_sq[:, c, :], ACT.Exp, scale=-0.5).then_inc(inv_ready, 1)

            def qk_out(T, par, c):
                act.wait_ge(tr_full, T * 4 + (c + 1))
                dst = (q_T, k_T)[c % 2][par]
                i = c // 2
                act.activation(flat(dst[:, 4 * i:4 * i + 4, :]), tr_ps[:], ACT.Copy).then_inc(tr_evac, 1)

            def v_out(T, par, i):
                act.wait_ge(proj_full, T * 6 + (V_AT[i] + 1))
                act.activation(v[par][:, 8 * i:8 * i + 8, 0:DH], proj_ps[V_AT[i] % 2][:].rearrange("p (h d) -> p h d", d=DH),
                               ACT.Copy).then_inc(v_ready, 1)

            def exps(T, g, first=False):
                act.wait_ge(centered, T * 4 + (g + 1))
                if not first:
                    act.wait_ge(pt_full, T * 4 + (g - 1))
                act.activation(flat(p_sb[:, g % 2]), flat(s_sb[:, g % 2]), ACT.Exp).then_inc(p_ready, 1)

            def p_out(T, g):
                act.wait_ge(pt_full, T * 4 + (g + 1))
                act.activation(flat(p_T[:, g % 2]), pt_ps[:], ACT.Copy).then_inc(pt_evac, 1)

            def att_out(T, i):
                act.wait_ge(ot_full, T * 2 + (i + 1))
                act.activation(flat(att_T[:, 4 * i:4 * i + 4, :]), y_ps[:], ACT.Copy).then_inc(ot_evac, 1)

            def ln_std(T):
                act.wait_ge(var_ready, T + 1)
                act.activation(log_var[:], mean_var[:, 1:2], ACT.Ln, bias=eps[:]).then_inc(log_done, 1)
                act.wait_ge(log_done, T + 1)
                act.activation(rstd[:], log_var[:], ACT.Exp, scale=-0.5).then_inc(rstd_ready, 1)

            act.wait_ge(bc_ld, N_BC)
            act.activation(tanh_g[:], gates[:, 2:4], ACT.Tanh).then_inc(tanh_done, 1)
            act.preload_act_table_set("natural_log_exp_and_others")
            act.wait_ge(xw_full, 1)
            act.activation(flat(xw_T[:]), pt_ps[:], ACT.Copy).then_inc(xw_evac, 1)
            act.wait_ge(xvar_ready, 1)
            act.activation(x_log[:], x_mv[:, :, 1], ACT.Ln, bias=eps[:]).then_inc(xlog_done, 1)
            act.wait_ge(xlog_done, 1)
            act.activation(x_rstd[:], x_log[:], ACT.Exp, scale=-0.5).then_inc(xrstd_ready, 1)
            act.wait_ge(scalar_ready, 1)

            def x_inputs_out(T):
                act.wait_ge(xt_full, T + 1)
                act.activation(flat(xc_T[:]), tr_ps[:, 0:256], ACT.Copy).then_inc(xt_evac, 1)

            def x_qk_out(T, par):
                act.wait_ge(xproj_full, T + 1)
                if not isinstance(T, int):
                    act.wait_ge(xk_ready, T)
                act.activation(xq[:, par], proj_ps[0][:, 0:128], ACT.Identity, bias=q_scale[:, 1:2], scale=q_scale[:, 0:1])
                act.activation(xk[:], proj_ps[0][:, 128:256], ACT.Identity, bias=xb_col[:, 1:2]).then_inc(xqk_out, 1)

            def x_att_out(T):
                act.wait_ge(xo_full, T + 1)
                act.activation(x_att_T[:], y_ps[:, 0:128], ACT.Copy).then_inc(xo_evac, 1)

            def x_slot(T, par, first=False, front_on=True):
                if not first:
                    p_out(T - 1, 3)
                exps(T, 0, first)
                p_out(T, 0)
                exps(T, 1, first)
                p_out(T, 1)
                if front_on:
                    x_inputs_out(T + 1)
                if not first:
                    x_att_out(T - 1)
                exps(T, 2)
                p_out(T, 2)
                if front_on:
                    x_qk_out(T + 1, 1 - par)
                exps(T, 3)

            x_inputs_out(0)
            x_qk_out(0, 0)
            x_slot(0, 0, first=True)
            with act.Fori(0, NB // 2 - 1) as pair:
                x_slot(pair * 2 + 1, 1)
                x_slot(pair * 2 + 2, 0)
            x_slot(NB - 1, 1, front_on=False)
            p_out(NB - 1, 3)
            x_att_out(NB - 1)
            act.wait_ge(xvar_ready, 2)
            act.activation(x_log[:], x_mv[:, :, 1], ACT.Ln, bias=eps[:]).then_inc(xlog_done, 1)
            act.wait_ge(xlog_done, 2)
            act.activation(x_rstd[:], x_log[:], ACT.Exp, scale=-0.5).then_inc(xrstd_ready, 1)

            with act.Fori(1, LAYERS + 1) as L:
                act.preload_act_table_set("natural_log_exp_and_others")

                def front(T):
                    x_out(T)
                    square_chunk(T, 0)
                    square_chunk(T, 1)
                    norms(T, 0)
                    v_out(T, 0, 0)
                    square_chunk(T, 2)
                    norms(T, 1)
                    v_out(T, 0, 1)
                    qk_out(T, 0, 0)
                    square_chunk(T, 3)
                    norms(T, 2)
                    qk_out(T, 0, 1)
                    x_out(T + 1)
                    qk_out(T, 0, 2)

                def slot(T, n, par, first=False, behind=2, front_on=True, last_front=False):
                    norms(T, 3)
                    if front_on:
                        square_chunk(T + 1, 0)
                    if behind >= 1:
                        p_out(T - 1, 3)
                    qk_out(T, par, 3)
                    exps(T, 0)
                    if front_on:
                        norms(T + 1, 0)
                        square_chunk(T + 1, 1)
                    p_out(T, 0)
                    if front_on:
                        qk_out(T + 1, 1 - par, 0)
                    exps(T, 1)
                    if behind >= 1:
                        att_out(T - 1, 0)
                    if front_on:
                        norms(T + 1, 1)
                        v_out(T + 1, 1 - par, 0)
                        square_chunk(T + 1, 2)
                    p_out(T, 1)
                    if behind >= 2:
                        ln_std(T - 2)
                    if front_on:
                        qk_out(T + 1, 1 - par, 1)
                    exps(T, 2)
                    if behind >= 1:
                        att_out(T - 1, 1)
                    if front_on:
                        norms(T + 1, 2)
                        v_out(T + 1, 1 - par, 1)
                        square_chunk(T + 1, 3)
                        if not last_front:
                            x_out(T + 2)
                    p_out(T, 2)
                    if front_on:
                        qk_out(T + 1, 1 - par, 2)
                    exps(T, 3)

                def drain(T, n, par):
                    p_out(T - 1, 3)
                    ln_std(T - 2)
                    att_out(T - 1, 0)
                    att_out(T - 1, 1)
                    ln_std(T - 1)

                layer_slots(act.Fori, L, front, slot, drain)

                act.preload_act_table_set("gelu_and_others")

                def f_out(j):
                    F = L * NF + j
                    act.wait_ge(ft_full, F + 1)
                    for dst in (f_all, f_hi):
                        last = act.activation(dst[:, j % 2, :], pt_ps[:], ACT.Identity,
                                              bias=param[:, 1:2], scale=param[:, 0:1])
                    last.then_inc(ft_evac, 1)

                def f_gelu(j, c):
                    F = L * NF + j
                    act.wait_ge(gate_full, F * 3 + (c + 1))
                    if j or c == 2:
                        act.wait_ge(h_ready, F * 3 + (c - 1))
                    m = FC[c]
                    act.activation(gelu[0:m, (3 * j + c) % 2, :], proj_ps[0][0:m, :], ACT.Gelu,
                                   bias=param[0:m, 5 + c:6 + c]).then_inc(gelu_done, 1)

                act.wait_ge(param_ready, L)
                f_out(0)
                for j in range(NF):
                    if j + 1 < NF:
                        f_out(j + 1)
                    for c in range(3):
                        f_gelu(j, c)

        @block.vector
        def _(dve):
            dve.sem_inc(rotated, 4 * NB)
            dve.sem_inc(summed, 4 * NB)
            dve.sem_inc(norm_ready, 4 * NB)
            dve.sem_inc(z_attn, NB)
            dve.sem_inc(xs_ready, 2 * NB)
            dve.sem_inc(stat_done, NB)
            dve.sem_inc(var_ready, NB)
            dve.sem_inc(xn_ready, NB)
            dve.sem_inc(h_ready, 3 * NF)
            dve.sem_inc(z_staged, NB)
            dve.memset(eps[:], LN_EPS)
            for i in range(2):
                dve.memset(v[i][:, :, DH], 1.0)
                dve.memset(h_T[i][2][:], 1.0)
            dve.memset(x_all[:], 0.0)
            dve.memset(x_hi[:].bitcast(f32), 0.0).then_inc(setup_done, 1)
            dve.wait_ge(const_ld, N_CONST)
            for i in range(4):
                last = dve.tensor_tensor(tab[:, i], qk_scale[:, i // 2],
                                         rot[:, i, :].unsqueeze(1).to_broadcast([128, LAYERS, DH]), ALU.mult)
            last.then_inc(setup_done, 1)
            dve.wait_ge(setup_done, 2)

            def w_round(k, L1):
                col = slice(INNER * k, INNER * (k + 1))
                dve.tensor_copy(w_hi[:, col], w_raw[:, col]).then_inc(w_hi_done, 1)

            dve.wait_ge(ld_w, 16)
            for k in range(3):
                w_round(k, 0)

            def by_table(T, c, L, i, dst):
                ps = proj_ps[QK_AT[c] % 2][:].rearrange("p (h d) -> p h d", d=DH)
                tb = tab[:, 2 * (c % 2) + i, bass.ds(L - 1, 1), :].to_broadcast([128, 8, DH])
                return dve.tensor_tensor(dst[:, c % 2, :].rearrange("p (h d) -> p h d", d=DH), ps, tb, ALU.mult)

            def times_cos(T, c, L):
                dve.wait_ge(squared, T * 4 + (c + 1))
                dve.wait_ge(qk_added, T * 4 + (c - 1))
                by_table(T, c, L, 0, by_cos)

            def times_sin(T, c, L):
                by_table(T, c, L, 1, by_sin).then_inc(rotated, 1)

            def sum_squares(T, c):
                dve.tensor_reduce(sumsq[:, c, :], square[:, c % 2, :].rearrange("p (h d) -> p h d", d=DH),
                                  AX, ALU.add).then_inc(summed, 1)

            def clamp_norm(T, c):
                dve.wait_ge(summed, T * 4 + (c + 1))
                dve.tensor_scalar(sumsq[:, c, :], sumsq[:, c, :], 1e-24, None, ALU.max).then_inc(norm_ready, 1)

            def mask(T, g):
                dve.wait_ge(s_full, T * 4 + (g + 1))
                dve.wait_ge(p_ready, T * 4 + (g - 1))
                dve.tensor_tensor(s_sb[:, g % 2].rearrange("p (a b) k -> p b a k", b=2),
                                  s_ps[:, :, 0:GH // 2 * NT].rearrange("p b (a k) -> p b a k", k=NT),
                                  band[:].unsqueeze(1).unsqueeze(1).to_broadcast([128, 2, GH // 2, NT]),
                                  ALU.add).then_inc(masked, 1)

            def row_maxima(T, g):
                dve.wait_ge(masked, T * 4 + (g + 1))
                dve.tensor_reduce(row_max[:, g % 2, :], s_sb[:, g % 2], AX, ALU.max).then_inc(max_ready, 1)

            def sums_inverse(T, g):
                dve.wait_ge(pv_full, T * 4 + (g + 1))
                o = pv_ps[:, 0:GH * (DH + 1)].rearrange("p (h d) -> p h d", d=DH + 1)
                dve.reciprocal(inv_sum[:], o[:, :, DH]).then_inc(recip_done, 1)

            def normalise(T, g):
                dve.wait_ge(recip_done, T * 4 + (g + 1))
                o = pv_ps[:, 0:GH * (DH + 1)].rearrange("p (h d) -> p h d", d=DH + 1)
                dve.tensor_tensor(att[:, GH * g:GH * g + GH, :], o[:, :, 0:DH],
                                  inv_sum[:].unsqueeze(2).to_broadcast([128, GH, DH]), ALU.mult).then_inc(att_ready, 1)

            dve.wait_ge(x_ld, 16)

            def x_moments(src, time):
                for b in range(NB):
                    last = dve.bn_stats(x_st[:, b], src[:, b])
                last.then_inc(xstat_done, 1)
                dve.wait_ge(xstat_done, time)
                for b in range(NB):
                    last = dve.bn_aggr(x_mv[:, b], x_st[:, b])
                last.then_inc(xvar_ready, 1)

            x_moments(x_res, 1)
            dve.memset(xv[:, :, :, XD], 1.0).then_inc(xscaled, 1)
            dve.wait_ge(bc_ld, N_BC)
            dve.tensor_scalar(q_scale[:, 0:1], gates[:, 0:1], float(XD) ** -0.5, None, ALU.mult).then_inc(xscaled, 1)
            dve.tensor_scalar(alpha[:, :, :], alpha[:, :, :], gates[:, 1:2], None, ALU.mult).then_inc(xscaled, 1)
            dve.wait_ge(xscaled, 3)
            dve.tensor_tensor(q_scale[:, 1:2], xb_col[:, 0:1], q_scale[:, 0:1], ALU.mult).then_inc(scalar_ready, 1)
            dve.wait_ge(tanh_done, 1)
            dve.tensor_scalar(xb_row[:, 1], xb_row[:, 1], tanh_g[:, 0:1], None, ALU.mult).then_inc(xscaled, 1)
            dve.wait_ge(xrstd_ready, 1)

            def x_normalise(T, par):
                if not isinstance(T, int):
                    dve.wait_ge(xt_full, T - 1)
                b = T if isinstance(T, int) else None
                src = x_res[:, T] if isinstance(T, int) else tile_of(x_res, T)
                mu = x_mv[:, T, 0:1] if b is not None else x_mv[:, bass.ds(T, 1), 0]
                rs = x_rstd[:, T:T + 1] if b is not None else x_rstd[:, bass.ds(T, 1)]
                dve.tensor_scalar(x_in[:, par], src, mu, rs, ALU.subtract, ALU.mult).then_inc(xin_ready, 1)

            def x_value_out(T, par):
                dve.wait_ge(xqk_out, T + 1)
                dve.tensor_tensor(xv[:, par, :, 0:XD], proj_ps[0][:, 256:384].rearrange("p (h d) -> p h d", d=XD),
                                  xb_row[:, 0].rearrange("p (h d) -> p h d", d=XD), ALU.add).then_inc(xv_ready, 1)

            def x_clip(T, par, n3):
                if not isinstance(T, int):
                    dve.wait_ge(bias_ready, T * 4 - 4)
                src = frac_k[:, T] if isinstance(T, int) else tile_of(frac_k, T)
                fq = frac_q[:, T:T + 1] if isinstance(T, int) else frac_q[:, bass.ds(T, 1)]
                dve.tensor_scalar(d_clip[:, par], src, fq, -CLAMP, ALU.subtract, ALU.max).then_inc(xclip, 1)
                dve.wait_ge(xclip, T + 1)
                dve.tensor_scalar(d_neg[:, par], d_clip[:, par], 0.0, None, ALU.min)
                dve.tensor_scalar(d_pos[:, par], d_clip[:, par], CLAMP, 0.0, ALU.min, ALU.max).then_inc(clip_ready, 1)

            def x_bias(T, par, g, first=False):
                G = T * 4 + g
                if not (first and g == 0):
                    dve.wait_ge(added_pos, G)
                dve.wait_ge(clip_ready, T + 1)
                dve.tensor_tensor(bias_neg[:], d_neg[:, par].unsqueeze(1).to_broadcast([128, GH, NT]),
                                  alpha[:, 1, GH * g:GH * g + GH].unsqueeze(2).to_broadcast([128, GH, NT]),
                                  ALU.mult).then_inc(neg_ready, 1)
                dve.wait_ge(s_full, G + 1)
                dve.wait_ge(bias_ready, G + 1)
                if not first:
                    dve.wait_ge(p_ready, G - 1)
                dve.tensor_tensor(s_sb[:, g % 2], s_ps[:, 0, :].rearrange("p (h k) -> p h k", k=NT),
                                  bias_pos[:, g % 2], ALU.add).then_inc(masked, 1)
                dve.wait_ge(masked, G + 1)
                dve.wait_ge(neg_ready, G + 1)
                dve.tensor_tensor(s_sb[:, g % 2], s_sb[:, g % 2], bias_neg[:], ALU.add).then_inc(added_pos, 1)
                dve.wait_ge(added_pos, G + 1)
                dve.tensor_reduce(row_max[:, g % 2, :], s_sb[:, g % 2], AX, ALU.max).then_inc(max_ready, 1)

            def x_attention(T, g):
                dve.wait_ge(pv_full, T * 4 + (g + 1))
                o = pv_ps[:, 0:GH * (XD + 1)].rearrange("p (h d) -> p h d", d=XD + 1)
                dve.reciprocal(inv_sum[:], o[:, :, XD]).then_inc(recip_done, 1)
                dve.wait_ge(recip_done, T * 4 + (g + 1))
                dve.tensor_tensor(x_att[:, GH * g:GH * g + GH, :], o[:, :, 0:XD],
                                  inv_sum[:].unsqueeze(2).to_broadcast([128, GH, XD]), ALU.mult).then_inc(att_ready, 1)

            def x_add(T):
                dve.wait_ge(xy_full, T + 1)
                xt = x_res[:, T] if isinstance(T, int) else tile_of(x_res, T)
                dve.scalar_tensor_tensor(xt, y_ps[:, 0:D], tanh_g[:, 0:1], xt, ALU.mult, ALU.add).then_inc(xy_ready, 1)

            def x_gate_bias(T):
                xt = x_res[:, T] if isinstance(T, int) else tile_of(x_res, T)
                dve.tensor_tensor(xt, xt, xb_row[:, 1], ALU.add).then_inc(xg_ready, 1)

            def x_slot(T, par, first=False, front_on=True):
                x_bias(T, par, 0, first)
                if not first:
                    x_attention(T - 1, 2)
                x_bias(T, par, 1, first)
                if front_on:
                    x_normalise(T + 1, 1 - par)
                if not first:
                    x_attention(T - 1, 3)
                x_bias(T, par, 2)
                if front_on:
                    x_gate_bias(T)
                    x_clip(T + 1, 1 - par, None)
                x_attention(T, 0)
                x_bias(T, par, 3)
                if front_on:
                    x_value_out(T + 1, 1 - par)
                if not first:
                    dve.wait_ge(xg_ready, T)
                    x_add(T - 1)
                x_attention(T, 1)

            dve.wait_ge(xscaled, 4)
            x_normalise(0, 0)
            x_clip(0, 0, None)
            x_value_out(0, 0)
            x_slot(0, 0, first=True)
            with dve.Fori(0, NB // 2 - 1) as pair:
                x_slot(pair * 2 + 1, 1)
                x_slot(pair * 2 + 2, 0)
            x_slot(NB - 1, 1, front_on=False)
            x_attention(NB - 1, 2)
            x_attention(NB - 1, 3)
            x_gate_bias(NB - 1)
            dve.wait_ge(xg_ready, NB)
            x_add(NB - 1)
            dve.wait_ge(xy_ready, NB)
            x_moments(x_res, 2)
            dve.wait_ge(xrstd_ready, 2)
            for b in range(NB):
                dve.tensor_scalar(z[:, b], x_res[:, b], x_mv[:, b, 0:1], x_rstd[:, b:b + 1],
                                  ALU.subtract, ALU.mult).then_inc(z_ready, 1)

            with dve.Fori(1, LAYERS + 1) as L:
                def add_out(T, n):
                    dve.wait_ge(y_full, T + 1)
                    zt = tile_of(z, n)
                    dve.tensor_tensor(zt, zt, y_ps[:, 0:D], ALU.add).then_inc(z_attn, 1)

                def ln_stats(T, n):
                    zt = tile_of(z, n, 0, D // 2)
                    dve.wait_ge(sh_full, T + 1)
                    dve.tensor_scalar(xs[:, 0:D // 2], zt, 1.0, None, ALU.mult).then_inc(xs_ready, 1)
                    dve.tensor_copy(xs[:, D // 2:D], y_ps[:, 0:D // 2]).then_inc(xs_ready, 1)
                    dve.wait_ge(xs_ready, T * 2 + 2)
                    dve.bn_stats(stats[:], xs[:]).then_inc(stat_done, 1)

                def ln_variance(T):
                    dve.bn_aggr(mean_var[:], stats[:]).then_inc(var_ready, 1)

                def ln_apply(T, n):
                    dve.wait_ge(rstd_ready, T + 1)
                    dve.tensor_scalar(tile_of(xn, n), xs[:],
                                      mean_var[:, 0:1], rstd[:], ALU.subtract, ALU.mult).then_inc(xn_ready, 1)

                def stage(T, n, groups_done):
                    dve.wait_ge(z_ready, groups_done)
                    dve.wait_ge(zt_full, T)
                    dve.tensor_scalar(z_stage[:], tile_of(z, n), 1.0, None, ALU.mult).then_inc(z_staged, 1)

                def front(T):
                    stage(T, 0, L * 4 + 12)
                    for c in range(4):
                        times_cos(T, c, L)
                        times_sin(T, c, L)
                        sum_squares(T, c)
                        clamp_norm(T, c)
                        if c == 2:
                            stage(T + 1, 1, L * 4 + 12)

                def step(T, g, behind=2, front_on=True, stats_ready=None):
                    Tn, gn = (T, g - 2) if g >= 2 else (T - 1, g + 2)
                    norm_on = g >= 2 or behind >= 1
                    mask(T, g)
                    row_maxima(T, g)
                    if front_on:
                        times_cos(T + 1, g, L)
                        times_sin(T + 1, g, L)
                        sum_squares(T + 1, g)
                    if norm_on:
                        sums_inverse(Tn, gn)
                    if front_on:
                        clamp_norm(T + 1, g)
                    if stats_ready is not None:
                        dve.wait_ge(stat_done, stats_ready)
                    if norm_on:
                        normalise(Tn, gn)

                def slot(T, n, par, first=False, behind=2, front_on=True, last_front=False):
                    if behind >= 2:
                        add_out(T - 2, n - 2)
                    step(T, 0, behind, front_on)
                    if behind >= 2:
                        ln_stats(T - 2, n - 2)
                    step(T, 1, behind, front_on, stats_ready=T - 1 if behind >= 2 else None)
                    if behind >= 2:
                        ln_variance(T - 2)
                    if front_on and not last_front:
                        stage(T + 2, n + 2, L * 4 + 12)
                    step(T, 2, behind, front_on)
                    step(T, 3, behind, front_on)
                    if behind >= 2:
                        ln_apply(T - 2, n - 2)
                    if first:
                        dve.wait_ge(ld_w1, L * 16)
                        dve.tensor_copy(w1_hi[:], w1_raw[:]).then_inc(w1_hi_done, 1)
                        dve.tensor_scalar(param[:], params[:, bass.ds(L - 1, 1), :].rearrange("p a b -> p (a b)"), 1.0, None,
                                          ALU.mult).then_inc(param_ready, 1)

                def drain(T, n, par):
                    add_out(T - 2, n - 2)
                    sums_inverse(T - 1, 2)
                    normalise(T - 1, 2)
                    ln_stats(T - 2, n - 2)
                    sums_inverse(T - 1, 3)
                    dve.wait_ge(stat_done, T - 1)
                    normalise(T - 1, 3)
                    ln_variance(T - 2)
                    ln_apply(T - 2, n - 2)
                    add_out(T - 1, n - 1)
                    ln_stats(T - 1, n - 1)
                    dve.wait_ge(ld_w, L * 16 + 16)
                    dve.wait_ge(stat_done, T)
                    w_round(0, L + 1)
                    ln_variance(T - 1)
                    ln_apply(T - 1, n - 1)

                layer_slots(dve.Fori, L, front, slot, drain)

                def f_gate(j, c):
                    F = L * NF + j
                    dve.wait_ge(gelu_done, F * 3 + (c + 1))
                    dve.wait_ge(a_full, F * 3 + (c + 1))
                    m = FC[c]
                    dve.scalar_tensor_tensor(h_T[j % 2][c][0:m, :], proj_ps[1][0:m, :], param[0:m, 2 + c:3 + c],
                                             gelu[0:m, (3 * j + c) % 2, :], ALU.add, ALU.mult).then_inc(h_ready, 1)

                def f_add(j):
                    F = L * NF + j
                    dve.wait_ge(fy_full, F + 1)
                    zg = flat(z[:, FG * j:FG * j + FG, :])
                    dve.tensor_tensor(zg, zg, s_ps[:, 0], ALU.add).then_inc(z_ready, 1)

                for j in range(NF):
                    f_gate(j, 0)
                    if j < 2:
                        w_round(j + 1, L + 1)
                    if j >= 1:
                        f_add(j - 1)
                    f_gate(j, 1)
                    f_gate(j, 2)
                f_add(NF - 1)

            dve.wait_ge(z_ready, NB + NF * LAYERS)
            dve.scalar_tensor_tensor(flat(z[:]), flat(z[:]), tanh_g[:, 1:2], flat(x_res[:]), ALU.mult, ALU.add).then_inc(result_ready, 1)

        @block.gpsimd
        def _(pool):
            pool.sem_inc(qk_added, 4 * NB)
            pool.sem_inc(qk_ready, 4 * NB)
            pool.sem_inc(x_split, NB)
            pool.sem_inc(f_split, NF)
            pool.memset(params[:], 0.0).then_inc(params_clear, 1)

            def w_rest(k, done):
                pool.wait_ge(w_hi_done, done)
                col = slice(INNER * k, INNER * (k + 1))
                pool.tensor_tensor(w_lo[:, col], w_raw[:, col], w_hi[:, col].bitcast(f32), ALU.subtract).then_inc(w_split, 1)

            for k in range(3):
                w_rest(k, k + 1)

            def split_x(T):
                pool.wait_ge(zt_evac, T + 1)
                pool.tensor_tensor(x_lo[:], x_all[:], x_hi[:].bitcast(f32), ALU.subtract).then_inc(x_split, 1)

            def add_rotated(T, c):
                pool.wait_ge(rotated, T * 4 + (c + 1))
                pool.wait_ge(tr_full, T * 4 + (c - 3))
                pool.tensor_tensor(heads(qk[:, c, :]), heads(by_cos[:, c % 2, :]),
                                   heads(by_sin[:, c % 2, :])[:, :, ::-1, :], ALU.add).then_inc(qk_added, 1)

            def scale_rotated(T, c):
                pool.wait_ge(qk_added, T * 4 + (c + 1))
                pool.wait_ge(inv_ready, T * 4 + (c + 1))
                ap = qk[:, c, :].rearrange("p (h d) -> p h d", d=DH)
                pool.tensor_tensor(ap, ap, inv_norm[:, c, :].unsqueeze(2).to_broadcast([128, 8, DH]),
                                   ALU.mult).then_inc(qk_ready, 1)

            def center(T, g):
                pool.wait_ge(max_ready, T * 4 + (g + 1))
                pool.tensor_tensor(s_sb[:, g % 2], s_sb[:, g % 2],
                                   row_max[:, g % 2, :].unsqueeze(2).to_broadcast([128, GH, NT]), ALU.subtract).then_inc(centered, 1)

            def x_keys(T, par):
                pool.wait_ge(xqk_out, T + 1)
                pool.tensor_tensor(xk_bd[:, par], xk[:].unsqueeze(1).to_broadcast([128, GH, NT]),
                                   head_of[:].unsqueeze(2).to_broadcast([128, GH, NT]), ALU.mult).then_inc(xk_ready, 1)

            def x_bias_pos(T, par, g, first=False):
                if not (first and g < 2):
                    pool.wait_ge(masked, T * 4 + (g - 1))
                pool.wait_ge(clip_ready, T + 1)
                pool.tensor_tensor(bias_pos[:, g % 2], d_pos[:, par].unsqueeze(1).to_broadcast([128, GH, NT]),
                                   alpha[:, 0, GH * g:GH * g + GH].unsqueeze(2).to_broadcast([128, GH, NT]),
                                   ALU.mult).then_inc(bias_ready, 1)

            def x_slot(T, par, first=False, front_on=True):
                x_bias_pos(T, par, 1, first)
                center(T, 0)
                x_bias_pos(T, par, 2)
                center(T, 1)
                x_bias_pos(T, par, 3)
                center(T, 2)
                if front_on:
                    x_bias_pos(T + 1, 1 - par, 0)
                    x_keys(T + 1, 1 - par)
                center(T, 3)

            pool.wait_ge(bc_ld, N_BC)
            pool.wait_ge(scalar_ready, 1)
            x_bias_pos(0, 0, 0, first=True)
            x_keys(0, 0)
            x_slot(0, 0, first=True)
            with pool.Fori(0, NB // 2 - 1) as pair:
                x_slot(pair * 2 + 1, 1)
                x_slot(pair * 2 + 2, 0)
            x_slot(NB - 1, 1, front_on=False)

            with pool.Fori(1, LAYERS + 1) as L:
                def front(T):
                    split_x(T)
                    add_rotated(T, 0)
                    for c in range(3):
                        add_rotated(T, c + 1)
                        scale_rotated(T, c)
                    split_x(T + 1)

                def slot(T, n, par, first=False, behind=2, front_on=True, last_front=False):
                    for g in range(NG):
                        if g == 0:
                            scale_rotated(T, 3)
                        elif front_on:
                            scale_rotated(T + 1, g - 1)
                        center(T, g)
                        if front_on:
                            if g == 3 and not last_front:
                                split_x(T + 2)
                            add_rotated(T + 1, g)
                    if first:
                        pool.wait_ge(w1_hi_done, L)
                        pool.tensor_tensor(w1_lo[:], w1_raw[:], w1_hi[:].bitcast(f32), ALU.subtract).then_inc(w1_split, 1)

                def drain(T, n, par):
                    pass

                layer_slots(pool.Fori, L, front, slot, drain)

                for j in range(NF):
                    F = L * NF + j
                    pool.wait_ge(ft_evac, F + 1)
                    pool.tensor_tensor(f_lo[:, j % 2, :], f_all[:, j % 2, :], f_hi[:, j % 2, :].bitcast(f32),
                                       ALU.subtract).then_inc(f_split, 1)
                    if j < 3:
                        w_rest(j, L * 3 + (j + 1))


def constants():
    one = np.float32
    half = np.arange(0, DH, 2, dtype=np.float32)
    inv_freq = (one(1.0) / one(10000.0) ** (half / one(DH))).astype(np.float32)
    pos = np.arange(NT, dtype=np.float32)
    freqs = pos[:, None] * inv_freq[None, :]
    base = (half + one(0.4 * DH)) / one(1.4 * DH)
    power = (pos - NT // 2) / one(WINDOW // 2)
    scale = base[None, :] ** power[:, None]
    cos, sin = np.cos(freqs), np.sin(freqs)
    rot = np.zeros((NT, 4, DH), np.float32)
    for i, s in ((0, QK_SCALE * scale), (2, 1.0 / scale)):
        rot[:, i] = np.concatenate([cos * s, cos * s], 1)
        rot[:, i + 1] = np.concatenate([sin * s, -sin * s], 1)
    p = np.arange(128)
    d = p[:, None] - p[None, :]
    band = np.where((d >= 0) & (d <= WINDOW), 0.0, NEG).astype(np.float32)
    head_of = (np.arange(128)[:, None] // XD % GH == np.arange(GH)[None, :]).astype(np.float32)
    return {"head_of": head_of, "ident": np.eye(128, dtype=np.float32), "shift": np.eye(128, k=1, dtype=np.float32),
            "band": band, "rot": rot.reshape(NT, 4 * DH)}


NAMES = ['x', 'ctx_1024', 'fside_BxS2_0', 'g_xattn', 'g_ffn', 'L0_xattn_Wq', 'L0_xattn_bq', 'L0_xattn_Wk', 'L0_xattn_bk',
         'L0_xattn_Wv', 'L0_xattn_bv', 'L0_xattn_Wo', 'L0_xattn_bo', 'L0_xattn_alpha_pos', 'L0_xattn_alpha_neg',
         'L0_xattn_gamma', 'L0_xattn_delta', 'L0_ffn_Wqkv', 'L0_ffn_q_scale', 'L0_ffn_k_scale', 'L0_ffn_Wo',
         'L0_ffn_ln_g', 'L0_ffn_ln_b', 'L0_ffn_W1', 'L0_ffn_b1', 'L0_ffn_W2', 'L0_ffn_b2']


def kernel(**inputs):
    import numpy as _np
    import concourse.bacc as _bacc
    from concourse import mybir as _mybir
    from concourse.bass_utils import run_bass_kernel_spmd as _run

    nc = _bacc.Bacc("TRN2", target_bir_lowering=False, num_devices=1)
    arrays, args = {}, {}
    given = {n: inputs[n] for n in NAMES} | constants()
    for name, a in given.items():
        a = _np.ascontiguousarray(a)
        arrays[f"in_{name}"] = a
        args[name] = nc.dram_tensor(f"in_{name}", a.shape, _mybir.dt.from_np(a.dtype), kind="ExternalInput").ap()
    args["out"] = nc.dram_tensor("out_0", (NB, NT, D), _mybir.dt.float32, kind="ExternalOutput").ap()
    build(nc, args)
    r = _run(nc, [arrays], core_ids=[0])
    return r.results[0]["out_0"]
```

```python
from contextlib import ExitStack

import concourse.bass as bass
import numpy as np
from concourse import mybir

f32 = mybir.dt.float32
f32r = mybir.dt.float32r
ALU = mybir.AluOpType
ACT = mybir.ActivationFunctionType
AX = mybir.AxisListType.X

NB, NT, D = 16, 128, 128
H, DH = 16, 64
HALF = DH // 2
LAYERS = 6
INNER = H * DH
WINDOW = 32
QK_SCALE = 8.0
FI = D * 4 * 2 // 3
FC = [128, 128, FI - 256]
XH, XD = 16, 8
GH = 4
NG = H // GH
FG = 4
NF = NB // FG
CLAMP = 0.2
NEG = -1.0e30
LN_EPS = 1e-5
CHUNK_COL = [0, INNER, 2 * INNER, 512, 2 * INNER + 512, INNER + 512]
QK_AT = [0, 1, 3, 5]
V_AT = [2, 4]


def build(nc, t):
    ctx = ExitStack()
    with ctx:
        ctx.enter_context(nc.allow_non_contiguous_dma(reason="small vectors laid along the partitions"))

        def sb(name, shape, dt=f32):
            return ctx.enter_context(nc.sbuf_tensor(name, shape, dt))

        def bank(name):
            return ctx.enter_context(nc.psum_tensor(name, [128, 512], f32))

        def sem(name):
            return ctx.enter_context(nc.semaphore(name))

        z = sb("z", [128, NB, D])
        ident = sb("ident", [128, 128])
        shift = sb("shift", [128, 128])
        band = sb("band", [128, 128])
        rot = sb("rot", [128, 4, DH])
        qk_scale = sb("qk_scale", [128, 2, LAYERS, DH])
        tab = sb("tab", [128, 4, LAYERS, DH])
        eps = sb("eps", [128, 1])
        params = sb("params", [128, LAYERS, 8])
        param = sb("param", [128, 8])
        w_raw = sb("w_raw", [128, 3 * INNER])
        w_hi = sb("w_hi", [128, 3 * INNER], f32r)
        w_lo = sb("w_lo", [128, 3 * INNER], f32r)
        w1_raw = sb("w1_raw", [128, 2 * FI])
        w1_hi = sb("w1_hi", [128, 2 * FI], f32r)
        w1_lo = sb("w1_lo", [128, 2 * FI], f32r)
        wo = sb("wo", [128, INNER // 128, D])
        w2 = sb("w2", [128, 3, D])
        z_stage = sb("z_stage", [128, D])
        x_all = sb("x_all", [128, NT])
        x_hi = sb("x_hi", [128, NT], f32r)
        x_lo = sb("x_lo", [128, NT], f32r)
        square = sb("square", [128, 2, 512])
        by_cos = sb("by_cos", [128, 2, 512])
        by_sin = sb("by_sin", [128, 2, 512])
        sumsq = sb("sumsq", [128, 4, 8])
        log_sq = sb("log_sq", [128, 4, 8])
        inv_norm = sb("inv_norm", [128, 4, 8])
        qk = sb("qk", [128, 4, 512])
        q_T = [sb(f"q_T{i}", [128, 8, NT]) for i in range(2)]
        k_T = [sb(f"k_T{i}", [128, 8, NT]) for i in range(2)]
        v = [sb(f"v{i}", [128, H, DH + 1]) for i in range(2)]
        s_sb = sb("s_sb", [128, 2, GH, NT])
        row_max = sb("row_max", [128, 2, GH])
        p_sb = sb("p_sb", [128, 2, GH, NT])
        p_T = sb("p_T", [128, 2, GH, NT])
        inv_sum = sb("inv_sum", [128, GH])
        att = sb("att", [128, H, DH])
        att_T = sb("att_T", [128, INNER // 128, NT])
        xs = sb("xs", [128, 2, D])
        x_res = sb("x_res", [128, NB, D])
        xw_raw = sb("xw_raw", [128, 4, D])
        xw_T = sb("xw_T", [128, 4, D])
        xb_col = sb("xb_col", [128, 2])
        xb_row = sb("xb_row", [128, 2, D])
        alpha = sb("alpha", [128, 2, XH])
        gates = sb("gates", [128, 4])
        tanh_g = sb("tanh_g", [128, 2])
        q_scale = sb("q_scale", [128, 2])
        frac_q = sb("frac_q", [128, NB])
        head_of = sb("head_of", [128, GH])
        x_mv = sb("x_mv", [128, NB, 2])
        x_st = sb("x_st", [128, NB, 6])
        x_log = sb("x_log", [128, NB])
        x_rstd = sb("x_rstd", [128, NB])
        x_in = sb("x_in", [128, 2, D])
        c_in = sb("c_in", [128, 2, D])
        xc_T = sb("xc_T", [128, 2, NT])
        xq = sb("xq", [128, 2, NT])
        xk = sb("xk", [128, NT])
        xv = sb("xv", [128, 2, NG, GH, GH * XD])
        d_clip = sb("d_clip", [128, 2, NT])
        d_pos = sb("d_pos", [128, 2, NT])
        d_neg = sb("d_neg", [128, 2, NT])
        row_min = sb("row_min", [128, 2, GH])
        p_sum = sb("p_sum", [128, 2, GH])
        x_inv_sum = sb("x_inv_sum", [128, 2, GH])
        x_att_T = sb("x_att_T", [128, NT])
        stats = sb("stats", [128, 2, 6])
        mean_var = sb("mean_var", [128, 2, 2])
        log_var = sb("log_var", [128, 2])
        rstd = sb("rstd", [128, 2])
        xn = sb("xn", [128, NB, D])
        f_all = sb("f_all", [128, 2, 512])
        f_hi = sb("f_hi", [128, 2, 512], f32r)
        f_lo = sb("f_lo", [128, 2, 512], f32r)
        gelu = sb("gelu", [128, 2, 512])
        frac_k = xn
        x_bias = f_all[:].rearrange("p i (h k) -> p i h k", k=NT)
        xk_bd = gelu[:].rearrange("p i (h k) -> p i h k", k=NT)
        h_T = [[sb(f"h_T{i}{c}", [128, 512]) for c in range(3)] for i in range(2)]

        proj_ps = [bank("proj_ps0"), bank("proj_ps1")]
        tr_ps = bank("tr_ps")
        pt_ps = bank("pt_ps")
        s_ps = ctx.enter_context(nc.psum_tensor("s_ps", [128, 2, 512], f32))
        pv_ps = bank("pv_ps")
        y_ps = bank("y_ps")

        first_ps = [pv_ps, y_ps]

        x_pv_ps = [proj_ps[1], pv_ps]

        ident_ld = sem("ident_ld")
        const_ld = sem("const_ld")
        param_ld = sem("param_ld")
        ld_w = sem("ld_w")
        ld_w1 = sem("ld_w1")
        ld_wo = sem("ld_wo")
        ld_w2 = sem("ld_w2")
        setup_done = sem("setup_done")
        w_hi_done = sem("w_hi_done")
        w_split = sem("w_split")
        w1_hi_done = sem("w1_hi_done")
        w1_split = sem("w1_split")
        params_clear = sem("params_clear")
        param_ready = sem("param_ready")
        z_staged = sem("z_staged")
        x_split = sem("x_split")
        tr_full = sem("tr_full")
        tr_evac = sem("tr_evac")
        zt_full = sem("zt_full")
        zt_evac = sem("zt_evac")
        proj_full = sem("proj_full")
        squared = sem("squared")
        rotated = sem("rotated")
        summed = sem("summed")
        norm_ready = sem("norm_ready")
        inv_log = sem("inv_log")
        inv_ready = sem("inv_ready")
        qk_added = sem("qk_added")
        qk_ready = sem("qk_ready")
        v_ready = sem("v_ready")
        s_full = sem("s_full")
        masked = sem("masked")
        max_ready = sem("max_ready")
        centered = sem("centered")
        p_ready = sem("p_ready")
        pt_full = sem("pt_full")
        pt_evac = sem("pt_evac")
        pv_full = sem("pv_full")
        recip_done = sem("recip_done")
        att_ready = sem("att_ready")
        ot_full = sem("ot_full")
        ot_evac = sem("ot_evac")
        y_full = sem("y_full")
        z_attn = sem("z_attn")
        sh_full = sem("sh_full")
        xs_ready = sem("xs_ready")
        stat_done = sem("stat_done")
        var_ready = sem("var_ready")
        log_done = sem("log_done")
        rstd_ready = sem("rstd_ready")
        xn_ready = sem("xn_ready")
        ft_full = sem("ft_full")
        ft_evac = sem("ft_evac")
        f_split = sem("f_split")
        gate_full = sem("gate_full")
        a_full = sem("a_full")
        gelu_done = sem("gelu_done")
        h_ready = sem("h_ready")
        fy_full = sem("fy_full")
        z_ready = sem("z_ready")
        out_done = sem("out_done")
        result_ready = sem("result_ready")
        xw_ld = sem("xw_ld")
        bc_ld = sem("bc_ld")
        frac_ld = sem("frac_ld")
        x_ld = sem("x_ld")
        ctx_ld = [sem("ctx_ld_even"), sem("ctx_ld_odd")]
        xw_full = sem("xw_full")
        xw_evac = sem("xw_evac")
        xstat_done = sem("xstat_done")
        xvar_ready = sem("xvar_ready")
        xlog_done = sem("xlog_done")
        xrstd_ready = sem("xrstd_ready")
        xin_ready = sem("xin_ready")
        xt_full = sem("xt_full")
        xt_evac = sem("xt_evac")
        xproj_full = sem("xproj_full")
        xqk_out = sem("xqk_out")
        xk_ready = sem("xk_ready")
        xv_ready = sem("xv_ready")
        scalar_ready = sem("scalar_ready")
        tanh_done = sem("tanh_done")
        xscaled = sem("xscaled")
        xclip = sem("xclip")
        clip_ready = sem("clip_ready")
        pos_ready = sem("pos_ready")
        bias_ready = sem("bias_ready")
        xv_clear = sem("xv_clear")
        min_ready = sem("min_ready")
        exp_ready = sem("exp_ready")
        x_recip_done = sem("x_recip_done")
        xo_evac = sem("xo_evac")
        xy_full = sem("xy_full")
        xy_ready = sem("xy_ready")
        xg_ready = sem("xg_ready")
        block = ctx.enter_context(nc.Block())

        def heads(ap):
            return ap.rearrange("p (h x d) -> p h x d", x=2, d=HALF)

        def tile_of(ap, n, lo=0, hi=D):
            return ap[:, bass.ds(n, 1), lo:hi].rearrange("p a b -> p (a b)")

        def flat(ap):
            return ap.rearrange("p a b -> p (a b)")

        def layer_slots(eng_fori, L, slot):
            T0 = L * NB
            slot(T0, 0, 0, first=True, behind=0)
            slot(T0 + 1, 1, 1, behind=1)
            with eng_fori(0, (NB - 4) // 2) as pair:
                n = pair * 2 + 2
                slot(T0 + n, n, 0)
                slot(T0 + n + 1, n + 1, 1)
            slot(T0 + NB - 2, NB - 2, 0, last_front=True)
            slot(T0 + NB - 1, NB - 1, 1, front_on=False)

        def after(T, n):
            return not isinstance(T, int) or T >= n

        @block.sync
        def _(sp):
            for i, n in enumerate(("Wq", "Wk", "Wv", "Wo")):
                sp.dma_start(xw_raw[:, i], t["L0_xattn_" + n]).then_inc(xw_ld, 16)
            sp.dma_start(ident[:], t["ident"]).then_inc(ident_ld, 16)
            sp.dma_start(x_res[:], t["x"].rearrange("b t d -> t b d")).then_inc(x_ld, 16)

            def load_w(layer):
                sp.dma_start(w_raw[:], t["L0_ffn_Wqkv"][layer]).then_inc(ld_w, 16)

            def load_w1(layer):
                sp.dma_start(w1_raw[:], t["L0_ffn_W1"][layer]).then_inc(ld_w1, 16)

            def load_wo(layer):
                sp.dma_start(wo[:], t["L0_ffn_Wo"][layer].rearrange("(c p) d -> p c d", p=128)).then_inc(ld_wo, 16)

            def load_w2(layer):
                w2_d = t["L0_ffn_W2"][layer]
                sp.dma_start(w2[:, 0:2, :], w2_d[0:256, :].rearrange("(c p) d -> p c d", p=128)).then_inc(ld_w2, 16)
                sp.dma_start(w2[0:FC[2], 2, :], w2_d[256:FI, :]).then_inc(ld_w2, 16)
                sp.dma_start(w2[FC[2]:FC[2] + 1, 2, :], t["L0_ffn_b2"][layer].unsqueeze(0)).then_inc(ld_w2, 16)

            for T in range(2):
                sp.dma_start(c_in[:, T], t["ctx_1024"][T]).then_inc(ctx_ld[T], 16)
            for i, n in enumerate(("bq", "bk")):
                sp.dma_start(xb_col[:, i:i + 1], t["L0_xattn_" + n].unsqueeze(1)).then_inc(bc_ld, 16)
            for i, n in enumerate(("bv", "bo")):
                sp.dma_start(xb_row[:, i], t["L0_xattn_" + n].unsqueeze(0).to_broadcast([128, D])).then_inc(bc_ld, 16)
            for i, n in enumerate(("alpha_pos", "alpha_neg")):
                sp.dma_start(alpha[:, i], t["L0_xattn_" + n].unsqueeze(0).to_broadcast([128, XH])).then_inc(bc_ld, 16)
            for i, n in enumerate(("L0_xattn_gamma", "L0_xattn_delta", "g_xattn", "g_ffn")):
                sp.dma_start(gates[:, i:i + 1], t[n].unsqueeze(0).to_broadcast([128, 1])).then_inc(bc_ld, 16)
            sp.dma_start(head_of[:], t["head_of"]).then_inc(bc_ld, 16)
            sp.dma_start(frac_q[:], t["fside_BxS2_0"].rearrange("b t -> t b")).then_inc(frac_ld, 16)
            sp.dma_start(flat(frac_k[:]), t["fside_BxS2_0"].rearrange("b t -> (b t)").unsqueeze(0).to_broadcast([128, NB * NT])).then_inc(frac_ld, 16)

            consts = [(shift[:], t["shift"]), (band[:], t["band"]),
                      (flat(rot[:]), t["rot"])]
            for dst, src in consts:
                sp.dma_start(dst, src).then_inc(const_ld, 16)
            for i, name in enumerate(("L0_ffn_q_scale", "L0_ffn_k_scale")):
                src = t[name].rearrange("l d -> (l d)").unsqueeze(0).to_broadcast([128, LAYERS * DH])
                sp.dma_start(flat(qk_scale[:, i]), src).then_inc(const_ld, 16)
            load_w(0)
            load_w1(0)
            load_wo(0)
            load_w2(0)
            sp.wait_ge(params_clear, 1)
            sp.dma_start(params[:, :, 0], t["L0_ffn_ln_g"].rearrange("l d -> d l")).then_inc(param_ld, 16)
            sp.dma_start(params[:, :, 1], t["L0_ffn_ln_b"].rearrange("l d -> d l")).then_inc(param_ld, 16)
            for half in range(2):
                for c in range(3):
                    col = half * FI + 128 * c
                    sp.dma_start(params[0:FC[c], :, 2 + 3 * half + c],
                                 t["L0_ffn_b1"][:, col:col + FC[c]].rearrange("l d -> d l")).then_inc(param_ld, 16)
            ctx_d = t["ctx_1024"].rearrange("b t d -> t b d")
            with sp.Fori(1, NB // 2) as pair:
                for par in range(2):
                    sp.wait_ge(xt_full, pair * 2 + (par - 1))
                    sp.dma_start(c_in[:, par:par + 1, :], ctx_d[:, bass.ds(pair * 2 + par, 1), :]).then_inc(ctx_ld[par], 16)
            with sp.Fori(1, LAYERS + 1) as L:
                nxt = L % LAYERS
                sp.wait_ge(w_split, L * 3)
                sp.dma_start(w_raw[:].unsqueeze(1), t["L0_ffn_Wqkv"].rearrange("l p n -> p l n")[:, bass.ds(nxt, 1), :]).then_inc(ld_w, 16)
                sp.wait_ge(w1_split, L)
                sp.dma_start(w1_raw[:].unsqueeze(1), t["L0_ffn_W1"].rearrange("l p n -> p l n")[:, bass.ds(nxt, 1), :]).then_inc(ld_w1, 16)
                sp.wait_ge(y_full, L * NB + NB)
                sp.dma_start(wo[:], t["L0_ffn_Wo"].rearrange("l (c p) d -> p (l c) d", p=128)[:, bass.ds(nxt * 8, 8), :]).then_inc(ld_wo, 16)
                sp.wait_ge(fy_full, L * NF + NF)
                w2_d = t["L0_ffn_W2"]
                for c in range(3):
                    sp.dma_start(w2[0:FC[c], c:c + 1, :], w2_d[:, 128 * c:128 * c + FC[c], :].rearrange("l p d -> p l d")[:, bass.ds(nxt, 1), :]).then_inc(ld_w2, 16)
                sp.dma_start(w2[FC[2]:FC[2] + 1, 2:3, :], t["L0_ffn_b2"].unsqueeze(0)[:, bass.ds(nxt, 1), :]).then_inc(ld_w2, 16)
            for j in range(NF):
                seqs = slice(FG * j, FG * (j + 1))
                sp.wait_ge(result_ready, j + 1)
                sp.dma_start(t["out"][seqs].rearrange("b t d -> t b d"), z[:, seqs]).then_inc(out_done, 16)
            sp.wait_ge(out_done, 16 * NF)
            sp.wait_ge(ld_w, 16 * (LAYERS + 1))
            sp.wait_ge(ld_w1, 16 * (LAYERS + 1))
            sp.wait_ge(ld_wo, 16 * (LAYERS + 1))
            sp.wait_ge(ld_w2, 48 + 64 * LAYERS)

        N_CONST = 16 * 5
        N_PARAM = 16 * 8
        N_BC = 16 * 11

        @block.tensor
        def _(pe):
            pe.sem_inc(tr_full, 4 * NB)
            pe.sem_inc(zt_full, NB)
            pe.sem_inc(proj_full, 6 * NB)
            pe.sem_inc(ot_full, 2 * NB)
            pe.sem_inc(y_full, NB)
            pe.sem_inc(sh_full, NB)
            pe.sem_inc(ft_full, NF)
            pe.sem_inc(gate_full, 3 * NF)
            pe.sem_inc(a_full, 3 * NF)
            pe.sem_inc(fy_full, NF)
            pe.wait_ge(ident_ld, 16)
            pe.wait_ge(setup_done, 1)

            def x_transpose(T, behind=2):
                pe.wait_ge(z_staged, T + 1)
                pe.wait_ge(tr_evac, T * 4 - behind)
                pe.transpose(tr_ps[:, 0:128], z_stage[:], ident[:]).then_inc(zt_full, 1)

            def project(T, m, banks=proj_ps):
                if m == 0:
                    pe.wait_ge(x_split, T + 1)
                    pe.wait_ge(v_ready, T * 2)
                elif m == 1:
                    pe.wait_ge(rotated, T * 4)
                elif m == 4:
                    pe.wait_ge(v_ready, T * 2 + 1)
                else:
                    pe.wait_ge(rotated, T * 4 + (1, 2, None, 3)[m - 2])
                col = slice(CHUNK_COL[m], CHUNK_COL[m] + 512)
                ps = banks[m % 2]
                pe.matmul(ps[:], x_hi[:], w_hi[:, col], start=True, stop=False)
                pe.matmul(ps[:], x_hi[:], w_lo[:, col], start=False, stop=False)
                pe.matmul(ps[:], x_lo[:], w_hi[:, col], start=False, stop=True).then_inc(proj_full, 1)

            def qk_transpose(T, c, after_x=False):
                pe.wait_ge(qk_ready, T * 4 + (c + 1))
                pe.wait_ge(tr_evac, T * 4 + c)
                if after_x:
                    pe.wait_ge(zt_evac, T + 2)
                for j in range(4):
                    mm = pe.transpose(tr_ps[:, 128 * j:128 * j + 128], qk[:, c, 128 * j:128 * j + 128], ident[:])
                mm.then_inc(tr_full, 1)

            def scores(T, par, g):
                pe.wait_ge(tr_evac, T * 4 + (2 * (g // 2) + 2))
                pe.wait_ge(masked, T * 4 + g)
                for j in range(GH):
                    pair, row = 2 * g + j // 2, 64 * (j % 2)
                    mm = pe.matmul(s_ps[:, j % 2, NT * (j // 2):NT * (j // 2 + 1)], q_T[par][row:row + 64, pair, :],
                                   k_T[par][row:row + 64, pair, :], start=True, stop=True)
                mm.then_inc(s_full, 1)

            def p_transpose(T, g):
                pe.wait_ge(p_ready, T * 4 + (g + 1))
                if after(T, 1) or g >= 1:
                    pe.wait_ge(pt_evac, T * 4 + g)
                for j in range(GH):
                    mm = pe.transpose(pt_ps[:, 128 * j:128 * j + 128], p_sb[:, g % 2, j, :], ident[:])
                mm.then_inc(pt_full, 1)

            def values(T, par, g):
                pe.wait_ge(pt_evac, T * 4 + (g + 1))
                pe.wait_ge(v_ready, T * 2 + 2)
                pe.wait_ge(att_ready, T * 4 + g)
                for j in range(GH):
                    mm = pe.matmul(pv_ps[:, (DH + 1) * j:(DH + 1) * (j + 1)], p_T[:, g % 2, j, :],
                                   v[par][:, GH * g + j, :], start=True, stop=True)
                mm.then_inc(pv_full, 1)

            def att_transpose(T, i):
                pe.wait_ge(att_ready, T * 4 + (2 * i + 2))
                pe.wait_ge(ot_evac, T * 2 + i)
                if i == 0:
                    pe.wait_ge(xs_ready, T * 2)
                for j in range(4):
                    mm = pe.transpose(y_ps[:, 128 * j:128 * j + 128],
                                      att[:, 8 * i + 2 * j:8 * i + 2 * j + 2, :].rearrange("p a b -> p (a b)"), ident[:])
                mm.then_inc(ot_full, 1)

            def out_project(T, L):
                pe.wait_ge(ld_wo, L * 16)
                pe.wait_ge(ot_evac, T * 2 + 2)
                for c in range(8):
                    mm = pe.matmul(y_ps[:, 0:D], att_T[:, c, :], wo[:, c, :], start=(c == 0), stop=(c == 7))
                mm.then_inc(y_full, 1)

            def shift_state(T, src):
                pe.wait_ge(z_attn, T + 1)
                pe.matmul(y_ps[:, 0:D // 2], shift[:], src, start=True, stop=True).then_inc(sh_full, 1)

            def x_setup():
                pe.wait_ge(xw_ld, 64)
                for i in range(4):
                    mm = pe.transpose(pt_ps[:, 128 * i:128 * i + 128], xw_raw[:, i], ident[:])
                mm.then_inc(xw_full, 1)

            def x_inputs(T, par):
                pe.wait_ge(ctx_ld[par], (T - par) * 8 + 16)
                pe.wait_ge(xin_ready, T + 1)
                pe.transpose(tr_ps[:, 0:128], x_in[:, par], ident[:])
                pe.transpose(tr_ps[:, 128:256], c_in[:, par], ident[:]).then_inc(xt_full, 1)

            def x_project(T):
                pe.wait_ge(xt_evac, T + 1)
                if after(T, 1):
                    pe.wait_ge(xv_ready, T)
                else:
                    pe.wait_ge(xw_evac, 1)
                pe.matmul(proj_ps[0][:, 0:128], xw_T[:, 0], xc_T[:, 0], start=True, stop=True)
                pe.matmul(proj_ps[0][:, 128:256], xw_T[:, 1], xc_T[:, 1], start=True, stop=True)
                pe.matmul(proj_ps[0][:, 256:384], xc_T[:, 1], xw_T[:, 2], start=True, stop=True).then_inc(xproj_full, 1)

            def x_scores(T, par, g):
                if g == 0:
                    pe.wait_ge(xk_ready, T + 1)
                if after(T, 1) or g >= 2:
                    pe.wait_ge(masked, T * 4 + (g - 1))
                rows = slice(32 * g, 32 * g + 32)
                pe.matmul(s_ps[:, g % 2, :], xq[rows, par, :], flat(xk_bd[rows, par]), start=True, stop=True).then_inc(s_full, 1)

            def x_values(T, par, g):
                pe.wait_ge(pt_evac, T * 4 + (g + 1))
                if g == 0:
                    pe.wait_ge(xv_ready, T + 1)
                    if after(T, 2):
                        pe.wait_ge(xo_evac, T - 1)
                rows = slice(32 * g, 32 * g + 32)
                for j in range(GH):
                    mm = pe.matmul(x_pv_ps[par][rows, 0:NT], xv[:, par, g, j, :], p_T[:, g % 2, j, :],
                                   start=(j == 0), stop=(j == GH - 1))
                mm.then_inc(pv_full, 1)

            def x_out_project(T):
                pe.wait_ge(xo_evac, T + 1)
                if after(T, 1):
                    pe.wait_ge(xy_ready, T)
                pe.matmul(y_ps[:, 0:128], x_att_T[:], xw_T[:, 3], start=True, stop=True).then_inc(xy_full, 1)

            def x_slot(T, par, first=False, front_on=True):
                x_scores(T, par, 0)
                if not first:
                    p_transpose(T - 1, 2)
                if front_on:
                    x_inputs(T + 1, 1 - par)
                if not first:
                    x_values(T - 1, 1 - par, 1)
                x_scores(T, par, 1)
                if not first:
                    p_transpose(T - 1, 3)
                if front_on:
                    x_project(T + 1)
                if not first:
                    x_values(T - 1, 1 - par, 2)
                x_scores(T, par, 2)
                p_transpose(T, 0)
                if not first:
                    x_values(T - 1, 1 - par, 3)
                x_scores(T, par, 3)
                p_transpose(T, 1)
                x_values(T, par, 0)
                if not first:
                    x_out_project(T - 1)

            x_setup()
            x_inputs(0, 0)
            x_project(0)
            x_slot(0, 0, first=True)
            x_slot(1, 1)
            with pe.Fori(1, NB // 2 - 1) as pair:
                x_slot(pair * 2, 0)
                x_slot(pair * 2 + 1, 1)
            x_slot(NB - 2, 0)
            x_slot(NB - 1, 1, front_on=False)
            def first_chunk(T, L, m, banks=first_ps):
                if m == 0:
                    pe.wait_ge(w_split, L * 3)
                    pe.wait_ge(att_ready, T * 4)
                    pe.wait_ge(xs_ready, T * 2)
                project(T, m, banks)

            p_transpose(NB - 1, 2)
            x_values(NB - 1, 1, 1)
            p_transpose(NB - 1, 3)
            x_values(NB - 1, 1, 2)
            pe.wait_ge(xv_ready, NB)
            x_transpose(NB, behind=0)
            x_values(NB - 1, 1, 3)
            first_chunk(NB, 1, 0, proj_ps)
            x_out_project(NB - 1)
            pe.wait_ge(const_ld, N_CONST)
            for m in range(1, 6):
                first_chunk(NB, 1, m, proj_ps)
            x_transpose(NB + 1, behind=4)
            qk_transpose(NB, 0, after_x=True)
            qk_transpose(NB, 1)

            with pe.Fori(1, LAYERS + 1) as L:
                def f_transpose(j, ps=pt_ps):
                    F = L * NF + j
                    pe.wait_ge(xn_ready, L * NB + (FG * j + FG))
                    pe.wait_ge(ft_evac, F)
                    if j == 0:
                        pe.wait_ge(tr_evac, (L * NB + NB) * 4)
                    for i in range(FG):
                        mm = pe.transpose(ps[:, 128 * i:128 * i + 128], xn[:, FG * j + i, :], ident[:])
                    mm.then_inc(ft_full, 1)

                def f_up(j, c):
                    F = L * NF + j
                    if c == 0:
                        pe.wait_ge(f_split, F + 1)
                    pe.wait_ge(w1_split, L)
                    for half, ps, full, free in ((1, proj_ps[0], gate_full, gelu_done), (0, proj_ps[1], a_full, h_ready)):
                        col = slice(half * FI + 128 * c, half * FI + 128 * c + FC[c])
                        pe.wait_ge(free, F * 3 + c)
                        o = ps[0:FC[c], :]
                        pe.matmul(o, w1_hi[:, col], f_hi[:, j % 2, :], start=True, stop=False)
                        pe.matmul(o, w1_hi[:, col], f_lo[:, j % 2, :], start=False, stop=False)
                        pe.matmul(o, w1_lo[:, col], f_hi[:, j % 2, :], start=False, stop=True).then_inc(full, 1)

                def f_down(j, seqs=range(FG)):
                    F = L * NF + j
                    if seqs[0] == 0:
                        pe.wait_ge(ld_w2, L * 64 - 16)
                        pe.wait_ge(h_ready, F * 3 + 3)
                        if j >= 2:
                            pe.wait_ge(z_ready, F + 11)
                    for i in seqs:
                        for c in range(3):
                            k = FC[c] + (c == 2)
                            mm = pe.matmul(s_ps[:, j % 2, 128 * i:128 * i + 128], h_T[j % 2][c][0:k, 128 * i:128 * i + 128],
                                           w2[0:k, c, :], start=(c == 0), stop=(c == 2))
                    if seqs[-1] == FG - 1:
                        mm.then_inc(fy_full, 1)

                def slot(T, n, par, first=False, behind=2, front_on=True, last_front=False):
                    if first:
                        pe.wait_ge(z_ready, L * NF + (NB - NF))
                    scores(T, par, 0)
                    if front_on:
                        project(T + 1, 0)
                    if behind >= 1:
                        p_transpose(T - 1, 3)
                        values(T - 1, 1 - par, 2)
                    if behind >= 2:
                        shift_state(T - 2, tile_of(z, n - 2, D // 2))
                    if first:
                        qk_transpose(T, 2)
                    qk_transpose(T, 3)
                    scores(T, par, 1)
                    if front_on:
                        project(T + 1, 1)
                    p_transpose(T, 0)
                    if behind >= 1:
                        values(T - 1, 1 - par, 3)
                        att_transpose(T - 1, 0)
                    if front_on:
                        project(T + 1, 2)
                        qk_transpose(T + 1, 0)
                    scores(T, par, 2)
                    if front_on:
                        project(T + 1, 3)
                    else:
                        f_transpose(0, tr_ps)
                    p_transpose(T, 1)
                    values(T, par, 0)
                    if behind >= 1:
                        att_transpose(T - 1, 1)
                    if front_on:
                        project(T + 1, 4)
                        qk_transpose(T + 1, 1)
                    scores(T, par, 3)
                    if front_on:
                        project(T + 1, 5)
                        if not last_front:
                            x_transpose(T + 2)
                    p_transpose(T, 2)
                    values(T, par, 1)
                    if behind >= 1:
                        out_project(T - 1, L)
                    if front_on:
                        qk_transpose(T + 1, 2, after_x=not last_front)

                layer_slots(pe.Fori, L, slot)

                T, n = L * NB + NB, NB
                p_transpose(T - 1, 3)
                values(T - 1, 1, 2)
                f_up(0, 0)
                shift_state(T - 2, tile_of(z, n - 2, D // 2))
                values(T - 1, 1, 3)
                f_transpose(1)
                f_up(0, 1)
                att_transpose(T - 1, 0)
                f_up(0, 2)
                att_transpose(T - 1, 1)
                f_up(1, 0)
                out_project(T - 1, L)
                f_down(0)
                f_up(1, 1)
                shift_state(T - 1, tile_of(z, n - 1, D // 2))
                x_transpose(T, behind=0)
                f_transpose(2)
                f_up(1, 2)
                first_chunk(T, L + 1, 0)
                f_up(2, 0)
                f_down(1)
                f_transpose(3)
                first_chunk(T, L + 1, 1)
                f_up(2, 1)
                first_chunk(T, L + 1, 2)
                f_up(2, 2)
                first_chunk(T, L + 1, 3)
                f_up(3, 0)
                first_chunk(T, L + 1, 4)
                f_up(3, 1)
                first_chunk(T, L + 1, 5)
                f_up(3, 2)
                f_down(2)
                x_transpose(T + 1, behind=4)
                f_down(3, range(2))
                qk_transpose(T, 0, after_x=True)
                f_down(3, range(2, FG))
                qk_transpose(T, 1)

        @block.scalar
        def _(act):
            act.sem_inc(tr_evac, 4 * NB)
            act.sem_inc(zt_evac, NB)
            act.sem_inc(squared, 4 * NB)
            act.sem_inc(inv_log, 4 * NB)
            act.sem_inc(inv_ready, 4 * NB)
            act.sem_inc(v_ready, 2 * NB)
            act.sem_inc(ot_evac, 2 * NB)
            act.sem_inc(log_done, NB)
            act.sem_inc(rstd_ready, NB)
            act.sem_inc(ft_evac, NF)
            act.sem_inc(gelu_done, 3 * NF)
            act.preload_act_table_set("natural_log_exp_and_others")
            act.wait_ge(setup_done, 1)

            def x_out(T):
                act.wait_ge(zt_full, T + 1)
                half = D // 2
                for dst in (x_all, x_hi):
                    act.activation(dst[0:half, :], tr_ps[0:half, 0:NT], ACT.Copy)
                    last = act.activation(dst[half:D, 1:NT], tr_ps[half:D, 0:NT - 1], ACT.Copy)
                last.then_inc(zt_evac, 1)

            def square_chunk(T, c, ps=proj_ps):
                act.wait_ge(proj_full, T * 6 + (QK_AT[c] + 1))
                act.wait_ge(summed, T * 4 + (c - 1))
                act.activation(square[:, c % 2, :], ps[QK_AT[c] % 2][:], ACT.Square).then_inc(squared, 1)

            def norms(T, c):
                act.wait_ge(norm_ready, T * 4 + (c + 1))
                act.activation(log_sq[:, c, :], sumsq[:, c, :], ACT.Ln).then_inc(inv_log, 1)
                act.wait_ge(inv_log, T * 4 + (c + 1))
                act.activation(inv_norm[:, c, :], log_sq[:, c, :], ACT.Exp, scale=-0.5).then_inc(inv_ready, 1)

            def qk_out(T, par, c):
                act.wait_ge(tr_full, T * 4 + (c + 1))
                dst = (q_T, k_T)[c % 2][par]
                i = c // 2
                act.activation(flat(dst[:, 4 * i:4 * i + 4, :]), tr_ps[:], ACT.Copy).then_inc(tr_evac, 1)

            def v_out(T, par, i, ps=proj_ps):
                act.wait_ge(proj_full, T * 6 + (V_AT[i] + 1))
                act.activation(v[par][:, 8 * i:8 * i + 8, 0:DH], ps[V_AT[i] % 2][:].rearrange("p (h d) -> p h d", d=DH),
                               ACT.Copy).then_inc(v_ready, 1)

            def exps(T, g):
                act.wait_ge(centered, T * 4 + (g + 1))
                act.wait_ge(pt_full, T * 4 + (g - 1))
                act.activation(flat(p_sb[:, g % 2]), flat(s_sb[:, g % 2]), ACT.Exp).then_inc(p_ready, 1)

            def p_out(T, g):
                act.wait_ge(pt_full, T * 4 + (g + 1))
                act.activation(flat(p_T[:, g % 2]), pt_ps[:], ACT.Copy).then_inc(pt_evac, 1)

            def att_out(T, i):
                act.wait_ge(ot_full, T * 2 + (i + 1))
                act.activation(flat(att_T[:, 4 * i:4 * i + 4, :]), y_ps[:], ACT.Copy).then_inc(ot_evac, 1)

            def ln_std(T, par):
                act.wait_ge(var_ready, T + 1)
                act.activation(log_var[:, par:par + 1], mean_var[:, par, 1:2], ACT.Ln, bias=eps[:]).then_inc(log_done, 1)
                act.wait_ge(log_done, T + 1)
                act.activation(rstd[:, par:par + 1], log_var[:, par:par + 1], ACT.Exp, scale=-0.5).then_inc(rstd_ready, 1)

            act.wait_ge(xw_full, 1)
            act.activation(flat(xw_T[:]), pt_ps[:], ACT.Copy).then_inc(xw_evac, 1)

            def x_std(time, lo, hi):
                act.wait_ge(xvar_ready, time)
                act.activation(x_log[:, lo:hi], x_mv[:, lo:hi, 1], ACT.Ln, bias=eps[:]).then_inc(xlog_done, 1)
                act.wait_ge(xlog_done, time)
                act.activation(x_rstd[:, lo:hi], x_log[:, lo:hi], ACT.Exp, scale=-0.5).then_inc(xrstd_ready, 1)

            x_std(1, 0, 2)

            def x_inputs_out(T):
                act.wait_ge(xt_full, T + 1)
                act.activation(flat(xc_T[:]), tr_ps[:, 0:256], ACT.Copy).then_inc(xt_evac, 1)

            def x_exps(T, g):
                act.wait_ge(min_ready, T * 4 + (g + 1))
                if after(T, 1) or g >= 2:
                    act.wait_ge(pt_full, T * 4 + (g - 1))
                for j in range(GH):
                    last = act.activation(p_sb[:, g % 2, j, :], s_sb[:, g % 2, j, :], ACT.Exp, scale=-1.0,
                                          bias=row_min[:, g % 2, j:j + 1], accum_out=p_sum[:, g % 2, j:j + 1])
                last.then_inc(exp_ready, 1)

            def x_qk_out(T, par):
                act.wait_ge(xproj_full, T + 1)
                if after(T, 1):
                    act.wait_ge(xk_ready, T)
                act.activation(xq[:, par], proj_ps[0][:, 0:128], ACT.Identity, bias=q_scale[:, 1:2], scale=q_scale[:, 0:1])
                act.activation(xk[:], proj_ps[0][:, 128:256], ACT.Identity, bias=xb_col[:, 1:2]).then_inc(xqk_out, 1)

            def x_att_out(T, par):
                act.wait_ge(pv_full, T * 4 + 4)
                if after(T, 1):
                    act.wait_ge(xy_full, T)
                act.activation(x_att_T[:], x_pv_ps[par][:, 0:128], ACT.Copy).then_inc(xo_evac, 1)

            def x_slot(T, par, first=False, front_on=True):
                if not first:
                    p_out(T - 1, 2)
                if front_on:
                    x_inputs_out(T + 1)
                x_exps(T, 0)
                if not first:
                    p_out(T - 1, 3)
                if front_on:
                    x_qk_out(T + 1, 1 - par)
                x_exps(T, 1)
                p_out(T, 0)
                x_exps(T, 2)
                p_out(T, 1)
                if not first:
                    x_att_out(T - 1, 1 - par)
                x_exps(T, 3)

            x_inputs_out(0)
            act.wait_ge(scalar_ready, 1)
            x_qk_out(0, 0)
            act.activation(tanh_g[:], gates[:, 2:4], ACT.Tanh).then_inc(tanh_done, 1)
            act.preload_act_table_set("natural_log_exp_and_others")
            x_std(2, 2, NB)
            x_slot(0, 0, first=True)
            x_slot(1, 1)
            with act.Fori(1, NB // 2 - 1) as pair:
                x_slot(pair * 2, 0)
                x_slot(pair * 2 + 1, 1)
            x_slot(NB - 2, 0)
            x_slot(NB - 1, 1, front_on=False)
            def first_out(T):
                for c in range(4):
                    norms(T, c)
                x_out(T + 1)
                for c in range(2):
                    qk_out(T, 0, c)

            p_out(NB - 1, 2)
            x_std(3, 0, NB - 2)
            p_out(NB - 1, 3)
            x_att_out(NB - 1, 1)
            x_out(NB)
            square_chunk(NB, 0)
            square_chunk(NB, 1)
            norms(NB, 0)
            v_out(NB, 0, 0)
            square_chunk(NB, 2)
            norms(NB, 1)
            v_out(NB, 0, 1)
            norms(NB, 2)
            square_chunk(NB, 3)
            x_out(NB + 1)
            norms(NB, 3)
            x_std(4, NB - 2, NB)
            for c in range(2):
                qk_out(NB, 0, c)

            with act.Fori(1, LAYERS + 1) as L:
                def f_out(j, ps=pt_ps):
                    F = L * NF + j
                    act.wait_ge(ft_full, F + 1)
                    if j == 0:
                        act.wait_ge(param_ready, L)
                    for dst in (f_all, f_hi):
                        last = act.activation(dst[:, j % 2, :], ps[:], ACT.Identity,
                                              bias=param[:, 1:2], scale=param[:, 0:1])
                    last.then_inc(ft_evac, 1)

                def f_gelu(j, c):
                    F = L * NF + j
                    act.wait_ge(gate_full, F * 3 + (c + 1))
                    if j or c == 2:
                        act.wait_ge(h_ready, F * 3 + (c - 1))
                    m = FC[c]
                    act.activation(gelu[0:m, (3 * j + c) % 2, :], proj_ps[0][0:m, :], ACT.Gelu,
                                   bias=param[0:m, 5 + c:6 + c]).then_inc(gelu_done, 1)

                def slot(T, n, par, first=False, behind=2, front_on=True, last_front=False):
                    if not first:
                        norms(T, 3)
                    if front_on:
                        square_chunk(T + 1, 0)
                    if behind >= 1:
                        p_out(T - 1, 3)
                    if first:
                        qk_out(T, par, 2)
                    qk_out(T, par, 3)
                    exps(T, 0)
                    if front_on:
                        norms(T + 1, 0)
                        square_chunk(T + 1, 1)
                    p_out(T, 0)
                    if front_on:
                        qk_out(T + 1, 1 - par, 0)
                    exps(T, 1)
                    if behind >= 1:
                        att_out(T - 1, 0)
                    if front_on:
                        norms(T + 1, 1)
                        v_out(T + 1, 1 - par, 0)
                        square_chunk(T + 1, 2)
                    p_out(T, 1)
                    if behind >= 2:
                        ln_std(T - 2, par)
                    if front_on:
                        qk_out(T + 1, 1 - par, 1)
                    exps(T, 2)
                    if behind >= 1:
                        att_out(T - 1, 1)
                    if not front_on:
                        f_out(0, tr_ps)
                    if front_on:
                        norms(T + 1, 2)
                        v_out(T + 1, 1 - par, 1)
                        square_chunk(T + 1, 3)
                        if not last_front:
                            x_out(T + 2)
                    p_out(T, 2)
                    if front_on:
                        qk_out(T + 1, 1 - par, 2)
                    exps(T, 3)

                layer_slots(act.Fori, L, slot)

                T = L * NB + NB
                p_out(T - 1, 3)
                act.preload_act_table_set("gelu_and_others")
                f_gelu(0, 0)
                f_out(1)
                f_gelu(0, 1)
                att_out(T - 1, 0)
                f_gelu(0, 2)
                att_out(T - 1, 1)
                f_gelu(1, 0)
                f_gelu(1, 1)
                x_out(T)
                f_out(2)
                f_gelu(1, 2)
                act.preload_act_table_set("natural_log_exp_and_others")
                ln_std(T - 2, 0)
                ln_std(T - 1, 1)
                act.preload_act_table_set("gelu_and_others")
                square_chunk(T, 0, first_ps)
                f_gelu(2, 0)
                f_out(3)
                square_chunk(T, 1, first_ps)
                f_gelu(2, 1)
                v_out(T, 0, 0, first_ps)
                f_gelu(2, 2)
                square_chunk(T, 2, first_ps)
                f_gelu(3, 0)
                v_out(T, 0, 1, first_ps)
                f_gelu(3, 1)
                square_chunk(T, 3, first_ps)
                f_gelu(3, 2)
                act.preload_act_table_set("natural_log_exp_and_others")
                first_out(T)

        @block.vector
        def _(dve):
            dve.sem_inc(rotated, 4 * NB)
            dve.sem_inc(summed, 4 * NB)
            dve.sem_inc(norm_ready, 4 * NB)
            dve.sem_inc(z_attn, NB)
            dve.sem_inc(xs_ready, 2 * NB)
            dve.sem_inc(stat_done, NB)
            dve.sem_inc(var_ready, NB)
            dve.sem_inc(xn_ready, NB)
            dve.sem_inc(h_ready, 3 * NF)
            dve.sem_inc(max_ready, 4 * NB)
            dve.sem_inc(recip_done, 4 * NB)
            dve.sem_inc(att_ready, 4 * NB)
            dve.sem_inc(z_staged, NB)
            dve.memset(eps[:], LN_EPS)
            for i in range(2):
                dve.memset(v[i][:, :, DH], 1.0)
                dve.memset(h_T[i][2][:], 1.0)
            dve.memset(x_all[:], 0.0)
            dve.memset(x_hi[:].bitcast(f32), 0.0).then_inc(setup_done, 1)

            def w_round(k, L1):
                col = slice(INNER * k, INNER * (k + 1))
                dve.tensor_copy(w_hi[:, col], w_raw[:, col]).then_inc(w_hi_done, 1)


            def by_table(T, c, layer, i, dst, banks):
                ps = banks[QK_AT[c] % 2][:].rearrange("p (h d) -> p h d", d=DH)
                tb = tab[:, 2 * (c % 2) + i, bass.ds(layer, 1), :].to_broadcast([128, 8, DH])
                return dve.tensor_tensor(dst[:, c % 2, :].rearrange("p (h d) -> p h d", d=DH), ps, tb, ALU.mult)

            def times_cos(T, c, layer, banks=proj_ps):
                dve.wait_ge(squared, T * 4 + (c + 1))
                dve.wait_ge(qk_added, T * 4 + (c - 1))
                by_table(T, c, layer, 0, by_cos, banks)

            def times_sin(T, c, layer, banks=proj_ps):
                by_table(T, c, layer, 1, by_sin, banks).then_inc(rotated, 1)

            def sum_squares(T, c):
                dve.tensor_reduce(sumsq[:, c, :], square[:, c % 2, :].rearrange("p (h d) -> p h d", d=DH),
                                  AX, ALU.add).then_inc(summed, 1)

            def clamp_norm(T, c):
                dve.wait_ge(summed, T * 4 + (c + 1))
                dve.tensor_scalar(sumsq[:, c, :], sumsq[:, c, :], 1e-24, None, ALU.max).then_inc(norm_ready, 1)

            def mask(T, g):
                dve.wait_ge(s_full, T * 4 + (g + 1))
                dve.wait_ge(p_ready, T * 4 + (g - 1))
                dve.tensor_tensor(s_sb[:, g % 2].rearrange("p (a b) k -> p b a k", b=2),
                                  s_ps[:, :, 0:GH // 2 * NT].rearrange("p b (a k) -> p b a k", k=NT),
                                  band[:].unsqueeze(1).unsqueeze(1).to_broadcast([128, 2, GH // 2, NT]),
                                  ALU.add).then_inc(masked, 1)

            def row_maxima(T, g):
                dve.wait_ge(masked, T * 4 + (g + 1))
                dve.tensor_reduce(row_max[:, g % 2, :], s_sb[:, g % 2], AX, ALU.max).then_inc(max_ready, 1)

            def sums_inverse(T, g):
                dve.wait_ge(pv_full, T * 4 + (g + 1))
                o = pv_ps[:, 0:GH * (DH + 1)].rearrange("p (h d) -> p h d", d=DH + 1)
                dve.reciprocal(inv_sum[:], o[:, :, DH]).then_inc(recip_done, 1)

            def normalise(T, g):
                dve.wait_ge(recip_done, T * 4 + (g + 1))
                o = pv_ps[:, 0:GH * (DH + 1)].rearrange("p (h d) -> p h d", d=DH + 1)
                dve.tensor_tensor(att[:, GH * g:GH * g + GH, :], o[:, :, 0:DH],
                                  inv_sum[:].unsqueeze(2).to_broadcast([128, GH, DH]), ALU.mult).then_inc(att_ready, 1)

            dve.wait_ge(x_ld, 16)

            def x_stats(lo, hi):
                for b in range(lo, hi):
                    last = dve.bn_stats(x_st[:, b], x_res[:, b])
                last.then_inc(xstat_done, 1)

            def x_moments(lo, hi):
                for b in range(lo, hi):
                    last = dve.bn_aggr(x_mv[:, b], x_st[:, b])
                last.then_inc(xvar_ready, 1)

            x_stats(0, 2)
            dve.wait_ge(xstat_done, 1)
            x_moments(0, 2)
            dve.memset(xv[:], 0.0).then_inc(xv_clear, 1)
            def x_normalise(T, par):
                if after(T, 2):
                    dve.wait_ge(xt_full, T - 1)
                src = x_res[:, T] if isinstance(T, int) else tile_of(x_res, T)
                mu = x_mv[:, T, 0:1] if isinstance(T, int) else x_mv[:, bass.ds(T, 1), 0]
                rs = x_rstd[:, T:T + 1] if isinstance(T, int) else x_rstd[:, bass.ds(T, 1)]
                dve.tensor_scalar(x_in[:, par], src, mu, rs, ALU.subtract, ALU.mult).then_inc(xin_ready, 1)

            dve.wait_ge(xrstd_ready, 1)
            x_normalise(0, 0)
            x_normalise(1, 1)
            dve.wait_ge(bc_ld, N_BC)
            dve.tensor_scalar(q_scale[:, 0:1], gates[:, 0:1], -float(XD) ** -0.5, None, ALU.mult).then_inc(xscaled, 1)
            dve.tensor_scalar(alpha[:, :, :], alpha[:, :, :], gates[:, 1:2], -1.0, ALU.mult, ALU.mult).then_inc(xscaled, 1)
            dve.wait_ge(xscaled, 2)
            dve.tensor_tensor(q_scale[:, 1:2], xb_col[:, 0:1], q_scale[:, 0:1], ALU.mult).then_inc(scalar_ready, 1)

            def x_minima(T, g):
                dve.wait_ge(masked, T * 4 + (g + 1))
                dve.tensor_reduce(row_min[:, g % 2, :], s_sb[:, g % 2], AX, ALU.min).then_inc(min_ready, 1)

            def x_sums_inverse(T, g):
                dve.wait_ge(exp_ready, T * 4 + (g + 1))
                dve.reciprocal(x_inv_sum[:, g % 2, :], p_sum[:, g % 2, :]).then_inc(x_recip_done, 1)

            def x_value_out(T, par):
                dve.wait_ge(xqk_out, T + 1)
                if after(T, 2):
                    dve.wait_ge(pv_full, T * 4 - 4)
                for j in range(GH):
                    last = dve.tensor_tensor(xv[:, par, :, j, XD * j:XD * (j + 1)],
                                             proj_ps[0][:, 256:384].rearrange("p (g j d) -> p g j d", j=GH, d=XD)[:, :, j],
                                             xb_row[:, 0].rearrange("p (g j d) -> p g j d", j=GH, d=XD)[:, :, j], ALU.add)
                last.then_inc(xv_ready, 1)

            def x_clip(T, par):
                if after(T, 2):
                    dve.wait_ge(pos_ready, T * 4 - 4)
                src = frac_k[:, T] if isinstance(T, int) else tile_of(frac_k, T)
                fq = frac_q[:, T:T + 1] if isinstance(T, int) else frac_q[:, bass.ds(T, 1)]
                dve.tensor_scalar(d_clip[:, par], src, fq, -CLAMP, ALU.subtract, ALU.max).then_inc(xclip, 1)

            def x_signs(T, par):
                dve.wait_ge(xclip, T + 1)
                dve.tensor_scalar(d_neg[:, par], d_clip[:, par], 0.0, None, ALU.min)
                dve.tensor_scalar(d_pos[:, par], d_clip[:, par], CLAMP, 0.0, ALU.min, ALU.max).then_inc(clip_ready, 1)

            def x_bias_out(T, par, g):
                dve.wait_ge(pos_ready, T * 4 + (g + 1))
                if g == 0:
                    dve.wait_ge(clip_ready, T + 1)
                for j in range(GH):
                    h = GH * g + j
                    last = dve.scalar_tensor_tensor(x_bias[:, g % 2, j], d_neg[:, par], alpha[:, 1, h:h + 1],
                                                    x_bias[:, g % 2, j], ALU.mult, ALU.add)
                last.then_inc(bias_ready, 1)

            def x_mask(T, g):
                dve.wait_ge(s_full, T * 4 + (g + 1))
                dve.wait_ge(bias_ready, T * 4 + (g + 1))
                if after(T, 1) or g >= 2:
                    dve.wait_ge(exp_ready, T * 4 + (g - 1))
                dve.tensor_tensor(s_sb[:, g % 2], s_ps[:, g % 2, :].rearrange("p (h k) -> p h k", k=NT),
                                  x_bias[:, g % 2], ALU.add).then_inc(masked, 1)

            def x_add(T):
                dve.wait_ge(xg_ready, T + 1)
                dve.wait_ge(xy_full, T + 1)
                xt = x_res[:, T] if isinstance(T, int) else tile_of(x_res, T)
                dve.scalar_tensor_tensor(xt, y_ps[:, 0:D], tanh_g[:, 0:1], xt, ALU.mult, ALU.add).then_inc(xy_ready, 1)

            def x_gate_bias(T):
                xt = x_res[:, T] if isinstance(T, int) else tile_of(x_res, T)
                dve.tensor_tensor(xt, xt, xb_row[:, 1], ALU.add).then_inc(xg_ready, 1)

            def x_slot(T, par, first=False, second=False, front_on=True, last_front=False):
                x_mask(T, 0)
                if not first:
                    x_sums_inverse(T - 1, 3)
                if not first and not second:
                    x_add(T - 2)
                x_minima(T, 0)
                x_bias_out(T, par, 1)
                if not front_on:
                    dve.wait_ge(xy_ready, NB - 2)
                    x_stats(0, 5)
                x_mask(T, 1)
                x_sums_inverse(T, 0)
                x_gate_bias(T)
                x_minima(T, 1)
                if front_on and not last_front:
                    x_normalise(T + 2, par)
                x_bias_out(T, par, 2)
                if not front_on:
                    x_stats(5, 10)
                x_mask(T, 2)
                x_sums_inverse(T, 1)
                if front_on:
                    x_clip(T + 1, 1 - par)
                x_minima(T, 2)
                if front_on:
                    x_signs(T + 1, 1 - par)
                x_bias_out(T, par, 3)
                if not front_on:
                    x_stats(10, NB - 2)
                x_mask(T, 3)
                x_sums_inverse(T, 2)
                if front_on:
                    x_value_out(T + 1, 1 - par)
                x_minima(T, 3)
                if front_on:
                    x_bias_out(T + 1, 1 - par, 0)

            dve.wait_ge(frac_ld, 32)
            x_clip(0, 0)
            x_signs(0, 0)
            x_stats(2, NB)
            dve.wait_ge(xstat_done, 2)
            x_moments(2, NB)
            dve.wait_ge(xv_clear, 1)
            x_value_out(0, 0)
            dve.wait_ge(tanh_done, 1)
            dve.tensor_scalar(xb_row[:, 1], xb_row[:, 1], tanh_g[:, 0:1], None, ALU.mult).then_inc(xscaled, 1)
            dve.wait_ge(xscaled, 3)
            x_bias_out(0, 0, 0)
            dve.wait_ge(const_ld, N_CONST)
            for i in range(4):
                last = dve.tensor_tensor(tab[:, i], qk_scale[:, i // 2],
                                         rot[:, i, :].unsqueeze(1).to_broadcast([128, LAYERS, DH]), ALU.mult)
            last.then_inc(setup_done, 1)
            dve.wait_ge(xrstd_ready, 2)
            x_slot(0, 0, first=True)
            x_slot(1, 1, second=True)
            dve.wait_ge(ld_w, 16)
            for k in range(3):
                w_round(k, 0)
            with dve.Fori(1, NB // 2 - 1) as pair:
                x_slot(pair * 2, 0)
                x_slot(pair * 2 + 1, 1)
            x_slot(NB - 2, 0, last_front=True)
            x_slot(NB - 1, 1, front_on=False)
            def stage(T, n, groups_done):
                dve.wait_ge(z_ready, groups_done)
                dve.wait_ge(zt_full, T)
                dve.tensor_scalar(z_stage[:], tile_of(z, n), 1.0, None, ALU.mult).then_inc(z_staged, 1)

            def first_rotate(T, c, layer, banks=first_ps):
                times_cos(T, c, layer, banks)
                times_sin(T, c, layer, banks)

            def first_norm(T, c):
                sum_squares(T, c)
                clamp_norm(T, c)

            def first_chunk(T, c, layer, banks):
                first_rotate(T, c, layer, banks)
                first_norm(T, c)

            def z_out(lo, hi):
                for b in range(lo, hi):
                    dve.tensor_scalar(z[:, b], x_res[:, b], x_mv[:, b, 0:1], x_rstd[:, b:b + 1],
                                      ALU.subtract, ALU.mult).then_inc(z_ready, 1)

            dve.wait_ge(xstat_done, 5)
            x_moments(0, NB - 2)
            x_sums_inverse(NB - 1, 3)
            dve.wait_ge(xrstd_ready, 3)
            z_out(0, 2)
            stage(NB, 0, 1)
            x_add(NB - 2)
            z_out(2, 6)
            x_add(NB - 1)
            dve.wait_ge(setup_done, 2)
            first_chunk(NB, 0, 0, proj_ps)
            dve.wait_ge(xy_ready, NB)
            x_stats(NB - 2, NB)
            first_chunk(NB, 1, 0, proj_ps)
            dve.wait_ge(xstat_done, 6)
            x_moments(NB - 2, NB)
            first_chunk(NB, 2, 0, proj_ps)
            stage(NB + 1, 1, 2)
            first_chunk(NB, 3, 0, proj_ps)
            z_out(6, NB - 2)
            dve.wait_ge(xrstd_ready, 4)
            z_out(NB - 2, NB)
            dve.wait_ge(param_ld, N_PARAM)

            with dve.Fori(1, LAYERS + 1) as L:
                def add_out(T, n):
                    dve.wait_ge(y_full, T + 1)
                    zt = tile_of(z, n)
                    dve.tensor_tensor(zt, zt, y_ps[:, 0:D], ALU.add).then_inc(z_attn, 1)

                def ln_stats(T, n, par):
                    zt = tile_of(z, n, 0, D // 2)
                    dve.wait_ge(sh_full, T + 1)
                    dve.tensor_scalar(xs[:, par, 0:D // 2], zt, 1.0, None, ALU.mult).then_inc(xs_ready, 1)
                    dve.tensor_copy(xs[:, par, D // 2:D], y_ps[:, 0:D // 2]).then_inc(xs_ready, 1)
                    dve.wait_ge(xs_ready, T * 2 + 2)
                    dve.bn_stats(stats[:, par], xs[:, par]).then_inc(stat_done, 1)

                def ln_variance(T, par):
                    dve.bn_aggr(mean_var[:, par], stats[:, par]).then_inc(var_ready, 1)

                def ln_apply(T, n, par):
                    dve.wait_ge(rstd_ready, T + 1)
                    dve.tensor_scalar(tile_of(xn, n), xs[:, par],
                                      mean_var[:, par, 0:1], rstd[:, par:par + 1], ALU.subtract, ALU.mult).then_inc(xn_ready, 1)

                def step(T, g, behind=2, front_on=True, stats_ready=None):
                    Tn, gn = (T, g - 2) if g >= 2 else (T - 1, g + 2)
                    norm_on = g >= 2 or behind >= 1
                    mask(T, g)
                    row_maxima(T, g)
                    if front_on:
                        times_cos(T + 1, g, L - 1)
                        times_sin(T + 1, g, L - 1)
                        sum_squares(T + 1, g)
                    if norm_on:
                        sums_inverse(Tn, gn)
                    if front_on:
                        clamp_norm(T + 1, g)
                    if stats_ready is not None:
                        dve.wait_ge(stat_done, stats_ready)
                    if norm_on:
                        normalise(Tn, gn)

                def slot(T, n, par, first=False, behind=2, front_on=True, last_front=False):
                    if first:
                        dve.wait_ge(ld_w1, L * 16)
                        dve.tensor_copy(w1_hi[:], w1_raw[:]).then_inc(w1_hi_done, 1)
                        dve.tensor_scalar(param[:], params[:, bass.ds(L - 1, 1), :].rearrange("p a b -> p (a b)"), 1.0, None,
                                          ALU.mult).then_inc(param_ready, 1)
                    if behind >= 2:
                        add_out(T - 2, n - 2)
                    step(T, 0, behind, front_on)
                    if behind >= 2:
                        ln_stats(T - 2, n - 2, par)
                    if not front_on:
                        dve.wait_ge(ld_w, L * 16 + 16)
                        w_round(0, L + 1)
                    step(T, 1, behind, front_on, stats_ready=T - 1 if behind >= 2 else None)
                    if behind >= 2:
                        ln_variance(T - 2, par)
                    if front_on and not last_front:
                        stage(T + 2, n + 2, L * 4 + 12)
                    if not front_on:
                        w_round(1, L + 1)
                    step(T, 2, behind, front_on)
                    if not front_on:
                        w_round(2, L + 1)
                    step(T, 3, behind, front_on)
                    if behind >= 2:
                        ln_apply(T - 2, n - 2, par)

                layer_slots(dve.Fori, L, slot)

                def f_gate(j, c):
                    F = L * NF + j
                    dve.wait_ge(gelu_done, F * 3 + (c + 1))
                    dve.wait_ge(a_full, F * 3 + (c + 1))
                    m = FC[c]
                    dve.scalar_tensor_tensor(h_T[j % 2][c][0:m, :], proj_ps[1][0:m, :], param[0:m, 2 + c:3 + c],
                                             gelu[0:m, (3 * j + c) % 2, :], ALU.add, ALU.mult).then_inc(h_ready, 1)

                def f_add(j):
                    F = L * NF + j
                    dve.wait_ge(fy_full, F + 1)
                    zg = flat(z[:, FG * j:FG * j + FG, :])
                    dve.tensor_tensor(zg, zg, s_ps[:, j % 2], ALU.add).then_inc(z_ready, 1)

                T, n = L * NB + NB, NB
                add_out(T - 2, n - 2)
                sums_inverse(T - 1, 2)
                normalise(T - 1, 2)
                ln_stats(T - 2, n - 2, 0)
                sums_inverse(T - 1, 3)
                dve.wait_ge(stat_done, T - 1)
                normalise(T - 1, 3)
                ln_variance(T - 2, 0)
                for c in range(3):
                    f_gate(0, c)
                f_gate(1, 0)
                add_out(T - 1, n - 1)
                f_add(0)
                stage(T, 0, L * NF + (NB - NF + 1))
                ln_stats(T - 1, n - 1, 1)
                dve.wait_ge(stat_done, T)
                f_gate(1, 1)
                ln_variance(T - 1, 1)
                f_gate(1, 2)
                ln_apply(T - 2, n - 2, 0)
                ln_apply(T - 1, n - 1, 1)
                first_rotate(T, 0, L % LAYERS)
                f_gate(2, 0)
                first_norm(T, 0)
                f_add(1)
                first_rotate(T, 1, L % LAYERS)
                f_gate(2, 1)
                first_norm(T, 1)
                f_gate(2, 2)
                first_rotate(T, 2, L % LAYERS)
                f_gate(3, 0)
                first_norm(T, 2)
                f_gate(3, 1)
                stage(T + 1, 1, L * NF + (NB - NF + 1))
                first_rotate(T, 3, L % LAYERS)
                f_gate(3, 2)
                first_norm(T, 3)
                f_add(2)
                f_add(3)

            dve.wait_ge(z_ready, NB + NF * LAYERS)
            for j in range(NF):
                zg, xg = flat(z[:, FG * j:FG * (j + 1)]), flat(x_res[:, FG * j:FG * (j + 1)])
                dve.scalar_tensor_tensor(zg, zg, tanh_g[:, 1:2], xg, ALU.mult, ALU.add).then_inc(result_ready, 1)

        @block.gpsimd
        def _(pool):
            pool.sem_inc(qk_added, 4 * NB)
            pool.sem_inc(qk_ready, 4 * NB)
            pool.sem_inc(x_split, NB)
            pool.sem_inc(f_split, NF)
            pool.sem_inc(centered, 4 * NB)
            pool.memset(params[:], 0.0).then_inc(params_clear, 1)

            def w_rest(k, done):
                pool.wait_ge(w_hi_done, done)
                col = slice(INNER * k, INNER * (k + 1))
                pool.tensor_tensor(w_lo[:, col], w_raw[:, col], w_hi[:, col].bitcast(f32), ALU.subtract).then_inc(w_split, 1)

            def split_x(T):
                pool.wait_ge(zt_evac, T + 1)
                pool.tensor_tensor(x_lo[:], x_all[:], x_hi[:].bitcast(f32), ALU.subtract).then_inc(x_split, 1)

            def add_rotated(T, c):
                pool.wait_ge(rotated, T * 4 + (c + 1))
                pool.wait_ge(tr_full, T * 4 + (c - 3))
                pool.tensor_tensor(heads(qk[:, c, :]), heads(by_cos[:, c % 2, :]),
                                   heads(by_sin[:, c % 2, :])[:, :, ::-1, :], ALU.add).then_inc(qk_added, 1)

            def scale_rotated(T, c):
                pool.wait_ge(qk_added, T * 4 + (c + 1))
                pool.wait_ge(inv_ready, T * 4 + (c + 1))
                ap = qk[:, c, :].rearrange("p (h d) -> p h d", d=DH)
                pool.tensor_tensor(ap, ap, inv_norm[:, c, :].unsqueeze(2).to_broadcast([128, 8, DH]),
                                   ALU.mult).then_inc(qk_ready, 1)

            def center(T, g):
                pool.wait_ge(max_ready, T * 4 + (g + 1))
                pool.tensor_tensor(s_sb[:, g % 2], s_sb[:, g % 2],
                                   row_max[:, g % 2, :].unsqueeze(2).to_broadcast([128, GH, NT]), ALU.subtract).then_inc(centered, 1)

            def x_keys(T, par):
                pool.wait_ge(xqk_out, T + 1)
                pool.tensor_tensor(xk_bd[:, par], xk[:].unsqueeze(1).to_broadcast([128, GH, NT]),
                                   head_of[:].unsqueeze(2).to_broadcast([128, GH, NT]), ALU.mult).then_inc(xk_ready, 1)

            def first_probs_scale(T, g):
                pool.wait_ge(x_recip_done, T * 4 + (g + 1))
                pool.tensor_tensor(p_sb[:, g % 2], p_sb[:, g % 2],
                                   x_inv_sum[:, g % 2, :].unsqueeze(2).to_broadcast([128, GH, NT]), ALU.mult).then_inc(p_ready, 1)

            def x_bias_pos(T, par, g):
                if after(T, 1) or g >= 2:
                    pool.wait_ge(masked, T * 4 + (g - 1))
                pool.wait_ge(clip_ready, T + 1)
                pool.tensor_tensor(x_bias[:, g % 2], d_pos[:, par].unsqueeze(1).to_broadcast([128, GH, NT]),
                                   alpha[:, 0, GH * g:GH * g + GH].unsqueeze(2).to_broadcast([128, GH, NT]),
                                   ALU.mult).then_inc(pos_ready, 1)

            def x_slot(T, par, first=False, front_on=True):
                x_bias_pos(T, par, 1)
                if not first:
                    first_probs_scale(T - 1, 3)
                x_bias_pos(T, par, 2)
                first_probs_scale(T, 0)
                x_bias_pos(T, par, 3)
                first_probs_scale(T, 1)
                if front_on:
                    x_keys(T + 1, 1 - par)
                    x_bias_pos(T + 1, 1 - par, 0)
                first_probs_scale(T, 2)

            pool.wait_ge(bc_ld, N_BC)
            pool.wait_ge(scalar_ready, 1)
            x_bias_pos(0, 0, 0)
            x_keys(0, 0)
            x_slot(0, 0, first=True)
            x_slot(1, 1)
            w_rest(0, 1)
            with pool.Fori(1, NB // 2 - 1) as pair:
                x_slot(pair * 2, 0)
                x_slot(pair * 2 + 1, 1)
            w_rest(1, 2)
            x_slot(NB - 2, 0)
            w_rest(2, 3)
            x_slot(NB - 1, 1, front_on=False)
            first_probs_scale(NB - 1, 3)

            def first_scales(T):
                scale_rotated(T, 0)
                scale_rotated(T, 1)
                split_x(T + 1)
                scale_rotated(T, 2)
                scale_rotated(T, 3)

            split_x(NB)
            add_rotated(NB, 0)
            for c in range(3):
                add_rotated(NB, c + 1)
                scale_rotated(NB, c)
            split_x(NB + 1)
            scale_rotated(NB, 3)

            with pool.Fori(1, LAYERS + 1) as L:
                def slot(T, n, par, first=False, behind=2, front_on=True, last_front=False):
                    if first:
                        pool.wait_ge(w1_hi_done, L)
                        pool.tensor_tensor(w1_lo[:], w1_raw[:], w1_hi[:].bitcast(f32), ALU.subtract).then_inc(w1_split, 1)
                    for g in range(NG):
                        if g == 0:
                            if not first:
                                scale_rotated(T, 3)
                        elif front_on:
                            scale_rotated(T + 1, g - 1)
                        center(T, g)
                        if not front_on and 1 <= g < 3:
                            w_rest(g - 1, L * 3 + g)
                        if front_on:
                            if g == 3 and not last_front:
                                split_x(T + 2)
                            add_rotated(T + 1, g)

                layer_slots(pool.Fori, L, slot)

                def f_rest(j):
                    pool.wait_ge(ft_evac, L * NF + (j + 1))
                    pool.tensor_tensor(f_lo[:, j % 2, :], f_all[:, j % 2, :], f_hi[:, j % 2, :].bitcast(f32),
                                       ALU.subtract).then_inc(f_split, 1)

                T = L * NB + NB
                f_rest(0)
                w_rest(2, L * 3 + 3)
                f_rest(1)
                split_x(T)
                f_rest(2)
                add_rotated(T, 0)
                f_rest(3)
                for c in range(1, 4):
                    add_rotated(T, c)
                first_scales(T)


def constants():
    one = np.float32
    half = np.arange(0, DH, 2, dtype=np.float32)
    inv_freq = (one(1.0) / one(10000.0) ** (half / one(DH))).astype(np.float32)
    pos = np.arange(NT, dtype=np.float32)
    freqs = pos[:, None] * inv_freq[None, :]
    base = (half + one(0.4 * DH)) / one(1.4 * DH)
    power = (pos - NT // 2) / one(WINDOW // 2)
    scale = base[None, :] ** power[:, None]
    cos, sin = np.cos(freqs), np.sin(freqs)
    rot = np.zeros((NT, 4, DH), np.float32)
    for i, s in ((0, QK_SCALE * scale), (2, 1.0 / scale)):
        rot[:, i] = np.concatenate([cos * s, cos * s], 1)
        rot[:, i + 1] = np.concatenate([sin * s, -sin * s], 1)
    p = np.arange(128)
    d = p[:, None] - p[None, :]
    band = np.where((d >= 0) & (d <= WINDOW), 0.0, NEG).astype(np.float32)
    head_of = (np.arange(128)[:, None] // XD % GH == np.arange(GH)[None, :]).astype(np.float32)
    return {"head_of": head_of, "ident": np.eye(128, dtype=np.float32), "shift": np.eye(128, k=1, dtype=np.float32),
            "band": band, "rot": rot.reshape(NT, 4 * DH)}


NAMES = ['x', 'ctx_1024', 'fside_BxS2_0', 'g_xattn', 'g_ffn', 'L0_xattn_Wq', 'L0_xattn_bq', 'L0_xattn_Wk', 'L0_xattn_bk',
         'L0_xattn_Wv', 'L0_xattn_bv', 'L0_xattn_Wo', 'L0_xattn_bo', 'L0_xattn_alpha_pos', 'L0_xattn_alpha_neg',
         'L0_xattn_gamma', 'L0_xattn_delta', 'L0_ffn_Wqkv', 'L0_ffn_q_scale', 'L0_ffn_k_scale', 'L0_ffn_Wo',
         'L0_ffn_ln_g', 'L0_ffn_ln_b', 'L0_ffn_W1', 'L0_ffn_b1', 'L0_ffn_W2', 'L0_ffn_b2']


def kernel(**inputs):
    import numpy as _np
    import concourse.bacc as _bacc
    from concourse import mybir as _mybir
    from concourse.bass_utils import run_bass_kernel_spmd as _run

    nc = _bacc.Bacc("TRN2", target_bir_lowering=False, num_devices=1)
    arrays, args = {}, {}
    given = {n: inputs[n] for n in NAMES} | constants()
    for name, a in given.items():
        a = _np.ascontiguousarray(a)
        arrays[f"in_{name}"] = a
        args[name] = nc.dram_tensor(f"in_{name}", a.shape, _mybir.dt.from_np(a.dtype), kind="ExternalInput").ap()
    args["out"] = nc.dram_tensor("out_0", (NB, NT, D), _mybir.dt.float32, kind="ExternalOutput").ap()
    build(nc, args)
    r = _run(nc, [arrays], core_ids=[0])
    return r.results[0]["out_0"]
```
